# Optimizing a Trainium2 kernel written in Bass

```python
import numpy as np
import jax
import jax.numpy as jnp

def _softmax(x, axis=-1):
    return jax.nn.softmax(x, axis=axis)

def _gelu(x):
    return jax.nn.gelu(x, approximate=True)

def _silu(x):
    return jax.nn.silu(x)

def _sigmoid(x):
    return jax.nn.sigmoid(x)

def _layernorm(x, axis=-1, eps=1e-05):
    m = jnp.mean(x, axis=axis, keepdims=True)
    v = jnp.var(x, axis=axis, keepdims=True)
    return (x - m) / jnp.sqrt(v + eps)

def _scatter_add(tgt, idx, src, axis=0):
    return tgt.at[idx].add(src)

def _segment_sum(src, seg, n):
    return jax.ops.segment_sum(src, seg, n)
kernel_name = 'mk_flamingo_gated_d2_seqx_r8_683344'

def setup_inputs(seed: int=0):
    np.random.seed(seed)
    _w = jnp.asarray

    def _rec_inputs():
        import jax
        import jax.numpy as jnp
        _rk = jax.random.key(seed)
        x = -0.0003929 + 0.9999 * jax.random.normal(jax.random.fold_in(_rk, 1), (8, 128, 256), jnp.float32)
        _lenS = 128 - jax.random.randint(jax.random.fold_in(_rk, 7), (8,), 0, max(1, 128 // 4) + 1, jnp.int32)
        _lenS2 = 128 - jax.random.randint(jax.random.fold_in(_rk, 8), (8,), 0, max(1, 128 // 4) + 1, jnp.int32)
        _ctx_1024P = jax.random.normal(jax.random.fold_in(_rk, 11), (8, 16, 128), jnp.float32)
        _ctx_1024c = jax.random.dirichlet(jax.random.fold_in(_rk, 511), 0.3 * jnp.ones((16,), jnp.float32), (8, 128))
        _ctx_1024t = jnp.einsum('bsk,bkd->bsd', _ctx_1024c, _ctx_1024P)
        _ctx_1024t = _ctx_1024t * jax.lax.rsqrt(jnp.mean(jnp.square(_ctx_1024t)) + 1e-12) * 0.953939
        ctx_1024 = 0.000227908 + 0.99994 * (_ctx_1024t + 0.3 * jax.random.normal(jax.random.fold_in(_rk, 611), (8, 128, 128), jnp.float32))
        fside_BxSx2_0 = jax.random.uniform(jax.random.fold_in(_rk, 12), (8, 128, 2), jnp.float32, 0.0, 0.999707)
        _g = jax.random.normal(jax.random.fold_in(_rk, 9001), (2, 2), jnp.float32)
        _g = jnp.sign(_g) * jnp.maximum(jnp.abs(_g), 1.0) + (_g == 0) * 1.0
        g_xattn = _g[0]
        g_ffn = _g[1]
        return (x, ctx_1024, fside_BxSx2_0, g_xattn, g_ffn)
    x, ctx_1024, fside_BxSx2_0, g_xattn, g_ffn = _rec_inputs()

    def _L0_xattn_setup():
        import jax, jax.numpy as jnp
        import numpy as np
        EPS = 1e-05

        def rmsnorm(x, g, eps=EPS):
            var = jnp.mean(jnp.square(x), axis=-1, keepdims=True)
            return x * jax.lax.rsqrt(var + eps) * g
        key = jax.random.key(seed)
        ks = jax.random.split(key, 8)
        B, Sq, Skv = (2, 512, 64)
        dim, cdim, H, D = (256, 128, 16, 128)
        inner = H * D
        s = lambda f: 1.0 / np.sqrt(f)
        return {'hidden_states': jax.random.normal(ks[0], (B, Sq, dim), jnp.float32), 'encoder_hidden_states': jax.random.normal(ks[1], (B, Skv, cdim), jnp.float32), 'Wq': jax.random.normal(ks[2], (dim, inner), jnp.float32) * s(dim), 'Wk': jax.random.normal(ks[3], (cdim, inner), jnp.float32) * s(cdim), 'Wv': jax.random.normal(ks[4], (cdim, inner), jnp.float32) * s(cdim), 'Wo': jax.random.normal(ks[5], (inner, dim), jnp.float32) * s(inner), 'gq': jnp.ones((D,), jnp.float32), 'gk': jnp.ones((D,), jnp.float32)}
    _L0_xattn_all = _L0_xattn_setup()
    _L0_xattn_in = {k: v for k, v in _L0_xattn_all.items() if k in ('Wq', 'Wk', 'Wv', 'Wo', 'gq', 'gk')}
    del _L0_xattn_all

    def _L0_ffn_setup():
        import jax, jax.numpy as jnp
        import numpy as np
        D_MODEL = 256
        D_EXPERT = 1024
        EPS = 1e-08

        def ternary_quant(w):
            scale = jnp.mean(jnp.abs(w)) + EPS
            q = jnp.clip(jnp.round(w / scale), -1.0, 1.0) * scale
            return w + jax.lax.stop_gradient(q - w)
        key = jax.random.key(seed)
        k_x, k_up, k_gate, k_down = jax.random.split(key, 4)
        std_in = 1.0 / np.sqrt(D_MODEL)
        std_exp = 1.0 / np.sqrt(D_EXPERT)
        return {'x': jax.random.normal(k_x, (4, 256, D_MODEL), dtype=jnp.float32), 'W_up': jax.random.normal(k_up, (D_EXPERT, D_MODEL), dtype=jnp.float32) * std_in, 'W_gate': jax.random.normal(k_gate, (D_EXPERT, D_MODEL), dtype=jnp.float32) * std_in, 'W_down': jax.random.normal(k_down, (D_MODEL, D_EXPERT), dtype=jnp.float32) * std_exp}
    _L0_ffn_all = _L0_ffn_setup()
    _L0_ffn_in = {k: v for k, v in _L0_ffn_all.items() if k in ('W_up', 'W_gate', 'W_down')}
    del _L0_ffn_all

    def _L1_xattn_setup():
        import jax, jax.numpy as jnp
        import numpy as np
        DIM = 256
        CTX_DIM = 128
        N_HEADS = 32
        HEAD_DIM = DIM // N_HEADS
        POS_DIM = 2
        B, N, CTXN = (2, 256, 256)
        ROPE_BASE = 10000.0

        def apply_axial_rope(x, pos):
            b, n, h, d = x.shape
            p = pos.shape[-1]
            dpa = d // p
            half = dpa // 2
            freqs = ROPE_BASE ** (-jnp.arange(half, dtype=x.dtype) / half)
            ang = pos[..., :, None] * freqs
            cos = jnp.cos(ang)[:, :, None, :, :]
            sin = jnp.sin(ang)[:, :, None, :, :]
            xr = x.reshape(b, n, h, p, half, 2)
            x1, x2 = (xr[..., 0], xr[..., 1])
            out = jnp.stack([x1 * cos - x2 * sin, x1 * sin + x2 * cos], axis=-1)
            return out.reshape(b, n, h, d)
        key = jax.random.key(seed)
        ks = jax.random.split(key, 8)
        x = jax.random.normal(ks[0], (B, N, DIM), jnp.float32)
        ctx = jax.random.normal(ks[1], (B, CTXN, CTX_DIM), jnp.float32)
        pos_map = jax.random.uniform(ks[2], (B, N, POS_DIM), jnp.float32)
        ctx_pos_map = jax.random.uniform(ks[3], (B, CTXN, POS_DIM), jnp.float32)
        Wq = jax.random.normal(ks[4], (DIM, DIM), jnp.float32) / np.sqrt(DIM)
        Wkv = jax.random.normal(ks[5], (CTX_DIM, 2 * DIM), jnp.float32) / np.sqrt(CTX_DIM)
        Wout = jax.random.normal(ks[6], (DIM, DIM), jnp.float32) / np.sqrt(DIM)
        bout = jnp.zeros((DIM,), jnp.float32)
        return {'x': x, 'ctx': ctx, 'pos_map': pos_map, 'ctx_pos_map': ctx_pos_map, 'Wq': Wq, 'Wkv': Wkv, 'Wout': Wout, 'bout': bout}
    _L1_xattn_all = _L1_xattn_setup()
    _L1_xattn_in = {k: v for k, v in _L1_xattn_all.items() if k in ('Wq', 'Wkv', 'Wout', 'bout')}
    del _L1_xattn_all

    def _L1_ffn_setup():
        import jax, jax.numpy as jnp
        import numpy as np
        B, S, D = (2, 128, 256)
        E, F, TOP_K = (8, 176, 2)
        key = jax.random.key(seed)
        k1, k2, k3, k4, k5 = jax.random.split(key, 5)
        scale = 0.02
        return {'hidden_states': jax.random.normal(k1, (B, S, D), jnp.float32), 'gate_w': jax.random.normal(k2, (E, D), jnp.float32) * scale, 'w_gate': jax.random.normal(k3, (E, D, F), jnp.float32) * scale, 'w_up': jax.random.normal(k4, (E, D, F), jnp.float32) * scale, 'w_down': jax.random.normal(k5, (E, F, D), jnp.float32) * scale}
    _L1_ffn_all = _L1_ffn_setup()
    _L1_ffn_in = {k: v for k, v in _L1_ffn_all.items() if k in ('gate_w', 'w_gate', 'w_up', 'w_down')}
    del _L1_ffn_all
    return {'x': x, 'ctx_1024': ctx_1024, 'fside_BxSx2_0': fside_BxSx2_0, 'g_xattn': g_xattn, 'g_ffn': g_ffn, 'L0_xattn_Wq': _L0_xattn_in['Wq'], 'L0_xattn_Wk': _L0_xattn_in['Wk'], 'L0_xattn_Wv': _L0_xattn_in['Wv'], 'L0_xattn_Wo': _L0_xattn_in['Wo'], 'L0_xattn_gq': _L0_xattn_in['gq'], 'L0_xattn_gk': _L0_xattn_in['gk'], 'L0_ffn_W_up': _L0_ffn_in['W_up'], 'L0_ffn_W_gate': _L0_ffn_in['W_gate'], 'L0_ffn_W_down': _L0_ffn_in['W_down'], 'L1_xattn_Wq': _L1_xattn_in['Wq'], 'L1_xattn_Wkv': _L1_xattn_in['Wkv'], 'L1_xattn_Wout': _L1_xattn_in['Wout'], 'L1_xattn_bout': _L1_xattn_in['bout'], 'L1_ffn_gate_w': _L1_ffn_in['gate_w'], 'L1_ffn_w_gate': _L1_ffn_in['w_gate'], 'L1_ffn_w_up': _L1_ffn_in['w_up'], 'L1_ffn_w_down': _L1_ffn_in['w_down']}

def reference(x, ctx_1024, fside_BxSx2_0, g_xattn, g_ffn, L0_xattn_Wq, L0_xattn_Wk, L0_xattn_Wv, L0_xattn_Wo, L0_xattn_gq, L0_xattn_gk, L0_ffn_W_up, L0_ffn_W_gate, L0_ffn_W_down, L1_xattn_Wq, L1_xattn_Wkv, L1_xattn_Wout, L1_xattn_bout, L1_ffn_gate_w, L1_ffn_w_gate, L1_ffn_w_up, L1_ffn_w_down):
    import jax
    import jax.numpy as jnp

    def _L0_xattn_ref(hidden_states, encoder_hidden_states, Wq, Wk, Wv, Wo, gq, gk):
        import jax, jax.numpy as jnp
        import numpy as np
        EPS = 1e-05

        def rmsnorm(x, g, eps=EPS):
            var = jnp.mean(jnp.square(x), axis=-1, keepdims=True)
            return x * jax.lax.rsqrt(var + eps) * g
        B, Sq, _ = hidden_states.shape
        Skv = encoder_hidden_states.shape[1]
        D = gq.shape[0]
        H = Wq.shape[1] // D
        scale = 1.0 / np.sqrt(D)
        q = (hidden_states @ Wq).reshape(B, Sq, H, D)
        k = (encoder_hidden_states @ Wk).reshape(B, Skv, H, D)
        v = (encoder_hidden_states @ Wv).reshape(B, Skv, H, D)
        q = rmsnorm(q, gq)
        k = rmsnorm(k, gk)
        scores = jnp.einsum('bqhd,bkhd->bhqk', q, k) * scale
        attn = jax.nn.softmax(scores, axis=-1)
        out = jnp.einsum('bhqk,bkhd->bqhd', attn, v)
        out = out.reshape(B, Sq, H * D)
        return out @ Wo

    def _L0_ffn_ref(x, W_up, W_gate, W_down):
        import jax, jax.numpy as jnp
        import numpy as np
        D_MODEL = 256
        D_EXPERT = 1024
        EPS = 1e-08

        def ternary_quant(w):
            scale = jnp.mean(jnp.abs(w)) + EPS
            q = jnp.clip(jnp.round(w / scale), -1.0, 1.0) * scale
            return w + jax.lax.stop_gradient(q - w)
        wu = ternary_quant(W_up)
        wg = ternary_quant(W_gate)
        wd = ternary_quant(W_down)
        up = jnp.einsum('bsd,ed->bse', x, wu)
        gate = jnp.einsum('bsd,ed->bse', x, wg)
        hidden = jax.nn.silu(up) * gate
        return jnp.einsum('bse,de->bsd', hidden, wd)

    def _L1_xattn_ref(x, ctx, pos_map, ctx_pos_map, Wq, Wkv, Wout, bout):
        import jax, jax.numpy as jnp
        import numpy as np
        DIM = 256
        CTX_DIM = 128
        N_HEADS = 32
        HEAD_DIM = DIM // N_HEADS
        POS_DIM = 2
        B, N, CTXN = (2, 256, 256)
        ROPE_BASE = 10000.0

        def apply_axial_rope(x, pos):
            b, n, h, d = x.shape
            p = pos.shape[-1]
            dpa = d // p
            half = dpa // 2
            freqs = ROPE_BASE ** (-jnp.arange(half, dtype=x.dtype) / half)
            ang = pos[..., :, None] * freqs
            cos = jnp.cos(ang)[:, :, None, :, :]
            sin = jnp.sin(ang)[:, :, None, :, :]
            xr = x.reshape(b, n, h, p, half, 2)
            x1, x2 = (xr[..., 0], xr[..., 1])
            out = jnp.stack([x1 * cos - x2 * sin, x1 * sin + x2 * cos], axis=-1)
            return out.reshape(b, n, h, d)
        b, n, _ = x.shape
        ctx_n = ctx.shape[1]
        q = (x @ Wq).reshape(b, n, N_HEADS, HEAD_DIM)
        k, v = jnp.split(ctx @ Wkv, 2, axis=-1)
        k = k.reshape(b, ctx_n, N_HEADS, HEAD_DIM)
        v = v.reshape(b, ctx_n, N_HEADS, HEAD_DIM)
        q = apply_axial_rope(q, pos_map)
        k = apply_axial_rope(k, ctx_pos_map)
        scale = 1.0 / np.sqrt(HEAD_DIM).astype(np.float32)
        logits = jnp.einsum('bqhd,bkhd->bhqk', q, k) * scale
        w = jax.nn.softmax(logits, axis=-1)
        attn = jnp.einsum('bhqk,bkhd->bqhd', w, v)
        attn = attn.reshape(b, n, N_HEADS * HEAD_DIM)
        return attn @ Wout + bout

    def _L1_ffn_ref(hidden_states, gate_w, w_gate, w_up, w_down):
        import jax, jax.numpy as jnp
        import numpy as np
        B, S, D = (2, 128, 256)
        E, F, TOP_K = (8, 176, 2)
        b, s, d = hidden_states.shape
        e = gate_w.shape[0]
        x = hidden_states.reshape(-1, d)
        t = x.shape[0]
        logits = x @ gate_w.T
        probs = jax.nn.softmax(logits.astype(jnp.float32), axis=-1)
        top_w, sel = jax.lax.top_k(probs, TOP_K)
        top_w = top_w / jnp.sum(top_w, axis=-1, keepdims=True)
        top_w = top_w.astype(logits.dtype)
        w_te = jnp.zeros((t, e), logits.dtype).at[jnp.arange(t)[:, None], sel].add(top_w)
        g = jnp.einsum('td,edf->tef', x, w_gate)
        u = jnp.einsum('td,edf->tef', x, w_up)
        h = jax.nn.silu(g) * u
        out = jnp.einsum('tef,efd->td', h * w_te[:, :, None], w_down)
        return out.reshape(b, s, d)
    x = x + jnp.tanh(g_xattn[0]) * _L0_xattn_ref(_layernorm(x, axis=-1), ctx_1024, L0_xattn_Wq, L0_xattn_Wk, L0_xattn_Wv, L0_xattn_Wo, L0_xattn_gq, L0_xattn_gk)
    x = x + jnp.tanh(g_ffn[0]) * _L0_ffn_ref(_layernorm(x, axis=-1), L0_ffn_W_up, L0_ffn_W_gate, L0_ffn_W_down)
    x = x + jnp.tanh(g_xattn[1]) * _L1_xattn_ref(_layernorm(x, axis=-1), ctx_1024, fside_BxSx2_0, fside_BxSx2_0, L1_xattn_Wq, L1_xattn_Wkv, L1_xattn_Wout, L1_xattn_bout)
    x = x + jnp.tanh(g_ffn[1]) * _L1_ffn_ref(_layernorm(x, axis=-1), L1_ffn_gate_w, L1_ffn_w_gate, L1_ffn_w_up, L1_ffn_w_down)
    return x

_drawn_inputs = setup_inputs


def setup_inputs(seed=0):
    import zlib

    import numpy as np

    out = dict(_drawn_inputs(seed))
    spreads = {'g_ffn': (-1.0, 0.6),
     'L0_xattn_gq': (1.0, 0.544),
     'L0_xattn_gk': (1.0, 0.6),
     'L1_xattn_bout': (0.0, 0.1)}
    factors = {'L1_ffn_gate_w': 8.0, 'L1_ffn_w_gate': 8.0, 'L1_ffn_w_up': 8.0, 'L1_ffn_w_down': 8.0}
    for name, (base, spread) in spreads.items():
        noise = np.random.default_rng([zlib.crc32(name.encode()), seed]).standard_normal(out[name].shape)
        drawn = base * np.exp(spread * noise) if base else spread * noise
        out[name] = jnp.asarray(drawn.astype(out[name].dtype))
    for name, factor in factors.items():
        out[name] = (out[name] * factor).astype(out[name].dtype)
    return out
```

```python
import math
from contextlib import ExitStack

import concourse.bass as bass
from concourse import mybir

F32 = mybir.dt.float32
F32R = mybir.dt.float32r
F16 = mybir.dt.float16
U32 = mybir.dt.uint32
ALU = mybir.AluOpType
ACT = mybir.ActivationFunctionType
AX = mybir.AxisListType

P = 128
GROUPS = 4
HG = 4
BANK = 512


def is_batch(b, batches):
    return not isinstance(b, int) or 0 <= b < batches


def wait_ge(engine, semaphore, value):
    if not isinstance(value, int) or value > 0:
        engine.wait_ge(semaphore, value)


def back(b, g, n):
    return (b, g - n) if g >= n else (b - 1, g - n + GROUPS)


def build(nc, io):
    B, S, D = io["x"].shape
    C = io["ctxT"].shape[0]
    INNER = io["Wq0"].shape[1]
    KT = D // P
    E0 = io["WuT"].shape[1]
    ET = E0 // P
    assert S == P and C == P and INNER == GROUPS * BANK and E0 == 2 * BANK and KT == 2
    SLOTS = B * GROUPS
    EX, _, CH = io["e_gate"].shape
    F2 = EX * CH
    D1 = 8
    H1 = D // D1
    L1_CHUNKS = 1 + EX // 2 + 2
    assert F2 % P == 0

    with ExitStack() as ctx:
        def sb(name, shape, dt=F32):
            return ctx.enter_context(nc.sbuf_tensor(name, shape, dt))

        def sem(name):
            return ctx.enter_context(nc.semaphore(name))

        bank = [ctx.enter_context(nc.psum_tensor(f"bank{n}", [P, BANK], F32)) for n in range(8)]
        q_bank, k_bank, v_bank, tq_bank, tk_bank, s_bank, o_bank, y_bank = bank

        X = sb("X", [P, B, D])
        W1h = sb("W1h", [P, GROUPS, 4, BANK], F32R)
        W1l = sb("W1l", [P, GROUPS, 4, BANK], F32R)
        Woh = sb("Woh", [P, INNER // P, D], F32R)
        Wol = sb("Wol", [P, INNER // P, D], F32R)
        T = sb("T", [P, 3, 4 * BANK], F32R)
        stage = sb("stage", [P, 2, 4 * BANK])
        ctxT = sb("ctxT_sb", [P, B, P])

        ident = sb("ident", [P, P])
        ones = sb("ones", [P, P])
        neg_half = sb("neg_half", [P, 2 * HG])
        gains = sb("gains", [P, 2])
        gqk = sb("gqk", [P, 1])
        gates = sb("gates", [P, 4])
        tgates = sb("tgates", [P, 4])
        wsum = sb("wsum", [P, 3])
        wscale = sb("wscale", [P, 3])
        half_up = sb("half_up", [P, 1])
        th = sb("th", [P, 3])
        nth = sb("nth", [P, 3])
        ffn_scale = sb("ffn_scale", [P, 2])

        stats = sb("stats", [P, 2, 6])
        mv = sb("mv", [P, 2, 2])
        var = sb("var", [P, 2])
        rstd = sb("rstd", [P, 2])
        xn = sb("xn", [P, 2, D])
        xaT = sb("xaT", [P, 2, D], F32R)
        cT = sb("cT", [P, 2, P], F32R)
        ss = sb("ss", [P, 2 * HG])
        rs = sb("rs", [P, 2 * HG])
        Qs = sb("Qs", [P, HG, P])
        Ks = sb("Ks", [P, HG, P])
        QT = sb("QT", [P, 2, BANK])
        KTr = sb("KTr", [P, 2, BANK])
        V = sb("V", [P, GROUPS, BANK])
        mx = sb("mx", [P, HG])
        Pr = sb("Pr", [P, HG, P])
        rsum = sb("rsum", [P, HG])
        rinv = sb("rinv", [P, HG])
        PT = sb("PT", [P, BANK])
        OTh = sb("OTh", [P, 2, BANK], F32R)
        OTl = sb("OTl", [P, 2, BANK], F32R)
        xfT = sb("xfT", [P, 2, D], F32R)
        H = sb("H", [P, 2, BANK])
        HTh = sb("HTh", [P, 2, BANK], F32R)
        HTl = sb("HTl", [P, 2, BANK], F32R)

        ident16 = sb("ident16", [P, P], F16)
        btg = sb("btg", [P, D])
        pos = sb("pos_sb", [P, B, 2])
        ang = sb("ang", [P, 2, B, 2, 2])
        turns = sb("turns", [P, 8 * B])
        trig = sb("trig", [P, 2, B, 2, 2])
        cos8 = sb("cos8", [P, B, D1])
        sin8 = sb("sin8", [P, B, D1])
        Mx = sb("Mx", [P, H1])
        Mr = sb("Mr", [P, H1])
        rz = sb("rz", [P, H1])
        iota8 = sb("iota8", [P, EX])
        lg, top, w_one, w_two, w_te = (sb(n, [P, EX]) for n in ("lg", "top", "w_one", "w_two", "w_te"))
        topi = sb("topi", [P, EX], U32)
        topf = sb("topf", [P, 2])
        gap = sb("gap", [P, 1])
        rw = sb("rw", [P, 6])
        ang_flat = ang[:, :, :, :, :].rearrange("p k b s f -> p (k b s f)")

        x_in = [sem(f"x_in{n}") for n in range(2)]
        ctx_in, small_in = sem("ctx_in"), sem("small_in")
        stage_in = [sem("stage_in0"), sem("stage_in1")]
        stage_hi, stage_lo = sem("stage_hi"), sem("stage_lo")
        consts, gains_done, gates_done = sem("consts"), sem("gains_done"), sem("gates_done")
        wsum_done, wtot_done, wscale_done = sem("wsum_done"), sem("wtot_done"), sem("wscale_done")
        low_done, sign_done = sem("low_done"), sem("sign_done")
        stats_done, aggr_done, eps_done, rstd_done, xn_done = (sem(n) for n in (
            "stats_done", "aggr_done", "eps_done", "rstd_done", "xn_done"))
        fstats_done, faggr_done, feps_done, frstd_done, fxn_done = (sem(n) for n in (
            "fstats_done", "faggr_done", "feps_done", "frstd_done", "fxn_done"))
        xt_done, xt_hi, xt_lo, c_hi, c_lo = (sem(n) for n in ("xt_done", "xt_hi", "xt_lo", "c_hi", "c_lo"))
        q_proj, k_proj, v_proj, sq_done, ss_done, ms_done, rs_done = (sem(n) for n in (
            "q_proj", "k_proj", "v_proj", "sq_done", "ss_done", "ms_done", "rs_done"))
        q_scaled, k_scaled, v_saved, tq_done, tk_done, qt_saved, kt_saved = (sem(n) for n in (
            "q_scaled", "k_scaled", "v_saved", "tq_done", "tk_done", "qt_saved", "kt_saved"))
        s_done, mx_done, sub_done, exp_done, sum_done, rinv_done, norm_done = (sem(n) for n in (
            "s_done", "mx_done", "sub_done", "exp_done", "sum_done", "rinv_done", "norm_done"))
        pt_done, pt_saved, o_done, o_hi, o_lo, w_done, res_done = (sem(n) for n in (
            "pt_done", "pt_saved", "o_done", "o_hi", "o_lo", "w_done", "res_done"))
        ft_done, ft_hi, ft_lo, up_done, gate_done, tanh_done, act_done, hid_done = (sem(n) for n in (
            "ft_done", "ft_hi", "ft_lo", "up_done", "gate_done", "tanh_done", "act_done", "hid_done"))
        ht_done, ht_hi, ht_lo, down_done, fres_done = (sem(n) for n in (
            "ht_done", "ht_hi", "ht_lo", "down_done", "fres_done"))
        pos_in, ang_step, ang_done, trig_done, c_stats, c_aggr = (sem(n) for n in (
            "pos_in", "ang_step", "ang_done", "trig_done", "c_stats", "c_aggr"))
        c_eps, c_rstd, c_xn, c_turned, c_chi, c_clo = (sem(n) for n in (
            "c_eps", "c_rstd", "c_xn", "c_turned", "c_chi", "c_clo"))
        c_xhi, c_xlo, qkv_done, qk_saved, vn_saved, va_done = (sem(n) for n in (
            "c_xhi", "c_xlo", "qkv_done", "qk_saved", "vn_saved", "va_done"))
        rope_a, rope_b, rope_done, stack_hi, stack_lo, t1_done = (sem(n) for n in (
            "rope_a", "rope_b", "rope_done", "stack_hi", "stack_lo", "t1_done"))
        t1_saved, sc_done, smax_done, m_split, t2_done, t2_saved = (sem(n) for n in (
            "t1_saved", "sc_done", "smax_done", "m_split", "t2_done", "t2_saved"))
        k2_saved, st_done, e_done, av_done, rz_done, on_done = (sem(n) for n in (
            "k2_saved", "st_done", "e_done", "av_done", "rz_done", "on_done"))
        ot2_done, ot2_hi, ot2_lo, w2_done, bias_added, cres_done = (sem(n) for n in (
            "ot2_done", "ot2_hi", "ot2_lo", "w2_done", "bias_added", "cres_done"))
        d_stats, d_aggr, d_eps, d_rstd, d_xn, d_turned = (sem(n) for n in (
            "d_stats", "d_aggr", "d_eps", "d_rstd", "d_xn", "d_turned"))
        d_xhi, d_xlo, route_done, route_step, gap_exp, g2_done = (sem(n) for n in (
            "d_xhi", "d_xlo", "route_done", "route_step", "gap_exp", "g2_done"))
        u2_done, g_tanh, g_act, h2_done, hw_done, h2t_done = (sem(n) for n in (
            "u2_done", "g_tanh", "g_act", "h2_done", "hw_done", "h2t_done"))
        h2t_hi, h2t_lo, dn_done, dres_done = (sem(n) for n in (
            "h2t_hi", "h2t_lo", "dn_done", "dres_done"))
        out_done = sem("out_done")

        w1h, w1l = (w[:, :, :, :].rearrange("p g m n -> p (g m n)") for w in (W1h, W1l))
        woh, wol = (w[:, :, :].rearrange("p t n -> p (t n)") for w in (Woh, Wol))
        at = 0
        place = {}
        for name, size in (("q", KT * D), ("kv", 2 * D), ("out", KT * D), ("route", KT * EX),
                           ("exp", EX // 2 * 4 * CH)):
            place[name] = at
            at += size
        assert at <= GROUPS * 4 * BANK

        def w2(name, n, size):
            a = place[name] + n * size
            return w1h[:, a:a + size], w1l[:, a:a + size]

        t_flat = T[:, :, :].rearrange("p m n -> p (m n)")
        HT2 = [t_flat[:, n * F2:(n + 1) * F2] for n in range(2)]
        OT2 = [t_flat[:, 2 * F2 + n * D:2 * F2 + (n + 1) * D] for n in range(2)]
        E2 = V
        QT1 = QT[:, 0, :].bitcast(F16).rearrange("p (t q) -> p t q", q=P)
        KT1 = QT[:, 1, :].bitcast(F16).rearrange("p (t q) -> p t q", q=P)
        QT2 = KTr[:, 0, :].bitcast(F16).rearrange("p (t q) -> p t q", q=P)
        KT2 = KTr[:, 1, :].bitcast(F16).rearrange("p (t q) -> p t q", q=P)
        qk = Qs[:, :, :].rearrange("p h d -> p (h d)")
        rot = Ks[:, :, :].rearrange("p h d -> p (h d)")
        SQ = PT[:, :].bitcast(F16).rearrange("p (h s d) -> p h s d", h=H1, s=4)
        SK = Pr[:, :, :].rearrange("p h d -> p (h d)").bitcast(F16).rearrange("p (h s d) -> p h s d", h=H1, s=4)
        h_flat = H[:, :, :].rearrange("p a n -> p (a n)")
        Vn = h_flat[:, 0:D]
        Va = h_flat[:, D:D + 9 * H1].rearrange("p (h c) -> p h c", h=H1)
        On = h_flat[:, D + 9 * H1:2 * D + 9 * H1]
        H2 = stage[:, 0, 0:F2]
        sa_bank, sb_bank, ov_bank, g_bank, u_bank, m1, m2, m3 = bank
        s_banks = (sa_bank, sb_bank)
        SG = 2 * HG

        def heads(j):
            return [HG * (HG * (j // HG) + k) + j % HG for k in range(HG)]

        CHUNK_TILES = ((0, 2), (2, 5), (5, 8), (8, 11))

        def layer1_chunk(n):
            src = stage[:, (CHUNKS + n) % 2, :]
            if n <= EX // 2:
                a = 0 if n == 0 else place["exp"] + (n - 1) * 4 * 2 * CH
                size = place["exp"] if n == 0 else 4 * 2 * CH
                return w1h[:, a:a + size], w1l[:, a:a + size], src[:, 0:size]
            a, z = ((0, 6), (6, F2 // P))[n - 1 - EX // 2]
            return woh[:, a * D:z * D], wol[:, a * D:z * D], src[:, 0:(z - a) * D]

        block = ctx.enter_context(nc.Block())

        WO, TERN = GROUPS, GROUPS + 2
        CHUNKS = TERN + 3
        SPLITS = ((1, 2), (3,), (4,), (5,))

        def chunk_ready(e, c):
            e.wait_ge(stage_in[c % 2], 64 * (c // 2 + 1))

        def body(i, slot, before=None):
            for g in range(GROUPS):
                slot(i, g)

        def loop2(slot):
            for i in range(B + 2):
                body(i, slot)

        def loop1(slot):
            for i in range(B + 2):
                body(i, slot)

        @block.sync
        def _(e):
            xd = io["x"].rearrange("b p d -> p b d")
            e.dma_start(X[:, 0:1, :], xd[:, 0:1, :]).then_inc(x_in[0], 16)
            e.dma_start(ctxT[:, :, :], io["ctxT"]).then_inc(ctx_in, 16)

            def load1(n, s, done):
                if n == 0:
                    for name, w in (("q", "Wq1"), ("kv", "Wkv1"), ("out", "Wout1"), ("route", "gwT")):
                        src = io[w].rearrange("(t p) n -> p t n", p=P)
                        size = src.shape[1] * src.shape[2]
                        e.dma_start(s[:, place[name]:place[name] + size].rearrange("p (t n) -> p t n", n=src.shape[2]),
                                    src).then_inc(done, 16)
                elif n <= EX // 2:
                    for m, w in enumerate(("e_gate", "e_up")):
                        for kt in range(KT):
                            a = (2 * m + kt) * 2 * CH
                            src = io[w][2 * n - 2:2 * n, kt * P:(kt + 1) * P, :].rearrange("e p f -> p e f")
                            e.dma_start(s[:, a:a + 2 * CH].rearrange("p (e f) -> p e f", f=CH), src).then_inc(done, 16)
                else:
                    a, z = ((0, 6), (6, F2 // P))[n - 1 - EX // 2]
                    src = io["e_down"].rearrange("e f d -> (e f) d").rearrange("(t p) d -> p t d", p=P)
                    e.dma_start(s[:, 0:(z - a) * D].rearrange("p (t d) -> p t d", d=D), src[:, a:z, :])\
                     .then_inc(done, 64)

            def load(c):
                s = stage[:, c % 2, :]
                if c >= 2:
                    if c - 2 < TERN:
                        e.wait_ge(stage_lo, c - 1)
                    elif c - 2 < CHUNKS:
                        e.wait_ge(sign_done, c - 2 - TERN + 1)
                    else:
                        e.wait_ge(stage_lo, TERN + c - 2 - CHUNKS + 1)
                if c < WO:
                    cols = slice(c * BANK, (c + 1) * BANK)
                    for kt in range(KT):
                        e.dma_start(s[:, kt * BANK:(kt + 1) * BANK],
                                    io["Wq0"][kt * P:(kt + 1) * P, cols]).then_inc(stage_in[c % 2], 16)
                    e.dma_start(s[:, 2 * BANK:3 * BANK], io["Wk0"][:, cols]).then_inc(stage_in[c % 2], 16)
                    e.dma_start(s[:, 3 * BANK:4 * BANK], io["Wv0"][:, cols]).then_inc(stage_in[c % 2], 16)
                elif c < TERN:
                    n = INNER // P // 2
                    src = io["Wo0"].rearrange("(t p) n -> p t n", p=P)[:, (c - WO) * n:(c - WO + 1) * n, :]
                    e.dma_start(s.rearrange("p (t n) -> p t n", n=D), src).then_inc(stage_in[c % 2], 64)
                elif c >= CHUNKS:
                    load1(c - CHUNKS, s, stage_in[c % 2])
                else:
                    src = io[("WuT", "WgT", "WdT")[c - TERN]].rearrange("(t p) n -> p t n", p=P)
                    e.dma_start(s.rearrange("p (t n) -> p t n", n=src.shape[2]), src)\
                     .then_inc(stage_in[c % 2], 64)

            load(0)
            e.dma_start(gains[:, 0:1], io["gq"].rearrange("(p a) -> p a", a=1)).then_inc(small_in, 16)
            e.dma_start(gains[:, 1:2], io["gk"].rearrange("(p a) -> p a", a=1)).then_inc(small_in, 16)
            e.dma_start(gates[:, 0:2], io["g_xattn"].rearrange("(a n) -> a n", a=1).to_broadcast([P, 2]))\
             .then_inc(small_in, 16)
            e.dma_start(gates[:, 2:4], io["g_ffn"].rearrange("(a n) -> a n", a=1).to_broadcast([P, 2]))\
             .then_inc(small_in, 16)
            load(1)
            e.dma_start(X[:, 1:B, :], xd[:, 1:B, :]).then_inc(x_in[1], 16)
            for c in range(2, CHUNKS):
                load(c)
            e.dma_start(pos[:, :, :], io["pos"].rearrange("b p a -> p b a")).then_inc(pos_in, 16)
            e.dma_start(btg[:, :], io["bout"].rearrange("(a n) -> a n", a=1).to_broadcast([P, D])).then_inc(pos_in, 32)
            for c in range(CHUNKS, CHUNKS + L1_CHUNKS):
                load(c)

            def slot2(i, g):
                if g == 2 and is_batch(i - 2, B):
                    e.wait_ge(dres_done, i - 1)
                    e.dma_start(io["out"][i - 2], X[:, i - 2, :]).then_inc(out_done, 16)

            loop2(slot2)
            e.wait_ge(out_done, 16 * B)

        @block.gpsimd
        def _(e):
            e.memset(ident[:, :], 0.0).then_inc(consts, 1)
            e.memset(ones[:, :], 1.0).then_inc(consts, 1)
            e.memset(neg_half[:, :], -0.5).then_inc(consts, 1)
            e.wait_ge(consts, 3)
            e.affine_select(out=ident[:, :], in_=ident[:, :], compare_op=ALU.not_equal, fill=1.0,
                            base=0, pattern=[[-1, P]], channel_multiplier=1).then_inc(consts, 1)
            e.wait_ge(consts, 4)
            e.tensor_copy(ident16[:, :], ident[:, :]).then_inc(consts, 1)

            def ln_rstd(b, n, aggr, eps, done, used):
                e.wait_ge(aggr, b + 1)
                wait_ge(e, used, b)
                e.tensor_scalar(var[:, n:n + 1], mv[:, n, 1:2], 1e-5, None, ALU.add).then_inc(eps, 1)
                e.wait_ge(eps, b + 1)
                e.tensor_tensor(rstd[:, n:n + 1], var[:, n:n + 1], neg_half[:, 0:1], ALU.pow).then_inc(done, 1)

            ln_rstd(0, 0, aggr_done, eps_done, rstd_done, xn_done)

            def slot(i, g):
                if g == 2 and is_batch(i - 1, B):
                    ln_rstd(i - 1, 1, faggr_done, feps_done, frstd_done, fxn_done)
                if is_batch(i, B):
                    t = GROUPS * i + g
                    e.wait_ge(ss_done, 2 * t + 2)
                    wait_ge(e, q_scaled, t)
                    wait_ge(e, k_scaled, t)
                    e.tensor_scalar(rs[:, :], ss[:, :], 1.0 / P, 1e-5, ALU.mult, ALU.add).then_inc(ms_done, 1)
                    e.wait_ge(ms_done, t + 1)
                    e.tensor_tensor(rs[:, :], rs[:, :], neg_half[:, :], ALU.pow).then_inc(rs_done, 1)
                b, h = back(i, g, 1)
                if is_batch(b, B):
                    t = GROUPS * b + h
                    e.wait_ge(rinv_done, t + 1)
                    e.tensor_tensor(Pr[:, :, :], Pr[:, :, :],
                                    rinv[:, :].unsqueeze(2).to_broadcast([P, HG, P]), ALU.mult)\
                     .then_inc(norm_done, 1)
                if g == 2 and is_batch(i, B) and is_batch(i + 1, B):
                    ln_rstd(i + 1, 0, aggr_done, eps_done, rstd_done, xn_done)

            loop1(slot)

            def ln_rstd2(b, n, aggr, eps, done, used):
                e.wait_ge(aggr, b + 1)
                wait_ge(e, used, b)
                e.tensor_scalar(var[:, n:n + 1], mv[:, n, 1:2], 1e-5, None, ALU.add).then_inc(eps, 1)
                e.wait_ge(eps, b + 1)
                e.tensor_tensor(rstd[:, n:n + 1], var[:, n:n + 1], neg_half[:, 0:1], ALU.pow).then_inc(done, 1)

            def add_bias(b):
                e.wait_ge(c_xn, b + 1)
                e.tensor_tensor(X[:, b, :], X[:, b, :], btg[:, :], ALU.add).then_inc(bias_added, 1)

            def move_v(b):
                e.wait_ge(vn_saved, b + 1)
                wait_ge(e, av_done, SG * b)
                e.tensor_copy(Va[:, :, 0:D1], Vn.rearrange("p (h d) -> p h d", h=H1)).then_inc(va_done, 1)

            def weigh(b, c):
                n = 4 * b + c
                v = H2[:, c * 2 * CH:(c + 1) * 2 * CH].rearrange("p (e f) -> p e f", e=2)
                e.wait_ge(h2_done, n + 1)
                e.wait_ge(route_step, 12 * b + 12)
                e.tensor_tensor(v, v, w_te[:, 2 * c:2 * c + 2].unsqueeze(2).to_broadcast([P, 2, CH]), ALU.mult)\
                 .then_inc(hw_done, 1)

            for k in range(EX):
                e.memset(iota8[:, k:k + 1], float(k)).then_inc(consts, 1)
            e.wait_ge(fres_done, B)
            e.memset(SQ[:, :, 3, :], 0.0).then_inc(consts, 1)
            e.memset(SK[:, :, 3, 3:D1], 0.0).then_inc(consts, 1)
            e.memset(SK[:, :, 3, 0:3], -64.0).then_inc(consts, 1)
            e.memset(Va[:, :, D1:D1 + 1], 1.0).then_inc(consts, 1)
            ln_rstd2(0, 0, c_aggr, c_eps, c_rstd, c_xn)
            add_bias(0)

            def slot2(i, g):
                if g == 0:
                    if is_batch(i, B):
                        move_v(i)
                    if is_batch(i - 1, B):
                        ln_rstd2(i - 1, 1, d_aggr, d_eps, d_rstd, d_xn)
                    if is_batch(i - 2, B):
                        weigh(i - 2, 3)
                if g == 1:
                    if is_batch(i - 1, B):
                        weigh(i - 1, 0)
                    if is_batch(i, B) and is_batch(i + 1, B):
                        ln_rstd2(i + 1, 0, c_aggr, c_eps, c_rstd, c_xn)
                if g == 2:
                    if is_batch(i - 1, B):
                        weigh(i - 1, 1)
                    if is_batch(i, B) and is_batch(i + 1, B):
                        add_bias(i + 1)
                if g == 3 and is_batch(i - 1, B):
                    weigh(i - 1, 2)

            loop2(slot2)

        @block.scalar
        def _(e):
            def split_chunk_hi(c):
                chunk_ready(e, c)
                dst = W1h[:, c, :, :] if c < WO else \
                    Woh[:, (c - WO) * 8:(c - WO + 1) * 8, :]
                e.activation(dst, stage[:, c % 2, :].rearrange("p (t n) -> p t n", n=dst.shape[2]), ACT.Copy)\
                 .then_inc(stage_hi, 1)

            def prep(b):
                wait_ge(e, v_proj, GROUPS * b)
                e.activation(cT[:, 0, :], ctxT[:, b, :], ACT.Copy).then_inc(c_hi, 1)
                e.wait_ge(xt_done, b + 1)
                e.activation(xaT[:, 0, :], v_bank[:, 0:D], ACT.Copy).then_inc(xt_hi, 1)

            e.wait_ge(small_in, 64)
            e.activation(tgates[:, :], gates[:, :], ACT.Tanh).then_inc(gates_done, 1)
            e.wait_ge(ctx_in, 16)
            split_chunk_hi(0)
            prep(0)

            def slot(i, g):
                t = GROUPS * i + g
                if is_batch(i, B):
                    e.wait_ge(q_proj, t + 1)
                    wait_ge(e, tq_done, t)
                    e.activation(Qs[:, :, :], q_bank[:, :].rearrange("p (h d) -> p h d", h=HG), ACT.Square)\
                     .then_inc(sq_done, 1)
                    e.wait_ge(k_proj, t + 1)
                    wait_ge(e, tk_done, t)
                    e.activation(Ks[:, :, :], k_bank[:, :].rearrange("p (h d) -> p h d", h=HG), ACT.Square)\
                     .then_inc(sq_done, 1)
                    e.wait_ge(v_proj, t + 1)
                    wait_ge(e, o_done, t - 3)
                    e.activation(V[:, g, :], v_bank[:, :], ACT.Copy).then_inc(v_saved, 1)
                if i == 0:
                    for c in SPLITS[g]:
                        split_chunk_hi(c)
                b, h = back(i, g, 2)
                if is_batch(b, B):
                    u = GROUPS * b + h
                    e.wait_ge(o_done, u + 1)
                    wait_ge(e, w_done, u - 1)
                    e.activation(OTh[:, h % 2, :], o_bank[:, :], ACT.Copy).then_inc(o_hi, 1)
                b, h = back(i, g, 1)
                if is_batch(b, B):
                    u = GROUPS * b + h
                    e.wait_ge(sub_done, u + 1)
                    e.activation(Pr[:, :, :], Pr[:, :, :], ACT.Exp, scale=float(P) ** -0.5)\
                     .then_inc(exp_done, 1)
                if g == 2 and is_batch(i - 1, B):
                    b = i - 1
                    e.wait_ge(ft_done, b + 1)
                    wait_ge(e, gate_done, 2 * b)
                    e.activation(xfT[:, 0, :], tk_bank[:, 0:D], ACT.Copy).then_inc(ft_hi, 1)
                for half, (fg, lag) in enumerate(((3, 1), (0, 2))):
                    b = i - lag
                    if g == fg and is_batch(b, B):
                        if half == 0 and isinstance(b, int) and b == 0:
                            e.wait_ge(wscale_done, 1)
                        e.wait_ge(up_done, 2 * b + half + 1)
                        wait_ge(e, ht_done, 2 * b + half - 1)
                        e.activation(H[:, half, :], k_bank[:, :], ACT.Tanh, scale=half_up[:, 0:1])\
                         .then_inc(tanh_done, 1)
                for half, fg in enumerate((0, 1)):
                    b = i - 2
                    if g == fg and is_batch(b, B):
                        e.wait_ge(ht_done, 2 * b + half + 1)
                        wait_ge(e, down_done, b)
                        e.activation(HTh[:, half, :], tk_bank[:, :], ACT.Copy).then_inc(ht_hi, 1)
                if is_batch(i, B):
                    e.wait_ge(tq_done, t + 1)
                    wait_ge(e, s_done, t - 1)
                    e.activation(QT[:, g % 2, :], tq_bank[:, :], ACT.Copy).then_inc(qt_saved, 1)
                    e.wait_ge(tk_done, t + 1)
                    if isinstance(i, int) and t == 0:
                        e.wait_ge(gains_done, 1)
                    e.activation(KTr[:, g % 2, :], tk_bank[:, :], ACT.Copy, scale=gqk[:, 0:1])\
                     .then_inc(kt_saved, 1)
                    if g == 3 and is_batch(i + 1, B):
                        prep(i + 1)

            loop1(slot)

            def split_hi(n):
                chunk_ready(e, CHUNKS + n)
                hi, lo, src = layer1_chunk(n)
                e.activation(hi, src, ACT.Copy).then_inc(stage_hi, 1)

            def c_inputs(b):
                e.activation(cT[:, 0, :], ctxT[:, b, :], ACT.Copy).then_inc(c_chi, 1)
                e.wait_ge(c_turned, b + 1)
                e.activation(xaT[:, 0, :], m1[:, 0:D], ACT.Copy).then_inc(c_xhi, 1)

            def c_save(b):
                e.wait_ge(qkv_done, b + 1)
                e.activation(qk[:, 0:D], m1[:, D:2 * D], ACT.Copy)
                e.activation(qk[:, D:2 * D], m2[:, 0:D], ACT.Copy).then_inc(qk_saved, 1)
                wait_ge(e, va_done, b)
                e.activation(Vn, m2[:, D:2 * D], ACT.Copy).then_inc(vn_saved, 1)

            def c_stack(b):
                r3 = rot.rearrange("p (s h d) -> p s h d", s=2, d=D1)
                e.wait_ge(rope_done, b + 1)
                wait_ge(e, t2_done, b)
                two = [P, H1, 2, D1]
                e.activation(SQ[:, :, 0:2, :], r3[:, 0].unsqueeze(2).to_broadcast(two), ACT.Copy).then_inc(stack_hi, 1)
                e.activation(SK[:, :, 0:3:2, :], r3[:, 1].unsqueeze(2).to_broadcast(two), ACT.Copy)\
                 .then_inc(stack_hi, 1)

            def exp_group(b, j):
                e.wait_ge(st_done, SG * b + j + 1)
                wait_ge(e, av_done, SG * b + j - 3)
                e.activation(E2[:, j % 4, :], s_banks[j % 2][:, :], ACT.Exp, scale=float(D1) ** -0.5)\
                 .then_inc(e_done, 1)

            def ot2_save(b):
                e.wait_ge(ot2_done, b + 1)
                e.activation(OT2[0], m1[:, 0:D], ACT.Copy).then_inc(ot2_hi, 1)

            def d_inputs(b):
                e.wait_ge(d_turned, b + 1)
                wait_ge(e, u2_done, 4 * b)
                e.activation(xfT[:, 0, :], m1[:, 0:D], ACT.Copy).then_inc(d_xhi, 1)

            def route(b):
                e.wait_ge(route_step, 12 * b + 5)
                e.activation(rw[:, 1:2], gap[:, :], ACT.Exp).then_inc(gap_exp, 1)

            def tanh_chunk(b, c):
                n = 4 * b + c
                e.wait_ge(g2_done, n + 1)
                if c == 3:
                    wait_ge(e, h2t_done, 4 * b)
                else:
                    wait_ge(e, h2t_done, 4 * (b - 1) + c + 2)
                e.activation(H2[:, c * 2 * CH:(c + 1) * 2 * CH], g_bank[:, 0:2 * CH], ACT.Tanh, scale=0.5)\
                 .then_inc(g_tanh, 1)

            def ht_hi2(b, c):
                a, z = CHUNK_TILES[c]
                e.wait_ge(h2t_done, 4 * b + c + 1)
                wait_ge(e, dn_done, b)
                e.activation(HT2[0][:, a * P:z * P], m3[:, 0:(z - a) * P], ACT.Copy).then_inc(h2t_hi, 1)

            e.wait_ge(ang_done, 1)
            e.activation(trig[:, :, :, :, :], ang[:, :, :, :, :], ACT.Sin).then_inc(trig_done, 1)
            e.wait_ge(fres_done, B)
            for n in range(L1_CHUNKS):
                split_hi(n)
            c_inputs(0)
            c_save(0)
            c_stack(0)

            def slot2(i, g):
                if g == 0:
                    if is_batch(i - 1, B):
                        ot2_save(i - 1)
                    if is_batch(i - 2, B):
                        tanh_chunk(i - 2, 3)
                        ht_hi2(i - 2, 2)
                if g == 1:
                    if is_batch(i, B):
                        e.wait_ge(t1_saved, 2 * i + 2)
                        wait_ge(e, st_done, SG * i)
                        e.activation(KT2.rearrange("p t q -> p (t q)"), KT1.rearrange("p t q -> p (t q)"), ACT.Copy)\
                         .then_inc(k2_saved, 1)
                    if is_batch(i - 1, B):
                        d_inputs(i - 1)
                    if is_batch(i - 2, B):
                        ht_hi2(i - 2, 3)
                    if is_batch(i, B):
                        exp_group(i, 0)
                        exp_group(i, 1)
                    if is_batch(i - 1, B):
                        route(i - 1)
                        tanh_chunk(i - 1, 0)
                    if is_batch(i, B):
                        exp_group(i, 2)
                if g == 2:
                    if is_batch(i, B):
                        exp_group(i, 3)
                    if is_batch(i - 1, B):
                        tanh_chunk(i - 1, 1)
                        ht_hi2(i - 1, 0)
                    if is_batch(i, B) and is_batch(i + 1, B):
                        wait_ge(e, qkv_done, i + 1)
                        c_inputs(i + 1)
                    if is_batch(i, B):
                        exp_group(i, 4)
                        exp_group(i, 5)
                    if is_batch(i, B) and is_batch(i + 1, B):
                        c_save(i + 1)
                if g == 3:
                    if is_batch(i, B):
                        exp_group(i, 6)
                    if is_batch(i - 1, B):
                        tanh_chunk(i - 1, 2)
                    if is_batch(i, B):
                        exp_group(i, 7)
                    if is_batch(i, B) and is_batch(i + 1, B):
                        c_stack(i + 1)
                    if is_batch(i - 1, B):
                        ht_hi2(i - 1, 1)

            loop2(slot2)

        @block.vector
        def _(e):
            def split_chunk_lo(c):
                e.wait_ge(stage_hi, c + 1)
                dst, hi = (W1l[:, c, :, :], W1h[:, c, :, :]) if c < WO else \
                    (Wol[:, (c - WO) * 8:(c - WO + 1) * 8, :], Woh[:, (c - WO) * 8:(c - WO + 1) * 8, :])
                e.tensor_tensor(dst, stage[:, c % 2, :].rearrange("p (t n) -> p t n", n=dst.shape[2]),
                                hi.bitcast(F32), ALU.subtract).then_inc(stage_lo, 1)

            def signs(n):
                c = TERN + n
                w, t = stage[:, c % 2, :], T[:, n, :]
                chunk_ready(e, c)
                e.tensor_reduce(wsum[:, n:n + 1], w, AX.X, ALU.add, apply_absolute_value=True)\
                 .then_inc(wsum_done, 1)
                e.wait_ge(wtot_done, n + 1)
                e.tensor_scalar(wscale[:, n:n + 1], y_sum[:, n:n + 1], 1.0 / (4 * BANK * P), 1e-8,
                                ALU.mult, ALU.add).then_inc(low_done, 1)
                e.wait_ge(low_done, 4 * n + 1)
                e.tensor_scalar(th[:, n:n + 1], wscale[:, n:n + 1], 0.5, None, ALU.mult).then_inc(low_done, 1)
                e.tensor_scalar(nth[:, n:n + 1], wscale[:, n:n + 1], -0.5, None, ALU.mult).then_inc(low_done, 1)
                e.wait_ge(low_done, 4 * n + 3)
                e.tensor_scalar(t, w, nth[:, n:n + 1], None, ALU.is_lt).then_inc(low_done, 1)
                e.wait_ge(low_done, 4 * n + 4)
                e.scalar_tensor_tensor(out=t, in0=w, scalar=th[:, n:n + 1], in1=t.bitcast(F32),
                                       op0=ALU.is_gt, op1=ALU.subtract).then_inc(sign_done, 1)

            y_sum = v_bank[:, D:D + 3]

            def ln_stats(b, n, stats_sem, aggr_sem, src):
                wait_ge(e, (rstd_done, frstd_done)[n], b)
                e.bn_stats(stats[:, n, :], src).then_inc(stats_sem, 1)
                e.wait_ge(stats_sem, b + 1)
                e.bn_aggr(mv[:, n, :], stats[:, n, :]).then_inc(aggr_sem, 1)

            def ln_apply(b, n, rstd_sem, done, src, turned):
                e.wait_ge(rstd_sem, b + 1)
                wait_ge(e, turned, b)
                e.tensor_scalar(xn[:, n, :], src, mv[:, n, 0:1], rstd[:, n:n + 1], ALU.subtract, ALU.mult)\
                 .then_inc(done, 1)

            def prep(b):
                e.wait_ge(c_hi, b + 1)
                e.tensor_tensor(cT[:, 1, :], ctxT[:, b, :], cT[:, 0, :].bitcast(F32), ALU.subtract)\
                 .then_inc(c_lo, 1)
                e.wait_ge(xt_hi, b + 1)
                e.tensor_tensor(xaT[:, 1, :], v_bank[:, 0:D], xaT[:, 0, :].bitcast(F32), ALU.subtract)\
                 .then_inc(xt_lo, 1)

            e.wait_ge(x_in[0], 16)
            ln_stats(0, 0, stats_done, aggr_done, X[:, 0, :])
            e.wait_ge(small_in, 64)
            e.tensor_tensor(gqk[:, :], gains[:, 0:1], gains[:, 1:2], ALU.mult).then_inc(gains_done, 1)
            ln_apply(0, 0, rstd_done, xn_done, X[:, 0, :], xt_done)
            split_chunk_lo(0)
            prep(0)

            def slot(i, g):
                t = GROUPS * i + g
                if g == 2 and is_batch(i - 1, B):
                    b = i - 1
                    e.wait_ge(w_done, GROUPS * b + GROUPS)
                    e.scalar_tensor_tensor(out=X[:, b, :], in0=y_bank[:, 0:D], scalar=tgates[:, 0:1],
                                           in1=X[:, b, :], op0=ALU.mult, op1=ALU.add).then_inc(res_done, 1)
                    e.wait_ge(res_done, b + 1)
                    ln_stats(b, 1, fstats_done, faggr_done, X[:, b, :])
                if is_batch(i, B):
                    wait_ge(e, rs_done, t)
                    e.wait_ge(sq_done, 2 * t + 1)
                    e.tensor_reduce(ss[:, 0:HG], Qs[:, :, :], AX.X, ALU.add).then_inc(ss_done, 1)
                    e.wait_ge(sq_done, 2 * t + 2)
                    e.tensor_reduce(ss[:, HG:2 * HG], Ks[:, :, :], AX.X, ALU.add).then_inc(ss_done, 1)
                if i == 0:
                    for c in SPLITS[g]:
                        split_chunk_lo(c)
                if g == 2 and is_batch(i - 1, B):
                    b = i - 1
                    ln_apply(b, 1, frstd_done, fxn_done, X[:, b, :], ft_done)
                b, h = back(i, g, 1)
                if is_batch(b, B):
                    u = GROUPS * b + h
                    sc = s_bank[:, :].rearrange("p (h k) -> p h k", h=HG)
                    e.wait_ge(s_done, u + 1)
                    e.tensor_reduce(mx[:, :], sc, AX.X, ALU.max).then_inc(mx_done, 1)
                    e.wait_ge(mx_done, u + 1)
                    wait_ge(e, pt_done, u)
                    e.tensor_tensor(Pr[:, :, :], sc, mx[:, :].unsqueeze(2).to_broadcast([P, HG, P]),
                                    ALU.subtract).then_inc(sub_done, 1)
                if is_batch(i, B):
                    e.wait_ge(rs_done, t + 1)
                    e.tensor_tensor(Qs[:, :, :], q_bank[:, :].rearrange("p (h d) -> p h d", h=HG),
                                    rs[:, 0:HG].unsqueeze(2).to_broadcast([P, HG, P]), ALU.mult)\
                     .then_inc(q_scaled, 1)
                    e.tensor_tensor(Ks[:, :, :], k_bank[:, :].rearrange("p (h d) -> p h d", h=HG),
                                    rs[:, HG:2 * HG].unsqueeze(2).to_broadcast([P, HG, P]), ALU.mult)\
                     .then_inc(k_scaled, 1)
                b, h = back(i, g, 2)
                if is_batch(b, B):
                    e.wait_ge(o_hi, GROUPS * b + h + 1)
                    e.tensor_tensor(OTl[:, h % 2, :], o_bank[:, :], OTh[:, h % 2, :].bitcast(F32),
                                    ALU.subtract).then_inc(o_lo, 1)
                b, h = back(i, g, 1)
                if is_batch(b, B):
                    u = GROUPS * b + h
                    e.wait_ge(exp_done, u + 1)
                    e.tensor_reduce(rsum[:, :], Pr[:, :, :], AX.X, ALU.add).then_inc(sum_done, 1)
                    e.wait_ge(sum_done, u + 1)
                    wait_ge(e, norm_done, u)
                    e.reciprocal(rinv[:, :], rsum[:, :]).then_inc(rinv_done, 1)
                if g == 2 and is_batch(i, B) and is_batch(i + 1, B):
                    if isinstance(i, int) and i == 0:
                        e.wait_ge(x_in[1], 16)
                    ln_stats(i + 1, 0, stats_done, aggr_done, X[:, i + 1, :])
                if g == 3 and is_batch(i, B) and is_batch(i + 1, B):
                    ln_apply(i + 1, 0, rstd_done, xn_done, X[:, i + 1, :], xt_done)
                if i == 1 and g < 2:
                    signs(g)
                if i == 1 and g == 2:
                    signs(2)
                    e.tensor_scalar(half_up[:, :], wscale[:, 0:1], 0.5, None, ALU.mult).then_inc(wscale_done, 1)
                    e.tensor_tensor(ffn_scale[:, 0:1], wscale[:, 1:2], wscale[:, 2:3], ALU.mult)\
                     .then_inc(wscale_done, 1)
                    e.wait_ge(wscale_done, 2)
                    e.scalar_tensor_tensor(out=ffn_scale[:, 0:1], in0=ffn_scale[:, 0:1], scalar=half_up[:, 0:1],
                                           in1=tgates[:, 2:3], op0=ALU.mult, op1=ALU.mult)\
                     .then_inc(wscale_done, 1)
                if g == 2 and is_batch(i - 1, B):
                    b = i - 1
                    e.wait_ge(ft_hi, b + 1)
                    e.tensor_tensor(xfT[:, 1, :], tk_bank[:, 0:D], xfT[:, 0, :].bitcast(F32), ALU.subtract)\
                     .then_inc(ft_lo, 1)
                for half, (fg, lag) in enumerate(((3, 1), (0, 2))):
                    b = i - lag
                    if g == fg and is_batch(b, B):
                        n = 2 * b + half
                        e.wait_ge(tanh_done, n + 1)
                        e.scalar_tensor_tensor(out=H[:, half, :], in0=H[:, half, :], scalar=1.0, in1=k_bank[:, :],
                                               op0=ALU.add, op1=ALU.mult).then_inc(act_done, 1)
                        e.wait_ge(act_done, n + 1)
                        e.wait_ge(gate_done, n + 1)
                        e.tensor_tensor(H[:, half, :], H[:, half, :], q_bank[:, :], ALU.mult).then_inc(hid_done, 1)
                for half, fg in enumerate((0, 1)):
                    b = i - 2
                    if g == fg and is_batch(b, B):
                        e.wait_ge(ht_hi, 2 * b + half + 1)
                        e.tensor_tensor(HTl[:, half, :], tk_bank[:, :], HTh[:, half, :].bitcast(F32),
                                        ALU.subtract).then_inc(ht_lo, 1)
                if g == 2 and is_batch(i - 2, B):
                    b = i - 2
                    e.wait_ge(down_done, b + 1)
                    if isinstance(b, int) and b == 0:
                        e.wait_ge(wscale_done, 3)
                    e.scalar_tensor_tensor(out=X[:, b, :], in0=v_bank[:, 0:D], scalar=ffn_scale[:, 0:1],
                                           in1=X[:, b, :], op0=ALU.mult, op1=ALU.add).then_inc(fres_done, 1)
                if g == 3 and is_batch(i, B) and is_batch(i + 1, B):
                    prep(i + 1)
                b, h = back(i, g, 1)
                if is_batch(b, B):
                    e.wait_ge(pt_done, GROUPS * b + h + 1)
                    wait_ge(e, o_done, GROUPS * b + h)
                    e.tensor_copy(PT[:, :], tq_bank[:, :]).then_inc(pt_saved, 1)

            loop1(slot)

            def split_lo(n):
                e.wait_ge(stage_hi, TERN + n + 1)
                hi, lo, src = layer1_chunk(n)
                e.tensor_tensor(lo, src, hi.bitcast(F32), ALU.subtract).then_inc(stage_lo, 1)

            def lnc_stats(b):
                wait_ge(e, c_rstd, b)
                e.bn_stats(stats[:, 0, :], X[:, b, :]).then_inc(c_stats, 1)
                e.wait_ge(c_stats, b + 1)
                e.bn_aggr(mv[:, 0, :], stats[:, 0, :]).then_inc(c_aggr, 1)

            def c_inputs(b):
                e.wait_ge(c_rstd, b + 1)
                wait_ge(e, c_turned, b)
                e.tensor_scalar(xn[:, 0, :], X[:, b, :], mv[:, 0, 0:1], rstd[:, 0:1], ALU.subtract, ALU.mult)\
                 .then_inc(c_xn, 1)
                e.wait_ge(c_chi, b + 1)
                e.tensor_tensor(cT[:, 1, :], ctxT[:, b, :], cT[:, 0, :].bitcast(F32), ALU.subtract)\
                 .then_inc(c_clo, 1)
                e.wait_ge(c_xhi, b + 1)
                e.tensor_tensor(xaT[:, 1, :], m1[:, 0:D], xaT[:, 0, :].bitcast(F32), ALU.subtract)\
                 .then_inc(c_xlo, 1)

            def rope(b):
                four = [P, 2 * H1, 4]
                x = qk.rearrange("p (h f c) -> p h f c", h=2 * H1, c=2)
                r = rot.rearrange("p (h f c) -> p h f c", h=2 * H1, c=2)
                s_ = sin8[:, b, :].rearrange("p (f c) -> p f c", c=2)
                e.wait_ge(qk_saved, b + 1)
                e.tensor_tensor(r[:, :, :, 0], x[:, :, :, 1],
                                s_[:, :, 0].unsqueeze(1).to_broadcast(four), ALU.mult).then_inc(rope_a, 1)
                e.tensor_tensor(r[:, :, :, 1], x[:, :, :, 0],
                                s_[:, :, 1].unsqueeze(1).to_broadcast(four), ALU.mult).then_inc(rope_a, 1)
                e.wait_ge(rope_a, 2 * b + 2)
                q3 = qk.rearrange("p (h d) -> p h d", d=D1)
                e.tensor_tensor(q3, q3, cos8[:, b, :].unsqueeze(1).to_broadcast([P, 2 * H1, D1]), ALU.mult)\
                 .then_inc(rope_b, 1)
                e.wait_ge(rope_b, b + 1)
                e.tensor_tensor(rot, rot, qk, ALU.add).then_inc(rope_done, 1)
                r3 = rot.rearrange("p (s h d) -> p s h d", s=2, d=D1)
                e.wait_ge(stack_hi, 2 * b + 2)
                e.tensor_tensor(SQ[:, :, 2, :], r3[:, 0], SQ[:, :, 0, :], ALU.subtract).then_inc(stack_lo, 1)
                e.tensor_tensor(SK[:, :, 1, :], r3[:, 1], SK[:, :, 0, :], ALU.subtract).then_inc(stack_lo, 1)

            def t1_save(b):
                e.wait_ge(t1_done, b + 1)
                wait_ge(e, smax_done, SG * b)
                wait_ge(e, k2_saved, b)
                e.tensor_copy(QT1.rearrange("p t q -> p (t q)"), m1[:, :].bitcast(F16)).then_inc(t1_saved, 1)
                e.tensor_copy(KT1.rearrange("p t q -> p (t q)"), m2[:, :].bitcast(F16)).then_inc(t1_saved, 1)

            def max_group(b, j):
                e.wait_ge(sc_done, SG * b + j + 1)
                if j == 0:
                    wait_ge(e, m_split, 4 * b)
                a = (j // HG) * HG * HG + j % HG
                e.tensor_reduce(Mx[:, a:a + HG * (HG - 1) + 1:HG], s_banks[j % 2][:, :]
                                .rearrange("p (h k) -> p h k", h=HG), AX.X, ALU.max).then_inc(smax_done, 1)

            def split_max(b):
                e.wait_ge(smax_done, SG * b + SG)
                e.tensor_scalar(SQ[:, :, 3, 0], Mx[:, :], 1.0 / 64, None, ALU.mult).then_inc(m_split, 1)
                e.wait_ge(m_split, 4 * b + 1)
                e.scalar_tensor_tensor(out=Mr[:, :], in0=Mx[:, :], scalar=1.0 / 64, in1=SQ[:, :, 3, 0],
                                       op0=ALU.mult, op1=ALU.subtract).then_inc(m_split, 1)
                e.wait_ge(m_split, 4 * b + 2)
                e.tensor_copy(SQ[:, :, 3, 1], Mr[:, :]).then_inc(m_split, 1)
                e.wait_ge(m_split, 4 * b + 3)
                e.tensor_tensor(SQ[:, :, 3, 2], Mr[:, :], SQ[:, :, 3, 1], ALU.subtract).then_inc(m_split, 1)

            def t2_save(b):
                e.wait_ge(t2_done, b + 1)
                wait_ge(e, st_done, SG * b)
                e.tensor_copy(QT2.rearrange("p t q -> p (t q)"), m2[:, :].bitcast(F16)).then_inc(t2_saved, 1)

            def attn_norm(b):
                e.wait_ge(av_done, SG * b + SG)
                ov = ov_bank[:, 0:9 * H1].rearrange("p (h c) -> p h c", h=H1)
                e.reciprocal(rz[:, :], ov[:, :, D1]).then_inc(rz_done, 1)
                e.wait_ge(rz_done, b + 1)
                wait_ge(e, ot2_done, b)
                e.tensor_tensor(On.rearrange("p (h c) -> p h c", h=H1), ov[:, :, 0:D1],
                                rz[:, :].unsqueeze(2).to_broadcast([P, H1, D1]), ALU.mult).then_inc(on_done, 1)

            def attn_out(b):
                e.wait_ge(ot2_hi, b + 1)
                e.tensor_tensor(OT2[1], m1[:, 0:D], OT2[0].bitcast(F32), ALU.subtract).then_inc(ot2_lo, 1)
                e.wait_ge(w2_done, b + 1)
                e.wait_ge(bias_added, b + 1)
                e.scalar_tensor_tensor(out=X[:, b, :], in0=m1[:, D:2 * D], scalar=tgates[:, 1:2],
                                       in1=X[:, b, :], op0=ALU.mult, op1=ALU.add).then_inc(cres_done, 1)
                e.wait_ge(cres_done, b + 1)
                wait_ge(e, d_rstd, b)
                e.bn_stats(stats[:, 1, :], X[:, b, :]).then_inc(d_stats, 1)
                e.wait_ge(d_stats, b + 1)
                e.bn_aggr(mv[:, 1, :], stats[:, 1, :]).then_inc(d_aggr, 1)

            def d_norm(b):
                e.wait_ge(d_rstd, b + 1)
                wait_ge(e, d_turned, b)
                e.tensor_scalar(xn[:, 1, :], X[:, b, :], mv[:, 1, 0:1], rstd[:, 1:2], ALU.subtract, ALU.mult)\
                 .then_inc(d_xn, 1)

            def d_inputs(b):
                e.wait_ge(d_xhi, b + 1)
                e.tensor_tensor(xfT[:, 1, :], m1[:, 0:D], xfT[:, 0, :].bitcast(F32), ALU.subtract)\
                 .then_inc(d_xlo, 1)

            def route(b):
                n = 12 * b
                def step(k, ins):
                    ins.then_inc(route_step, 1)
                    e.wait_ge(route_step, n + k)
                e.wait_ge(route_done, b + 1)
                step(1, e.tensor_copy(lg[:, :], m1[:, D:D + EX]))
                step(2, e.max(top[:, :], lg[:, :]))
                step(3, e.max_index(topi[:, :], top[:, :], lg[:, :]))
                step(4, e.tensor_copy(topf[:, :], topi[:, 0:2]))
                step(5, e.tensor_tensor(gap[:, :], top[:, 1:2], top[:, 0:1], ALU.subtract))
                e.wait_ge(gap_exp, b + 1)
                step(6, e.tensor_scalar(rw[:, 2:3], rw[:, 1:2], 1.0, None, ALU.add))
                step(7, e.reciprocal(rw[:, 3:4], rw[:, 2:3]))
                step(8, e.tensor_scalar(rw[:, 4:5], rw[:, 3:4], 0.5, None, ALU.mult))
                step(9, e.tensor_tensor(rw[:, 5:6], rw[:, 1:2], rw[:, 4:5], ALU.mult))
                step(10, e.tensor_scalar(w_one[:, :], iota8[:, :], topf[:, 0:1], rw[:, 4:5], ALU.is_equal, ALU.mult))
                step(11, e.tensor_scalar(w_two[:, :], iota8[:, :], topf[:, 1:2], rw[:, 5:6], ALU.is_equal, ALU.mult))
                wait_ge(e, hw_done, 4 * b)
                step(12, e.tensor_tensor(w_te[:, :], w_one[:, :], w_two[:, :], ALU.add))

            def hidden(b, c):
                cols = slice(c * 2 * CH, (c + 1) * 2 * CH)
                n = 4 * b + c
                e.wait_ge(g_tanh, n + 1)
                e.scalar_tensor_tensor(out=H2[:, cols], in0=H2[:, cols], scalar=1.0, in1=g_bank[:, 0:2 * CH],
                                       op0=ALU.add, op1=ALU.mult).then_inc(g_act, 1)
                e.wait_ge(g_act, n + 1)
                e.wait_ge(u2_done, n + 1)
                e.tensor_tensor(H2[:, cols], H2[:, cols], u_bank[:, 0:2 * CH], ALU.mult).then_inc(h2_done, 1)

            def ht_lo2(b, c):
                a, z = CHUNK_TILES[c]
                e.wait_ge(h2t_hi, 4 * b + c + 1)
                e.tensor_tensor(HT2[1][:, a * P:z * P], m3[:, 0:(z - a) * P], HT2[0][:, a * P:z * P].bitcast(F32),
                                ALU.subtract).then_inc(h2t_lo, 1)

            def d_out(b):
                e.wait_ge(dn_done, b + 1)
                e.scalar_tensor_tensor(out=X[:, b, :], in0=m3[:, 0:D], scalar=tgates[:, 3:4],
                                       in1=X[:, b, :], op0=ALU.mult, op1=ALU.add).then_inc(dres_done, 1)

            def angles():
                n = [0]
                def step(ins):
                    n[0] += 1
                    ins.then_inc(ang_step, 1)
                    e.wait_ge(ang_step, n[0])
                e.wait_ge(pos_in, 48)
                step(e.tensor_tensor(btg[:, :], btg[:, :], tgates[:, 1:2].to_broadcast([P, D]), ALU.mult))
                for f in range(2):
                    step(e.tensor_scalar(ang[:, 0, :, :, f], pos[:, :, :], 10000.0 ** (-f / 2.0), None, ALU.mult))
                step(e.tensor_scalar(ang[:, 1], ang[:, 0], math.pi / 2, None, ALU.add))
                step(e.tensor_scalar(turns[:, :], ang_flat, 1 / (2 * math.pi), 1.5 * 2 ** 23, ALU.mult, ALU.add))
                step(e.tensor_scalar(turns[:, :], turns[:, :], 1.5 * 2 ** 23, None, ALU.subtract))
                step(e.scalar_tensor_tensor(out=ang_flat, in0=turns[:, :], scalar=-6.28125, in1=ang_flat,
                                            op0=ALU.mult, op1=ALU.add))
                step(e.scalar_tensor_tensor(out=ang_flat, in0=turns[:, :], scalar=-(2 * math.pi - 6.28125),
                                            in1=ang_flat, op0=ALU.mult, op1=ALU.add))
                e.tensor_scalar(ang_flat, ang_flat, 3.1415925, -3.1415925, ALU.min, ALU.max).then_inc(ang_done, 1)
                e.wait_ge(trig_done, 1)
                four = [P, B, 4]
                s3, c3 = (trig[:, k].rearrange("p b s f -> p b (s f)") for k in (0, 1))
                s8, c8 = (t.rearrange("p b (f c) -> p b f c", c=2) for t in (sin8[:, :, :], cos8[:, :, :]))
                step(e.tensor_copy(c8[:, :, :, 0], c3))
                step(e.tensor_copy(c8[:, :, :, 1], c3))
                step(e.tensor_copy(s8[:, :, :, 1], s3))
                step(e.tensor_scalar(s8[:, :, :, 0], s3, -1.0, None, ALU.mult))

            angles()
            e.wait_ge(fres_done, B)
            for n in range(L1_CHUNKS):
                split_lo(n)
            lnc_stats(0)
            c_inputs(0)
            rope(0)
            t1_save(0)

            def slot2(i, g):
                if g == 0:
                    if is_batch(i - 1, B):
                        attn_norm(i - 1)
                    if is_batch(i, B):
                        for j in range(0, HG):
                            max_group(i, j)
                    if is_batch(i - 1, B):
                        attn_out(i - 1)
                    if is_batch(i - 2, B):
                        hidden(i - 2, 3)
                    if is_batch(i, B):
                        for j in range(HG, SG):
                            max_group(i, j)
                        split_max(i)
                    if is_batch(i - 2, B):
                        ht_lo2(i - 2, 2)
                    if is_batch(i - 1, B):
                        d_norm(i - 1)
                if g == 1:
                    if is_batch(i, B):
                        t2_save(i)
                    if is_batch(i - 1, B):
                        d_inputs(i - 1)
                    if is_batch(i - 2, B):
                        ht_lo2(i - 2, 3)
                    if is_batch(i - 1, B):
                        route(i - 1)
                        hidden(i - 1, 0)
                    if is_batch(i, B) and is_batch(i + 1, B):
                        lnc_stats(i + 1)
                if g == 2:
                    if is_batch(i - 2, B):
                        d_out(i - 2)
                    if is_batch(i - 1, B):
                        hidden(i - 1, 1)
                        ht_lo2(i - 1, 0)
                    if is_batch(i, B) and is_batch(i + 1, B):
                        c_inputs(i + 1)
                if g == 3:
                    if is_batch(i, B) and is_batch(i + 1, B):
                        rope(i + 1)
                    if is_batch(i - 1, B):
                        hidden(i - 1, 2)
                        ht_lo2(i - 1, 1)
                    if is_batch(i, B) and is_batch(i + 1, B):
                        t1_save(i + 1)

            loop2(slot2)

        @block.tensor
        def _(e):
            def three(out, lh, ll, rh, rl, start, stop):
                e.matmul(out, lh, rh, start=start, stop=False)
                e.matmul(out, lh, rl, start=False, stop=False)
                return e.matmul(out, ll, rh, start=False, stop=stop)

            def turn(out_bank, src, n, done):
                for k in range(n):
                    ins = e.transpose(out_bank[:, k * P:(k + 1) * P], src(k), ident[:, :])
                ins.then_inc(done, 1)

            def prep(b):
                e.wait_ge(xn_done, b + 1)
                wait_ge(e, v_saved, GROUPS * b)
                turn(v_bank, lambda k: xn[:, 0, k * P:(k + 1) * P], KT, xt_done)

            e.wait_ge(consts, 4)
            prep(0)

            def slot(i, g):
                t = GROUPS * i + g
                if is_batch(i, B):
                    if g == 0:
                        e.wait_ge(xt_lo, i + 1)
                        e.wait_ge(c_lo, i + 1)
                    if isinstance(i, int) and i == 0:
                        e.wait_ge(stage_lo, g + 1)
                    wait_ge(e, q_scaled, t)
                    if g == 0:
                        wait_ge(e, hid_done, 2 * (i - 2) + 1)
                    if g == 1:
                        wait_ge(e, hid_done, 2 * (i - 2) + 2)
                    for kt in range(KT):
                        ins = three(q_bank[:, :], xaT[:, 0, kt * P:(kt + 1) * P], xaT[:, 1, kt * P:(kt + 1) * P],
                                    W1h[:, g, kt, :], W1l[:, g, kt, :], kt == 0, kt == KT - 1)
                    ins.then_inc(q_proj, 1)
                    wait_ge(e, k_scaled, t)
                    three(k_bank[:, :], cT[:, 0, :], cT[:, 1, :], W1h[:, g, 2, :], W1l[:, g, 2, :], True, True)\
                        .then_inc(k_proj, 1)
                    wait_ge(e, v_saved, t)
                    if g == 3:
                        wait_ge(e, fres_done, i - 1)
                    if isinstance(i, int) and i == 1 and g > 0:
                        e.wait_ge(low_done, 4 * (g - 1) + 1)
                    three(v_bank[:, :], cT[:, 0, :], cT[:, 1, :], W1h[:, g, 3, :], W1l[:, g, 3, :], True, True)\
                        .then_inc(v_proj, 1)
                b, h = back(i, g, 1)
                if is_batch(b, B):
                    u = GROUPS * b + h
                    e.wait_ge(qt_saved, u + 1)
                    e.wait_ge(kt_saved, u + 1)
                    wait_ge(e, sub_done, u)
                    for k in range(HG):
                        cols = slice(k * P, (k + 1) * P)
                        ins = e.matmul(s_bank[:, cols], QT[:, h % 2, cols], KTr[:, h % 2, cols],
                                       start=True, stop=True)
                    ins.then_inc(s_done, 1)
                b, h = back(i, g, 2)
                if is_batch(b, B):
                    u = GROUPS * b + h
                    e.wait_ge(pt_saved, u + 1)
                    wait_ge(e, o_lo, u)
                    for k in range(HG):
                        cols = slice(k * P, (k + 1) * P)
                        ins = e.matmul(o_bank[:, cols], V[:, h, cols], PT[:, cols], start=True, stop=True)
                    ins.then_inc(o_done, 1)

                if i == 1 and g < 3:
                    e.wait_ge(wsum_done, g + 1)
                    e.wait_ge(v_saved, t + 1)
                    e.matmul(v_bank[:, D + g:D + g + 1], ones[:, :], wsum[:, g:g + 1], start=True, stop=True)\
                     .then_inc(wtot_done, 1)
                if g == 2 and is_batch(i - 1, B):
                    b = i - 1
                    e.wait_ge(fxn_done, b + 1)
                    e.wait_ge(kt_saved, t if is_batch(i, B) else SLOTS)
                    turn(tk_bank, lambda k: xn[:, 1, k * P:(k + 1) * P], KT, ft_done)
                for half, (fg, lag) in enumerate(((3, 1), (0, 2))):
                    b = i - lag
                    if g == fg and is_batch(b, B):
                        if half == 0:
                            e.wait_ge(ft_lo, b + 1)
                        if isinstance(b, int) and b == 0:
                            e.wait_ge(sign_done, 2)
                        e.wait_ge(k_scaled, t + 1 if is_batch(i, B) else SLOTS)
                        e.wait_ge(q_scaled, t + 1 if is_batch(i, B) else SLOTS)
                        if half == 1:
                            e.wait_ge(hid_done, 2 * b + 1)
                        for bank_, m, done in ((k_bank, 0, up_done), (q_bank, 1, gate_done)):
                            for kt in range(KT):
                                w = T[:, m, kt * E0 + half * BANK:kt * E0 + (half + 1) * BANK]
                                for part in range(2):
                                    ins = e.matmul(bank_[:, :], xfT[:, part, kt * P:(kt + 1) * P], w,
                                                   start=(kt == 0 and part == 0), stop=(kt == KT - 1 and part == 1))
                            ins.then_inc(done, 1)
                for half, fg in enumerate((0, 1)):
                    b = i - 2
                    if g == fg and is_batch(b, B):
                        n = 2 * b + half
                        e.wait_ge(hid_done, n + 1)
                        wait_ge(e, ht_lo, n)
                        e.wait_ge(kt_saved, t if is_batch(i, B) else SLOTS)
                        turn(tk_bank, lambda k: H[:, half, k * P:(k + 1) * P], HG, ht_done)
                if g == 2 and is_batch(i - 2, B):
                    b = i - 2
                    e.wait_ge(ht_lo, 2 * b + 2)
                    if isinstance(b, int) and b == 0:
                        e.wait_ge(sign_done, 3)
                    e.wait_ge(v_saved, t + 1 if is_batch(i, B) else SLOTS)
                    for k in range(ET):
                        cols = slice((k % HG) * P, (k % HG + 1) * P)
                        for part, HT in enumerate((HTh, HTl)):
                            ins = e.matmul(v_bank[:, 0:D], HT[:, k // HG, cols], T[:, 2, k * D:(k + 1) * D],
                                           start=(k == 0 and part == 0), stop=(k == ET - 1 and part == 1))
                    ins.then_inc(down_done, 1)

                if is_batch(i, B):
                    e.wait_ge(q_scaled, t + 1)
                    wait_ge(e, pt_saved, t - 1)
                    turn(tq_bank, lambda k: Qs[:, k, :], HG, tq_done)
                    e.wait_ge(k_scaled, t + 1)
                    wait_ge(e, kt_saved, t)
                    if g < 2 and is_batch(i - 2, B):
                        e.wait_ge(ht_lo, 2 * (i - 2) + g + 1)
                    if g == 2 and is_batch(i - 1, B):
                        e.wait_ge(ft_lo, i)
                    turn(tk_bank, lambda k: Ks[:, k, :], HG, tk_done)
                b, h = back(i, g, 2)
                if is_batch(b, B):
                    u = GROUPS * b + h
                    e.wait_ge(o_lo, u + 1)
                    if h == 0:
                        wait_ge(e, res_done, b)
                    if isinstance(b, int) and b == 0:
                        e.wait_ge(stage_lo, WO + h // 2 + 1)
                    for k in range(HG):
                        cols = slice(k * P, (k + 1) * P)
                        ins = three(y_bank[:, 0:D], OTh[:, h % 2, cols], OTl[:, h % 2, cols],
                                    Woh[:, h * HG + k, :], Wol[:, h * HG + k, :],
                                    h == 0 and k == 0, h == GROUPS - 1 and k == HG - 1)
                    ins.then_inc(w_done, 1)
                if g == 3 and is_batch(i, B) and is_batch(i + 1, B):
                    prep(i + 1)
                b, h = back(i, g, 1)
                if is_batch(b, B):
                    u = GROUPS * b + h
                    e.wait_ge(norm_done, u + 1)
                    if is_batch(i, B):
                        e.wait_ge(qt_saved, t + 1)
                    wait_ge(e, pt_saved, u)
                    turn(tq_bank, lambda k: Pr[:, k, :], HG, pt_done)

            loop1(slot)

            def c_turn(b):
                e.wait_ge(c_xn, b + 1)
                if b is not None:
                    wait_ge(e, route_step, 12 * (b - 2) + 1)
                turn(m1, lambda k: xn[:, 0, k * P:(k + 1) * P], KT, c_turned)

            def c_project(b):
                e.wait_ge(c_xlo, b + 1)
                e.wait_ge(c_clo, b + 1)
                wait_ge(e, t2_saved, b)
                for kt in range(KT):
                    wh, wl = w2("q", kt, D)
                    three(m1[:, D:2 * D], xaT[:, 0, kt * P:(kt + 1) * P], xaT[:, 1, kt * P:(kt + 1) * P],
                          wh, wl, kt == 0, kt == KT - 1)
                wh, wl = w2("kv", 0, 2 * D)
                three(m2[:, :], cT[:, 0, :], cT[:, 1, :], wh, wl, True, True).then_inc(qkv_done, 1)

            def t1(b):
                e.wait_ge(stack_lo, 2 * b + 2)
                e.wait_ge(qk_saved, b + 1)
                e.wait_ge(vn_saved, b + 1)
                for stack, out in ((SQ, m1), (SK, m2)):
                    flat = stack.rearrange("p h s d -> p (h s d)")
                    for k in range(SG):
                        ins = e.transpose(out[:, :].bitcast(F16)[:, k * P:(k + 1) * P],
                                          flat[:, k * P:(k + 1) * P], ident16[:, :])
                ins.then_inc(t1_done, 1)

            def t2(b):
                e.wait_ge(m_split, 4 * b + 4)
                flat = SQ.rearrange("p h s d -> p (h s d)")
                for k in range(SG):
                    ins = e.transpose(m2[:, :].bitcast(F16)[:, k * P:(k + 1) * P],
                                      flat[:, k * P:(k + 1) * P], ident16[:, :])
                ins.then_inc(t2_done, 1)

            def score_group(b, j):
                if j == 0:
                    e.wait_ge(t1_saved, 2 * b + 2)
                    wait_ge(e, e_done, SG * b)
                elif j >= 2:
                    e.wait_ge(smax_done, SG * b + j - 1)
                rows = slice(32 * (j % HG), 32 * (j % HG) + 24)
                for k in range(HG):
                    tile = HG * (j // HG) + k
                    ins = e.matmul(s_banks[j % 2][:, k * P:(k + 1) * P], QT1[rows, tile, :], KT1[rows, tile, :],
                                   start=True, stop=True)
                ins.then_inc(sc_done, 1)

            def shifted_group(b, j):
                if j == 0:
                    e.wait_ge(t2_saved, b + 1)
                    e.wait_ge(k2_saved, b + 1)
                elif j >= 2:
                    e.wait_ge(e_done, SG * b + j - 1)
                rows = slice(32 * (j % HG), 32 * (j % HG) + 32)
                for k in range(HG):
                    tile = HG * (j // HG) + k
                    ins = e.matmul(s_banks[j % 2][:, k * P:(k + 1) * P], KT2[rows, tile, :], QT2[rows, tile, :],
                                   start=True, stop=True)
                ins.then_inc(st_done, 1)

            def av_group(b, j):
                e.wait_ge(e_done, SG * b + j + 1)
                if j == 0:
                    e.wait_ge(va_done, b + 1)
                    wait_ge(e, on_done, b)
                for k, h in enumerate(heads(j)):
                    ins = e.matmul(ov_bank[:, 9 * h:9 * h + 9], E2[:, j % 4, k * P:(k + 1) * P], Va[:, h, :],
                                   start=True, stop=True)
                ins.then_inc(av_done, 1)

            def attn_out(b):
                e.wait_ge(on_done, b + 1)
                turn(m1, lambda k: On[:, k * P:(k + 1) * P], KT, ot2_done)
                e.wait_ge(ot2_lo, b + 1)
                for kt in range(KT):
                    wh, wl = w2("out", kt, D)
                    ins = three(m1[:, D:2 * D], OT2[0][:, kt * P:(kt + 1) * P], OT2[1][:, kt * P:(kt + 1) * P],
                                wh, wl, kt == 0, kt == KT - 1)
                ins.then_inc(w2_done, 1)

            def d_turn(b):
                e.wait_ge(d_xn, b + 1)
                turn(m1, lambda k: xn[:, 1, k * P:(k + 1) * P], KT, d_turned)

            def logits(b):
                e.wait_ge(d_xlo, b + 1)
                for kt in range(KT):
                    wh, wl = w2("route", kt, EX)
                    ins = three(m1[:, D:D + EX], xfT[:, 0, kt * P:(kt + 1) * P], xfT[:, 1, kt * P:(kt + 1) * P],
                                wh, wl, kt == 0, kt == KT - 1)
                ins.then_inc(route_done, 1)

            def expert_chunk(b, c):
                wait_ge(e, h2_done, 4 * b + c)
                for m, (out, done) in enumerate(((g_bank, g2_done), (u_bank, u2_done))):
                    for kt in range(KT):
                        wh, wl = w2("exp", 4 * c + 2 * m + kt, 2 * CH)
                        ins = three(out[:, 0:2 * CH], xfT[:, 0, kt * P:(kt + 1) * P], xfT[:, 1, kt * P:(kt + 1) * P],
                                    wh, wl, kt == 0, kt == KT - 1)
                    ins.then_inc(done, 1)

            def hidden_turn(b, c):
                a, z = CHUNK_TILES[c]
                e.wait_ge(hw_done, 4 * b + c + 1)
                wait_ge(e, h2t_lo, 4 * b + c)
                if c == 0:
                    wait_ge(e, dres_done, b)
                turn(m3, lambda k: H2[:, (a + k) * P:(a + k + 1) * P], z - a, h2t_done)

            def down(b):
                e.wait_ge(h2t_lo, 4 * b + 4)
                for k in range(F2 // P):
                    cols = slice(k * P, (k + 1) * P)
                    ins = three(m3[:, 0:D], HT2[0][:, cols], HT2[1][:, cols], woh[:, k * D:(k + 1) * D],
                                wol[:, k * D:(k + 1) * D], k == 0, k == F2 // P - 1)
                ins.then_inc(dn_done, 1)

            e.wait_ge(fres_done, B)
            e.wait_ge(consts, 5 + EX + 4)
            e.wait_ge(stage_lo, TERN + L1_CHUNKS)
            c_turn(0)
            c_project(0)
            t1(0)

            def slot2(i, g):
                if g == 0:
                    if is_batch(i, B):
                        for j in range(0, HG):
                            score_group(i, j)
                    if is_batch(i - 2, B):
                        expert_chunk(i - 2, 3)
                    if is_batch(i - 1, B):
                        attn_out(i - 1)
                    if is_batch(i, B):
                        for j in range(HG, SG):
                            score_group(i, j)
                    if is_batch(i - 2, B):
                        hidden_turn(i - 2, 2)
                if g == 1:
                    if is_batch(i, B):
                        t2(i)
                    if is_batch(i - 1, B):
                        d_turn(i - 1)
                    if is_batch(i - 2, B):
                        hidden_turn(i - 2, 3)
                    if is_batch(i, B):
                        shifted_group(i, 0)
                        shifted_group(i, 1)
                    if is_batch(i - 1, B):
                        logits(i - 1)
                        expert_chunk(i - 1, 0)
                    if is_batch(i, B):
                        shifted_group(i, 2)
                        av_group(i, 0)
                        av_group(i, 1)
                    if is_batch(i - 2, B):
                        down(i - 2)
                if g == 2:
                    if is_batch(i, B):
                        shifted_group(i, 3)
                        av_group(i, 2)
                    if is_batch(i - 1, B):
                        expert_chunk(i - 1, 1)
                        hidden_turn(i - 1, 0)
                    if is_batch(i, B) and is_batch(i + 1, B):
                        c_turn(i + 1)
                    if is_batch(i, B):
                        shifted_group(i, 4)
                        av_group(i, 3)
                        shifted_group(i, 5)
                        av_group(i, 4)
                    if is_batch(i, B) and is_batch(i + 1, B):
                        c_project(i + 1)
                if g == 3:
                    if is_batch(i, B):
                        shifted_group(i, 6)
                        av_group(i, 5)
                    if is_batch(i - 1, B):
                        expert_chunk(i - 1, 2)
                        hidden_turn(i - 1, 1)
                    if is_batch(i, B):
                        shifted_group(i, 7)
                        av_group(i, 6)
                        av_group(i, 7)
                    if is_batch(i, B) and is_batch(i + 1, B):
                        t1(i + 1)

            loop2(slot2)


INS = {"x": "x", "ctxT": "ctx_1024", "g_xattn": "g_xattn", "g_ffn": "g_ffn", "Wq0": "L0_xattn_Wq",
       "Wk0": "L0_xattn_Wk", "Wv0": "L0_xattn_Wv", "Wo0": "L0_xattn_Wo", "gq": "L0_xattn_gq",
       "gk": "L0_xattn_gk", "WuT": "L0_ffn_W_up", "WgT": "L0_ffn_W_gate", "WdT": "L0_ffn_W_down",
       "pos": "fside_BxSx2_0", "Wq1": "L1_xattn_Wq", "Wkv1": "L1_xattn_Wkv", "Wout1": "L1_xattn_Wout",
       "bout": "L1_xattn_bout", "gwT": "L1_ffn_gate_w", "e_gate": "L1_ffn_w_gate", "e_up": "L1_ffn_w_up",
       "e_down": "L1_ffn_w_down"}
TURNED = {"ctxT": (2, 0, 1), "WuT": (1, 0), "WgT": (1, 0), "WdT": (1, 0), "gwT": (1, 0)}


def kernel(**inputs):
    import numpy as np
    import concourse.bacc as bacc
    from concourse.bass_utils import run_bass_kernel_spmd

    nc = bacc.Bacc("TRN2", target_bir_lowering=False, num_devices=1)
    arrays, io = {}, {}
    for name, source in INS.items():
        a = np.asarray(inputs[source])
        a = np.ascontiguousarray(a.transpose(TURNED[name]) if name in TURNED else a)
        arrays[f"in_{name}"] = a
        io[name] = nc.dram_tensor(f"in_{name}", a.shape, mybir.dt.from_np(a.dtype), kind="ExternalInput").ap()
    shape = np.asarray(inputs["x"]).shape
    io["out"] = nc.dram_tensor("out_x", shape, F32, kind="ExternalOutput").ap()
    build(nc, io)
    return run_bass_kernel_spmd(nc, [arrays], core_ids=[0]).results[0]["out_x"]
```

```python
import math
from contextlib import ExitStack

import concourse.bass as bass
from concourse import mybir

F32 = mybir.dt.float32
F32R = mybir.dt.float32r
F16 = mybir.dt.float16
U32 = mybir.dt.uint32
ALU = mybir.AluOpType
ACT = mybir.ActivationFunctionType
AX = mybir.AxisListType

P = 128
GROUPS = 4
HG = 4
BANK = 512


def is_batch(b, batches):
    return not isinstance(b, int) or 0 <= b < batches


def is_step(i, n):
    return isinstance(i, int) and i == n


def wait_ge(engine, semaphore, value):
    if not isinstance(value, int) or value > 0:
        engine.wait_ge(semaphore, value)


def back(b, g, n):
    return (b, g - n) if g >= n else (b - 1, g - n + GROUPS)


def build(nc, io):
    B, S, D = io["x"].shape
    C = io["ctxT"].shape[0]
    INNER = io["Wq0"].shape[1]
    KT = D // P
    E0 = io["WuT"].shape[1]
    ET = E0 // P
    assert S == P and C == P and INNER == GROUPS * BANK and E0 == 2 * BANK and KT == 2
    SLOTS = B * GROUPS
    EX, _, CH = io["e_gate"].shape
    F2 = EX * CH
    D1 = 8
    H1 = D // D1
    L1_CHUNKS = 1 + EX // 2 + 2
    assert F2 % P == 0

    with ExitStack() as ctx:
        def sb(name, shape, dt=F32):
            return ctx.enter_context(nc.sbuf_tensor(name, shape, dt))

        def sem(name):
            return ctx.enter_context(nc.semaphore(name))

        bank = [ctx.enter_context(nc.psum_tensor(f"bank{n}", [P, BANK], F32)) for n in range(8)]
        q_bank, k_bank, v_bank, tq_bank, tk_bank, s_bank, o_bank, y_bank = bank

        X = sb("X", [P, B, D])
        W1h = sb("W1h", [P, GROUPS, 4, BANK], F32R)
        W1l = sb("W1l", [P, GROUPS, 4, BANK], F32R)
        Woh = sb("Woh", [P, INNER // P, D], F32R)
        Wol = sb("Wol", [P, INNER // P, D], F32R)
        T = sb("T", [P, 3, 4 * BANK], F32R)
        stage = sb("stage", [P, 2, 4 * BANK])
        ctxT = sb("ctxT_sb", [P, B, P])

        ident = sb("ident", [P, P])
        ones = sb("ones", [P, P])
        neg_half = sb("neg_half", [P, 2 * HG])
        eps = sb("eps", [P, 1])
        p_eps = sb("p_eps", [P, 2 * HG])
        gains = sb("gains", [P, 2])
        gqk = sb("gqk", [P, 1])
        gates = sb("gates", [P, 4])
        tgates = sb("tgates", [P, 4])
        wsum = sb("wsum", [P, 3])
        wscale = sb("wscale", [P, 3])
        half_up = sb("half_up", [P, 1])
        th = sb("th", [P, 3])
        nth = sb("nth", [P, 3])
        ffn_scale = sb("ffn_scale", [P, 2])

        stats = sb("stats", [P, 2, 6])
        mv = sb("mv", [P, 2, 2])
        var = sb("var", [P, 2])
        rstd = sb("rstd", [P, 2])
        xn = sb("xn", [P, 2, D])
        xaT = sb("xaT", [P, 2, D], F32R)
        cT = sb("cT", [P, 2, P], F32R)
        ss = sb("ss", [P, 2 * HG])
        rs = sb("rs", [P, 2 * HG])
        Qs = sb("Qs", [P, HG, P])
        Ks = sb("Ks", [P, HG, P])
        QT = sb("QT", [P, 2, BANK])
        KTr = sb("KTr", [P, 2, BANK])
        V = sb("V", [P, GROUPS, BANK])
        mx = sb("mx", [P, HG])
        Pr = sb("Pr", [P, HG, P])
        rsum = sb("rsum", [P, HG])
        rinv = sb("rinv", [P, HG])
        PT = sb("PT", [P, BANK])
        OTh = sb("OTh", [P, 2, BANK], F32R)
        OTl = sb("OTl", [P, 2, BANK], F32R)
        xfT = sb("xfT", [P, 2, D], F32R)
        H = sb("H", [P, 2, BANK])
        HTh = sb("HTh", [P, 2, BANK], F32R)
        HTl = sb("HTl", [P, 2, BANK], F32R)

        ident16 = sb("ident16", [P, P], F16)
        btg = sb("btg", [P, D])
        pos = sb("pos_sb", [P, B, 2])
        ang = sb("ang", [P, 2, B, 2, 2])
        turns = sb("turns", [P, 8 * B])
        trig = sb("trig", [P, 2, B, 2, 2])
        cos8 = sb("cos8", [P, B, D1])
        sin8 = sb("sin8", [P, B, D1])
        Mx = sb("Mx", [P, H1])
        Mr = sb("Mr", [P, H1])
        rz = sb("rz", [P, H1])
        iota8 = sb("iota8", [P, EX])
        lg, top, w_one, w_two, w_te = (sb(n, [P, EX]) for n in ("lg", "top", "w_one", "w_two", "w_te"))
        topi = sb("topi", [P, EX], U32)
        topf = sb("topf", [P, 2])
        gap = sb("gap", [P, 1])
        rw = sb("rw", [P, 6])
        ang_flat = ang[:, :, :, :, :].rearrange("p k b s f -> p (k b s f)")

        x_in = [sem(f"x_in{n}") for n in range(2)]
        ctx_in, small_in = sem("ctx_in"), sem("small_in")
        stage_in = [sem("stage_in0"), sem("stage_in1")]
        stage_hi, stage_lo = sem("stage_hi"), sem("stage_lo")
        consts, gains_done, gates_done = sem("consts"), sem("gains_done"), sem("gates_done")
        wsum_done, wtot_done, wscale_done = sem("wsum_done"), sem("wtot_done"), sem("wscale_done")
        low_done, sign_done = sem("low_done"), sem("sign_done")
        stats_done, aggr_done, eps_done, rstd_done, xn_done = (sem(n) for n in (
            "stats_done", "aggr_done", "eps_done", "rstd_done", "xn_done"))
        fstats_done, faggr_done, feps_done, frstd_done, fxn_done = (sem(n) for n in (
            "fstats_done", "faggr_done", "feps_done", "frstd_done", "fxn_done"))
        xt_done, xt_hi, xt_lo, c_hi, c_lo = (sem(n) for n in ("xt_done", "xt_hi", "xt_lo", "c_hi", "c_lo"))
        q_proj, k_proj, v_proj, sq_done, ss_done, ms_done, rs_done = (sem(n) for n in (
            "q_proj", "k_proj", "v_proj", "sq_done", "ss_done", "ms_done", "rs_done"))
        q_scaled, k_scaled, v_saved, tq_done, tk_done, qt_saved, kt_saved = (sem(n) for n in (
            "q_scaled", "k_scaled", "v_saved", "tq_done", "tk_done", "qt_saved", "kt_saved"))
        s_done, mx_done, sub_done, exp_done, sum_done, rinv_done, norm_done = (sem(n) for n in (
            "s_done", "mx_done", "sub_done", "exp_done", "sum_done", "rinv_done", "norm_done"))
        pt_done, pt_saved, o_done, o_hi, o_lo, w_done, res_done = (sem(n) for n in (
            "pt_done", "pt_saved", "o_done", "o_hi", "o_lo", "w_done", "res_done"))
        ft_done, ft_hi, ft_lo, up_done, gate_done, tanh_done, act_done, hid_done = (sem(n) for n in (
            "ft_done", "ft_hi", "ft_lo", "up_done", "gate_done", "tanh_done", "act_done", "hid_done"))
        ht_done, ht_hi, ht_lo, down_done, fres_done = (sem(n) for n in (
            "ht_done", "ht_hi", "ht_lo", "down_done", "fres_done"))
        pos_in, ang_step, ang_done, trig_done, c_stats, c_aggr = (sem(n) for n in (
            "pos_in", "ang_step", "ang_done", "trig_done", "c_stats", "c_aggr"))
        c_eps, c_rstd, c_xn, c_turned, c_chi, c_clo = (sem(n) for n in (
            "c_eps", "c_rstd", "c_xn", "c_turned", "c_chi", "c_clo"))
        c_xhi, c_xlo, qkv_done, qk_saved, vn_saved, va_done = (sem(n) for n in (
            "c_xhi", "c_xlo", "qkv_done", "qk_saved", "vn_saved", "va_done"))
        rope_a, rope_b, rope_done, stack_hi, stack_lo, t1_done = (sem(n) for n in (
            "rope_a", "rope_b", "rope_done", "stack_hi", "stack_lo", "t1_done"))
        t1q_saved, sc_done, smax_done, m_split, t2_done, t2_saved = (sem(n) for n in (
            "t1q_saved", "sc_done", "smax_done", "m_split", "t2_done", "t2_saved"))
        t1k_saved, st_done, e_done, av_done, rz_done, on_done = (sem(n) for n in (
            "t1k_saved", "st_done", "e_done", "av_done", "rz_done", "on_done"))
        ot2_done, ot2_hi, ot2_lo, w2_done, bias_added, cres_done = (sem(n) for n in (
            "ot2_done", "ot2_hi", "ot2_lo", "w2_done", "bias_added", "cres_done"))
        d_stats, d_aggr, d_eps, d_rstd, d_xn, d_turned = (sem(n) for n in (
            "d_stats", "d_aggr", "d_eps", "d_rstd", "d_xn", "d_turned"))
        d_xhi, d_xlo, route_done, route_step, gap_exp, g2_done = (sem(n) for n in (
            "d_xhi", "d_xlo", "route_done", "route_step", "gap_exp", "g2_done"))
        u2_done, g_tanh, g_act, h2_done, wte_step, h2t_done = (sem(n) for n in (
            "u2_done", "g_tanh", "g_act", "h2_done", "wte_step", "h2t_done"))
        h2t_hi, h2t_lo, dn_done, dres_done = (sem(n) for n in (
            "h2t_hi", "h2t_lo", "dn_done", "dres_done"))
        out_done = sem("out_done")
        waits_passed = sem("waits_passed")

        w1h, w1l = (w[:, :, :, :].rearrange("p g m n -> p (g m n)") for w in (W1h, W1l))
        woh, wol = (w[:, :, :].rearrange("p t n -> p (t n)") for w in (Woh, Wol))
        at = 0
        place = {}
        for name, size in (("q", KT * D), ("kv", 2 * D), ("out", KT * D), ("route", KT * EX),
                           ("exp", EX // 2 * 4 * CH)):
            place[name] = at
            at += size
        assert at <= GROUPS * 4 * BANK

        def w2(name, n, size):
            a = place[name] + n * size
            return w1h[:, a:a + size], w1l[:, a:a + size]

        t_flat = T[:, :, :].rearrange("p m n -> p (m n)")
        HT2 = [t_flat[:, n * F2:(n + 1) * F2] for n in range(2)]
        OT2 = [t_flat[:, 2 * F2 + n * D:2 * F2 + (n + 1) * D] for n in range(2)]
        E2 = V
        QT1 = QT[:, 0, :].bitcast(F16).rearrange("p (t q) -> p t q", q=P)
        QT2 = QT[:, 1, :].bitcast(F16).rearrange("p (t q) -> p t q", q=P)
        KT1 = KTr[:, 0, :].bitcast(F16).rearrange("p (t q) -> p t q", q=P)
        qk = Qs[:, :, :].rearrange("p h d -> p (h d)")
        rot = Ks[:, :, :].rearrange("p h d -> p (h d)")
        SQ = PT[:, :].bitcast(F16).rearrange("p (h s d) -> p h s d", h=H1, s=4)
        SK = Pr[:, :, :].rearrange("p h d -> p (h d)").bitcast(F16).rearrange("p (h s d) -> p h s d", h=H1, s=4)
        h_flat = H[:, :, :].rearrange("p a n -> p (a n)")
        Vn = h_flat[:, 0:D]
        Va = h_flat[:, D:D + 9 * H1].rearrange("p (h c) -> p h c", h=H1)
        On = h_flat[:, D + 9 * H1:2 * D + 9 * H1]
        H2 = stage[:, 0, 0:F2]
        sa_bank, sb_bank, ov_bank, g_bank, u_bank, m1, m2, m3 = bank
        s_banks = (sa_bank, sb_bank)
        SG = 2 * HG

        def heads(j):
            return [HG * (HG * (j // HG) + k) + j % HG for k in range(HG)]

        CHUNK_TILES = ((0, 2), (2, 5), (5, 8), (8, 11))

        def layer1_chunk(n):
            src = stage[:, (CHUNKS + n) % 2, :]
            if n <= EX // 2:
                a = 0 if n == 0 else place["exp"] + (n - 1) * 4 * 2 * CH
                size = place["exp"] if n == 0 else 4 * 2 * CH
                return w1h[:, a:a + size], w1l[:, a:a + size], src[:, 0:size]
            a, z = ((0, 6), (6, F2 // P))[n - 1 - EX // 2]
            return woh[:, a * D:z * D], wol[:, a * D:z * D], src[:, 0:(z - a) * D]

        block = ctx.enter_context(nc.Block())

        WO, TERN = GROUPS, GROUPS + 2
        CHUNKS = TERN + 3
        SPLITS = ((1, 2), (3,), (4,), (5,))

        def chunk_ready(e, c):
            e.wait_ge(stage_in[c % 2], 64 * (c // 2 + 1))

        def last(b, g):
            t = GROUPS * b + g
            return min(t, SLOTS - 1) if isinstance(t, int) else t

        def batches(e, step):
            for i in range(3):
                step(i, True, i > 0, i > 1, True)
            with e.Fori(3, B - 1) as i:
                step(i, True, True, True, True)
            for i in range(B - 1, B + 2):
                step(i, i < B, i <= B, True, False)

        def steps(e, step):
            for i in (0, 1):
                step(i, True, i > 0, True)
            with e.Fori(2, B - 1) as i:
                step(i, True, True, True)
            for i in (B - 1, B):
                step(i, i < B, True, False)

        @block.sync
        def _(e):
            xd = io["x"].rearrange("b p d -> p b d")
            e.dma_start(X[:, 0:1, :], xd[:, 0:1, :]).then_inc(x_in[0], 16)
            e.dma_start(ctxT[:, :, :], io["ctxT"]).then_inc(ctx_in, 16)

            def load1(n, s, done):
                if n == 0:
                    for name, w in (("q", "Wq1"), ("kv", "Wkv1"), ("out", "Wout1"), ("route", "gwT")):
                        src = io[w].rearrange("(t p) n -> p t n", p=P)
                        size = src.shape[1] * src.shape[2]
                        e.dma_start(s[:, place[name]:place[name] + size].rearrange("p (t n) -> p t n", n=src.shape[2]),
                                    src).then_inc(done, 16)
                elif n <= EX // 2:
                    for m, w in enumerate(("e_gate", "e_up")):
                        for kt in range(KT):
                            a = (2 * m + kt) * 2 * CH
                            src = io[w][2 * n - 2:2 * n, kt * P:(kt + 1) * P, :].rearrange("e p f -> p e f")
                            e.dma_start(s[:, a:a + 2 * CH].rearrange("p (e f) -> p e f", f=CH), src).then_inc(done, 16)
                else:
                    a, z = ((0, 6), (6, F2 // P))[n - 1 - EX // 2]
                    src = io["e_down"].rearrange("e f d -> (e f) d").rearrange("(t p) d -> p t d", p=P)
                    e.dma_start(s[:, 0:(z - a) * D].rearrange("p (t d) -> p t d", d=D), src[:, a:z, :])\
                     .then_inc(done, 64)

            def load(c):
                s = stage[:, c % 2, :]
                if c >= 2:
                    if c - 2 < TERN:
                        e.wait_ge(stage_lo, c - 1)
                    elif c - 2 < CHUNKS:
                        e.wait_ge(sign_done, c - 2 - TERN + 1)
                    else:
                        e.wait_ge(stage_lo, TERN + c - 2 - CHUNKS + 1)
                if c < WO:
                    cols = slice(c * BANK, (c + 1) * BANK)
                    for kt in range(KT):
                        e.dma_start(s[:, kt * BANK:(kt + 1) * BANK],
                                    io["Wq0"][kt * P:(kt + 1) * P, cols]).then_inc(stage_in[c % 2], 16)
                    e.dma_start(s[:, 2 * BANK:3 * BANK], io["Wk0"][:, cols]).then_inc(stage_in[c % 2], 16)
                    e.dma_start(s[:, 3 * BANK:4 * BANK], io["Wv0"][:, cols]).then_inc(stage_in[c % 2], 16)
                elif c < TERN:
                    n = INNER // P // 2
                    src = io["Wo0"].rearrange("(t p) n -> p t n", p=P)[:, (c - WO) * n:(c - WO + 1) * n, :]
                    e.dma_start(s.rearrange("p (t n) -> p t n", n=D), src).then_inc(stage_in[c % 2], 64)
                elif c >= CHUNKS:
                    load1(c - CHUNKS, s, stage_in[c % 2])
                else:
                    src = io[("WuT", "WgT", "WdT")[c - TERN]].rearrange("(t p) n -> p t n", p=P)
                    e.dma_start(s.rearrange("p (t n) -> p t n", n=src.shape[2]), src)\
                     .then_inc(stage_in[c % 2], 64)

            load(0)
            e.dma_start(gains[:, 0:1], io["gq"].rearrange("(p a) -> p a", a=1)).then_inc(small_in, 16)
            e.dma_start(gains[:, 1:2], io["gk"].rearrange("(p a) -> p a", a=1)).then_inc(small_in, 16)
            e.dma_start(gates[:, 0:2], io["g_xattn"].rearrange("(a n) -> a n", a=1).to_broadcast([P, 2]))\
             .then_inc(small_in, 16)
            e.dma_start(gates[:, 2:4], io["g_ffn"].rearrange("(a n) -> a n", a=1).to_broadcast([P, 2]))\
             .then_inc(small_in, 16)
            e.dma_start(pos[:, :, :], io["pos"].rearrange("b p a -> p b a")).then_inc(pos_in, 16)
            e.dma_start(btg[:, :], io["bout"].rearrange("(a n) -> a n", a=1).to_broadcast([P, D])).then_inc(pos_in, 32)
            load(1)
            e.dma_start(X[:, 1:B, :], xd[:, 1:B, :]).then_inc(x_in[1], 16)
            for c in range(2, CHUNKS):
                load(c)
            for c in range(CHUNKS, CHUNKS + L1_CHUNKS):
                load(c)

            def store(i, cur, prv, nxt):
                if prv:
                    e.wait_ge(dres_done, i)
                    e.dma_start(io["out"][i - 1], X[:, i - 1, :]).then_inc(out_done, 16)

            steps(e, store)
            e.wait_ge(out_done, 16 * B)

        @block.gpsimd
        def _(e):
            e.memset(ident[:, :], 0.0).then_inc(consts, 1)
            e.memset(ones[:, :], 1.0).then_inc(consts, 1)
            e.memset(neg_half[:, :], -0.5).then_inc(consts, 1)
            e.memset(eps[:, :], 1e-5).then_inc(consts, 1)
            e.memset(p_eps[:, :], 1e-5 * P).then_inc(consts, 1)
            e.wait_ge(consts, 5)
            e.affine_select(out=ident[:, :], in_=ident[:, :], compare_op=ALU.not_equal, fill=1.0,
                            base=0, pattern=[[-1, P]], channel_multiplier=1).then_inc(consts, 1)
            e.wait_ge(consts, 6)
            e.tensor_copy(ident16[:, :], ident[:, :]).then_inc(consts, 1)

            def ln_rstd(b, n, aggr, added, done, used):
                e.wait_ge(aggr, b + 1)
                wait_ge(e, used, b)
                e.tensor_tensor(var[:, n:n + 1], mv[:, n, 1:2], eps[:, :], ALU.add).then_inc(added, 1)
                e.wait_ge(added, b + 1)
                e.tensor_tensor(rstd[:, n:n + 1], var[:, n:n + 1], neg_half[:, 0:1], ALU.pow).then_inc(done, 1)

            ln_rstd(0, 0, aggr_done, eps_done, rstd_done, xn_done)

            def ln_a(b):
                ln_rstd(b, 0, aggr_done, eps_done, rstd_done, xn_done)

            def ln_f(b):
                ln_rstd(b, 1, faggr_done, feps_done, frstd_done, fxn_done)

            def rms(b, g):
                t = GROUPS * b + g
                e.wait_ge(ss_done, 2 * t + 2)
                wait_ge(e, q_scaled, t)
                wait_ge(e, k_scaled, t)
                e.tensor_tensor(rs[:, :], ss[:, :], p_eps[:, :], ALU.add).then_inc(ms_done, 1)
                e.wait_ge(ms_done, t + 1)
                e.tensor_tensor(rs[:, :], rs[:, :], neg_half[:, :], ALU.pow).then_inc(rs_done, 1)

            def normalise(b, g):
                e.wait_ge(rinv_done, GROUPS * b + g + 1)
                e.tensor_tensor(Pr[:, :, :], Pr[:, :, :], rinv[:, :].unsqueeze(2).to_broadcast([P, HG, P]),
                                ALU.mult).then_inc(norm_done, 1)

            def ln_c(b):
                ln_rstd(b, 0, c_aggr, c_eps, c_rstd, c_xn)

            def ln_d(b):
                ln_rstd(b, 1, d_aggr, d_eps, d_rstd, d_xn)

            def add_bias(b):
                e.wait_ge(c_xn, b + 1)
                e.tensor_tensor(X[:, b, :], X[:, b, :], btg[:, :], ALU.add).then_inc(bias_added, 1)

            def weights(b):
                n = 5 * b
                e.wait_ge(route_step, 7 * b + 7)
                e.tensor_tensor(rw[:, 5:6], rw[:, 1:2], rw[:, 3:4], ALU.mult).then_inc(wte_step, 1)
                e.tensor_scalar(w_one[:, :], iota8[:, :], topf[:, 0:1], rw[:, 3:4], ALU.is_equal, ALU.mult)\
                 .then_inc(wte_step, 1)
                e.tensor_scalar(w_two[:, :], iota8[:, :], topf[:, 1:2], None, ALU.is_equal).then_inc(wte_step, 1)
                e.wait_ge(wte_step, n + 3)
                e.tensor_tensor(w_two[:, :], w_two[:, :], rw[:, 5:6].to_broadcast([P, EX]), ALU.mult)\
                 .then_inc(wte_step, 1)
                e.wait_ge(wte_step, n + 4)
                wait_ge(e, h2_done, 4 * b)
                e.tensor_tensor(w_te[:, :], w_one[:, :], w_two[:, :], ALU.add).then_inc(wte_step, 1)

            def ready_layer1(b):
                if is_step(b, B):
                    for k in range(EX):
                        e.memset(iota8[:, k:k + 1], float(k)).then_inc(consts, 1)
                    e.wait_ge(o_done, SLOTS)
                    e.memset(SQ[:, :, 3, :], 0.0).then_inc(consts, 1)
                    e.memset(SK[:, :, 3, 3:D1], 0.0).then_inc(consts, 1)
                    e.memset(SK[:, :, 3, 0:3], -64.0).then_inc(consts, 1)
                    e.wait_ge(ht_done, 2 * B)
                    e.memset(Va[:, :, D1:D1 + 1], 1.0).then_inc(consts, 1)

            def step1(i, cur, prv, old, nxt):
                if cur:
                    rms(i, 0)
                if prv:
                    normalise(i - 1, 3)
                if cur:
                    rms(i, 1)
                    normalise(i, 0)
                if prv:
                    ln_f(i - 1)
                if cur:
                    rms(i, 2)
                    normalise(i, 1)
                if nxt:
                    ln_a(i + 1)
                if cur:
                    rms(i, 3)
                    normalise(i, 2)
                ready_layer1(i)
                if is_step(i, B + 1):
                    ln_c(0)
                    add_bias(0)

            batches(e, step1)

            def step(i, cur, prv, nxt):
                if nxt:
                    ln_c(i + 1)
                    add_bias(i + 1)
                if cur:
                    ln_d(i)
                    weights(i)

            steps(e, step)

        @block.scalar
        def _(e):
            def split_chunk_hi(c):
                chunk_ready(e, c)
                dst = W1h[:, c, :, :] if c < WO else \
                    Woh[:, (c - WO) * 8:(c - WO + 1) * 8, :]
                e.activation(dst, stage[:, c % 2, :].rearrange("p (t n) -> p t n", n=dst.shape[2]), ACT.Copy)\
                 .then_inc(stage_hi, 1)

            def prep(b):
                wait_ge(e, v_proj, GROUPS * b)
                e.activation(cT[:, 0, :], ctxT[:, b, :], ACT.Copy).then_inc(c_hi, 1)
                e.wait_ge(xt_done, b + 1)
                e.activation(xaT[:, 0, :], tk_bank[:, 0:D], ACT.Copy).then_inc(xt_hi, 1)

            e.wait_ge(small_in, 64)
            e.activation(tgates[:, :], gates[:, :], ACT.Tanh).then_inc(gates_done, 1)
            e.wait_ge(ang_done, 1)
            e.activation(trig[:, :, :, :, :], ang[:, :, :, :, :], ACT.Sin).then_inc(trig_done, 1)
            e.wait_ge(ctx_in, 16)
            split_chunk_hi(0)
            prep(0)

            def square_q(b, g):
                t = GROUPS * b + g
                e.wait_ge(q_proj, t + 1)
                wait_ge(e, tq_done, t)
                e.activation(Qs[:, :, :], q_bank[:, :].rearrange("p (h d) -> p h d", h=HG), ACT.Square)\
                 .then_inc(sq_done, 1)

            def square_k(b, g):
                t = GROUPS * b + g
                e.wait_ge(k_proj, t + 1)
                wait_ge(e, tk_done, t)
                e.activation(Ks[:, :, :], k_bank[:, :].rearrange("p (h d) -> p h d", h=HG), ACT.Square)\
                 .then_inc(sq_done, 1)

            def save_v(b, g):
                t = GROUPS * b + g
                e.wait_ge(v_proj, t + 1)
                wait_ge(e, o_done, t - 3)
                e.activation(V[:, g, :], v_bank[:, :], ACT.Copy).then_inc(v_saved, 1)

            def split_hi0(b, g):
                if is_step(b, 0):
                    for c in SPLITS[g]:
                        split_chunk_hi(c)

            def out_hi(b, g):
                u = GROUPS * b + g
                e.wait_ge(o_done, u + 1)
                wait_ge(e, w_done, u - 1)
                e.activation(OTh[:, g % 2, :], o_bank[:, :], ACT.Copy).then_inc(o_hi, 1)

            def exponentials(b, g):
                e.wait_ge(sub_done, GROUPS * b + g + 1)
                e.activation(Pr[:, :, :], Pr[:, :, :], ACT.Exp, scale=float(P) ** 0.5).then_inc(exp_done, 1)

            def tanh_up(b, half):
                if half == 0 and is_step(b, 0):
                    e.wait_ge(wscale_done, 1)
                e.wait_ge(up_done, 2 * b + half + 1)
                wait_ge(e, ht_done, 2 * b + half - 1)
                e.activation(H[:, half, :], v_bank[:, :], ACT.Tanh, scale=half_up[:, 0:1]).then_inc(tanh_done, 1)

            def save_qt(b, g):
                t = GROUPS * b + g
                e.wait_ge(tq_done, t + 1)
                wait_ge(e, s_done, t - 1)
                e.activation(QT[:, g % 2, :], tq_bank[:, :], ACT.Copy).then_inc(qt_saved, 1)

            def save_kt(b, g):
                t = GROUPS * b + g
                e.wait_ge(tk_done, t + 1)
                wait_ge(e, s_done, t - 1)
                if is_step(b, 0) and g == 0:
                    e.wait_ge(gains_done, 1)
                e.activation(KTr[:, g % 2, :], tk_bank[:, :], ACT.Copy, scale=gqk[:, 0:1]).then_inc(kt_saved, 1)

            def hidden_hi(b, half):
                e.wait_ge(ht_done, 2 * b + half + 1)
                wait_ge(e, down_done, b)
                e.activation(HTh[:, half, :], tk_bank[:, :], ACT.Copy).then_inc(ht_hi, 1)

            def ffn_in_hi(b):
                e.wait_ge(ft_done, b + 1)
                wait_ge(e, gate_done, 2 * b)
                e.activation(xfT[:, 0, :], tk_bank[:, 0:D], ACT.Copy).then_inc(ft_hi, 1)

            def split_hi(b, n):
                if is_step(b, B):
                    if n == 0:
                        e.wait_ge(v_proj, SLOTS)
                    if n == EX // 2 + 1:
                        e.wait_ge(w_done, SLOTS)
                    chunk_ready(e, CHUNKS + n)
                    hi, lo, src = layer1_chunk(n)
                    e.activation(hi, src, ACT.Copy).then_inc(stage_hi, 1)

            def c_ctx(b):
                wait_ge(e, qkv_done, b)
                e.activation(cT[:, 0, :], ctxT[:, b, :], ACT.Copy).then_inc(c_chi, 1)

            def c_inputs(b):
                e.wait_ge(c_turned, b + 1)
                e.activation(xaT[:, 0, :], m1[:, 0:D], ACT.Copy).then_inc(c_xhi, 1)

            def c_save(b):
                e.wait_ge(qkv_done, b + 1)
                e.activation(qk[:, 0:D], m1[:, D:2 * D], ACT.Copy)
                e.activation(qk[:, D:2 * D], m2[:, 0:D], ACT.Copy).then_inc(qk_saved, 1)
                if is_step(b, 0):
                    e.wait_ge(ht_done, 2 * B)
                e.activation(Vn, m2[:, D:2 * D], ACT.Copy).then_inc(vn_saved, 1)

            def move_v(b):
                e.wait_ge(vn_saved, b + 1)
                wait_ge(e, av_done, SG * b)
                e.activation(Va[:, :, 0:D1], Vn.rearrange("p (h d) -> p h d", h=H1), ACT.Copy).then_inc(va_done, 1)

            def c_stack(b):
                r3 = rot.rearrange("p (s h d) -> p s h d", s=2, d=D1)
                e.wait_ge(rope_done, b + 1)
                wait_ge(e, t2_done, b)
                two = [P, H1, 2, D1]
                e.activation(SQ[:, :, 0:2, :], r3[:, 0].unsqueeze(2).to_broadcast(two), ACT.Copy).then_inc(stack_hi, 1)
                e.activation(SK[:, :, 0:3:2, :], r3[:, 1].unsqueeze(2).to_broadcast(two), ACT.Copy)\
                 .then_inc(stack_hi, 1)

            def t1k_save(b):
                e.wait_ge(t1_done, b + 1)
                wait_ge(e, st_done, SG * b)
                e.activation(KT1.rearrange("p t q -> p (t q)"), m2[:, :].bitcast(F16), ACT.Copy)\
                 .then_inc(t1k_saved, 1)

            def exp_group(b, j):
                e.wait_ge(st_done, SG * b + j + 1)
                wait_ge(e, av_done, SG * b + j - 3)
                e.activation(E2[:, j % 4, :], s_banks[j % 2][:, :], ACT.Exp, scale=float(D1) ** -0.5)\
                 .then_inc(e_done, 1)

            def ot2_save(b):
                e.wait_ge(ot2_done, b + 1)
                e.activation(OT2[0], m1[:, 0:D], ACT.Copy).then_inc(ot2_hi, 1)

            def d_inputs(b):
                e.wait_ge(d_turned, b + 1)
                wait_ge(e, u2_done, 4 * b)
                e.activation(xfT[:, 0, :], m1[:, 0:D], ACT.Copy).then_inc(d_xhi, 1)

            def route(b):
                e.wait_ge(route_step, 7 * b + 5)
                e.activation(rw[:, 1:2], gap[:, :], ACT.Exp).then_inc(gap_exp, 1)

            def tanh_chunk(b, c):
                n = 4 * b + c
                e.wait_ge(g2_done, n + 1)
                if c == 3:
                    wait_ge(e, h2t_done, 4 * b)
                else:
                    wait_ge(e, h2t_done, 4 * (b - 1) + c + 2)
                e.activation(H2[:, c * 2 * CH:(c + 1) * 2 * CH], g_bank[:, 0:2 * CH], ACT.Tanh, scale=0.5)\
                 .then_inc(g_tanh, 1)

            def ht_hi2(b, c):
                a, z = CHUNK_TILES[c]
                e.wait_ge(h2t_done, 4 * b + c + 1)
                wait_ge(e, dn_done, b)
                e.activation(HT2[0][:, a * P:z * P], m3[:, 0:(z - a) * P], ACT.Copy).then_inc(h2t_hi, 1)
            def step1(i, cur, prv, old, nxt):
                split_hi(i, 0)
                if cur:
                    square_q(i, 0)
                    square_k(i, 0)
                    save_v(i, 0)
                    split_hi0(i, 0)
                if prv:
                    out_hi(i - 1, 2)
                    exponentials(i - 1, 3)
                split_hi(i, 1)
                if old:
                    tanh_up(i - 2, 1)
                if cur:
                    save_qt(i, 0)
                    save_kt(i, 0)
                split_hi(i, 2)
                if old:
                    hidden_hi(i - 2, 0)
                if cur:
                    square_q(i, 1)
                    square_k(i, 1)
                split_hi(i, 3)
                if cur:
                    save_v(i, 1)
                    split_hi0(i, 1)
                if prv:
                    out_hi(i - 1, 3)
                if cur:
                    exponentials(i, 0)
                    save_qt(i, 1)
                    save_kt(i, 1)
                if old:
                    hidden_hi(i - 2, 1)
                split_hi(i, 4)
                if cur:
                    square_q(i, 2)
                    square_k(i, 2)
                    save_v(i, 2)
                    split_hi0(i, 2)
                    out_hi(i, 0)
                    exponentials(i, 1)
                split_hi(i, 5)
                if cur:
                    save_qt(i, 2)
                    save_kt(i, 2)
                if prv:
                    ffn_in_hi(i - 1)
                if cur:
                    square_q(i, 3)
                    square_k(i, 3)
                    save_v(i, 3)
                split_hi(i, 6)
                if cur:
                    split_hi0(i, 3)
                    out_hi(i, 1)
                    exponentials(i, 2)
                if prv:
                    tanh_up(i - 1, 0)
                if cur:
                    save_qt(i, 3)
                    save_kt(i, 3)
                if nxt:
                    prep(i + 1)
                if is_step(i, B + 1):
                    c_ctx(0)
                    c_inputs(0)
                    c_save(0)
                    c_stack(0)
                    move_v(0)
                    t1k_save(0)

            batches(e, step1)

            def step(i, cur, prv, nxt):
                if prv:
                    tanh_chunk(i - 1, 0)
                if cur:
                    exp_group(i, 0)
                if nxt:
                    c_ctx(i + 1)
                if cur:
                    exp_group(i, 1)
                    exp_group(i, 2)
                if prv:
                    tanh_chunk(i - 1, 1)
                if nxt:
                    c_inputs(i + 1)
                if cur:
                    exp_group(i, 3)
                    exp_group(i, 4)
                    exp_group(i, 5)
                    exp_group(i, 6)
                if nxt:
                    c_save(i + 1)
                if prv:
                    ht_hi2(i - 1, 0)
                    tanh_chunk(i - 1, 2)
                if cur:
                    exp_group(i, 7)
                if nxt:
                    c_stack(i + 1)
                if prv:
                    ht_hi2(i - 1, 1)
                    tanh_chunk(i - 1, 3)
                if nxt:
                    move_v(i + 1)
                    t1k_save(i + 1)
                if cur:
                    ot2_save(i)
                if prv:
                    ht_hi2(i - 1, 2)
                    ht_hi2(i - 1, 3)
                if cur:
                    d_inputs(i)
                    route(i)

            steps(e, step)

        @block.vector
        def _(e):
            def split_chunk_lo(c):
                e.wait_ge(stage_hi, c + 1)
                dst, hi = (W1l[:, c, :, :], W1h[:, c, :, :]) if c < WO else \
                    (Wol[:, (c - WO) * 8:(c - WO + 1) * 8, :], Woh[:, (c - WO) * 8:(c - WO + 1) * 8, :])
                e.tensor_tensor(dst, stage[:, c % 2, :].rearrange("p (t n) -> p t n", n=dst.shape[2]),
                                hi.bitcast(F32), ALU.subtract).then_inc(stage_lo, 1)

            def signs(n):
                c = TERN + n
                w, t = stage[:, c % 2, :], T[:, n, :]
                chunk_ready(e, c)
                e.tensor_reduce(wsum[:, n:n + 1], w, AX.X, ALU.add, apply_absolute_value=True)\
                 .then_inc(wsum_done, 1)
                e.wait_ge(wtot_done, n + 1)
                e.tensor_scalar(wscale[:, n:n + 1], y_sum[:, n:n + 1], 1.0 / (4 * BANK * P), 1e-8,
                                ALU.mult, ALU.add).then_inc(low_done, 1)
                e.wait_ge(low_done, 4 * n + 1)
                e.tensor_scalar(th[:, n:n + 1], wscale[:, n:n + 1], 0.5, None, ALU.mult).then_inc(low_done, 1)
                e.tensor_scalar(nth[:, n:n + 1], wscale[:, n:n + 1], -0.5, None, ALU.mult).then_inc(low_done, 1)
                e.wait_ge(low_done, 4 * n + 3)
                e.tensor_scalar(t, w, nth[:, n:n + 1], None, ALU.is_lt).then_inc(low_done, 1)
                e.wait_ge(low_done, 4 * n + 4)
                e.scalar_tensor_tensor(out=t, in0=w, scalar=th[:, n:n + 1], in1=t.bitcast(F32),
                                       op0=ALU.is_gt, op1=ALU.subtract).then_inc(sign_done, 1)

            y_sum = v_bank[:, D:D + 3]

            def ln_stats(b, n, stats_sem, aggr_sem, src):
                wait_ge(e, (rstd_done, frstd_done)[n], b)
                e.sem_inc(waits_passed, 1)
                e.bn_stats(stats[:, n, :], src).then_inc(stats_sem, 1)
                e.wait_ge(stats_sem, b + 1)
                e.sem_inc(waits_passed, 1)
                e.bn_aggr(mv[:, n, :], stats[:, n, :]).then_inc(aggr_sem, 1)

            def ln_apply(b, n, rstd_sem, done, src, turned):
                e.wait_ge(rstd_sem, b + 1)
                wait_ge(e, turned, b)
                e.tensor_scalar(xn[:, n, :], src, mv[:, n, 0:1], rstd[:, n:n + 1], ALU.subtract, ALU.mult)\
                 .then_inc(done, 1)

            def prep(b):
                e.wait_ge(c_hi, b + 1)
                e.tensor_tensor(cT[:, 1, :], ctxT[:, b, :], cT[:, 0, :].bitcast(F32), ALU.subtract)\
                 .then_inc(c_lo, 1)
                e.wait_ge(xt_hi, b + 1)
                e.tensor_tensor(xaT[:, 1, :], tk_bank[:, 0:D], xaT[:, 0, :].bitcast(F32), ALU.subtract)\
                 .then_inc(xt_lo, 1)

            def angles():
                n = [0]
                def step(ins):
                    n[0] += 1
                    ins.then_inc(ang_step, 1)
                    e.wait_ge(ang_step, n[0])
                e.wait_ge(pos_in, 48)
                e.wait_ge(gates_done, 1)
                step(e.tensor_tensor(btg[:, :], btg[:, :], tgates[:, 1:2].to_broadcast([P, D]), ALU.mult))
                for f in range(2):
                    step(e.tensor_scalar(ang[:, 0, :, :, f], pos[:, :, :], 10000.0 ** (-f / 2.0), None, ALU.mult))
                step(e.tensor_scalar(ang[:, 1], ang[:, 0], math.pi / 2, None, ALU.add))
                step(e.tensor_scalar(turns[:, :], ang_flat, 1 / (2 * math.pi), 1.5 * 2 ** 23, ALU.mult, ALU.add))
                step(e.tensor_scalar(turns[:, :], turns[:, :], 1.5 * 2 ** 23, None, ALU.subtract))
                step(e.scalar_tensor_tensor(out=ang_flat, in0=turns[:, :], scalar=-6.28125, in1=ang_flat,
                                            op0=ALU.mult, op1=ALU.add))
                step(e.scalar_tensor_tensor(out=ang_flat, in0=turns[:, :], scalar=-(2 * math.pi - 6.28125),
                                            in1=ang_flat, op0=ALU.mult, op1=ALU.add))
                e.tensor_scalar(ang_flat, ang_flat, 3.1415925, -3.1415925, ALU.min, ALU.max).then_inc(ang_done, 1)
                e.wait_ge(trig_done, 1)
                four = [P, B, 4]
                s3, c3 = (trig[:, k].rearrange("p b s f -> p b (s f)") for k in (0, 1))
                s8, c8 = (t.rearrange("p b (f c) -> p b f c", c=2) for t in (sin8[:, :, :], cos8[:, :, :]))
                step(e.tensor_copy(c8[:, :, :, 0], c3))
                step(e.tensor_copy(c8[:, :, :, 1], c3))
                step(e.tensor_copy(s8[:, :, :, 1], s3))
                step(e.tensor_scalar(s8[:, :, :, 0], s3, -1.0, None, ALU.mult))

            e.wait_ge(x_in[0], 16)
            ln_stats(0, 0, stats_done, aggr_done, X[:, 0, :])
            e.wait_ge(small_in, 64)
            e.tensor_tensor(gqk[:, :], gains[:, 0:1], gains[:, 1:2], ALU.mult).then_inc(gains_done, 1)
            ln_apply(0, 0, rstd_done, xn_done, X[:, 0, :], xt_done)
            angles()
            split_chunk_lo(0)
            prep(0)

            def attn_residual(b):
                e.wait_ge(w_done, GROUPS * b + GROUPS)
                e.scalar_tensor_tensor(out=X[:, b, :], in0=y_bank[:, 0:D], scalar=tgates[:, 0:1],
                                       in1=X[:, b, :], op0=ALU.mult, op1=ALU.add).then_inc(res_done, 1)
                e.wait_ge(res_done, b + 1)
                ln_stats(b, 1, fstats_done, faggr_done, X[:, b, :])

            def sum_q(b, g):
                t = GROUPS * b + g
                wait_ge(e, rs_done, t)
                e.wait_ge(sq_done, 2 * t + 1)
                e.tensor_reduce(ss[:, 0:HG], Qs[:, :, :], AX.X, ALU.add).then_inc(ss_done, 1)

            def sum_k(b, g):
                e.wait_ge(sq_done, 2 * (GROUPS * b + g) + 2)
                e.tensor_reduce(ss[:, HG:2 * HG], Ks[:, :, :], AX.X, ALU.add).then_inc(ss_done, 1)

            def split_lo0(b, g):
                if is_step(b, 0):
                    for c in SPLITS[g]:
                        split_chunk_lo(c)

            def ffn_norm(b):
                ln_apply(b, 1, frstd_done, fxn_done, X[:, b, :], ft_done)

            def shift_scores(b, g):
                u = GROUPS * b + g
                sc = s_bank[:, :].rearrange("p (h k) -> p h k", h=HG)
                e.wait_ge(s_done, u + 1)
                e.tensor_reduce(mx[:, :], sc, AX.X, ALU.max).then_inc(mx_done, 1)
                e.wait_ge(mx_done, u + 1)
                wait_ge(e, pt_done, u)
                e.tensor_tensor(Pr[:, :, :], sc, mx[:, :].unsqueeze(2).to_broadcast([P, HG, P]),
                                ALU.subtract).then_inc(sub_done, 1)

            def scale_q(b, g):
                e.wait_ge(rs_done, GROUPS * b + g + 1)
                e.tensor_tensor(Qs[:, :, :], q_bank[:, :].rearrange("p (h d) -> p h d", h=HG),
                                rs[:, 0:HG].unsqueeze(2).to_broadcast([P, HG, P]), ALU.mult).then_inc(q_scaled, 1)

            def scale_k(b, g):
                e.wait_ge(rs_done, GROUPS * b + g + 1)
                e.tensor_tensor(Ks[:, :, :], k_bank[:, :].rearrange("p (h d) -> p h d", h=HG),
                                rs[:, HG:2 * HG].unsqueeze(2).to_broadcast([P, HG, P]), ALU.mult)\
                 .then_inc(k_scaled, 1)

            def out_lo(b, g):
                e.wait_ge(o_hi, GROUPS * b + g + 1)
                e.tensor_tensor(OTl[:, g % 2, :], o_bank[:, :], OTh[:, g % 2, :].bitcast(F32),
                                ALU.subtract).then_inc(o_lo, 1)

            def row_sums(b, g):
                u = GROUPS * b + g
                e.wait_ge(exp_done, u + 1)
                e.tensor_reduce(rsum[:, :], Pr[:, :, :], AX.X, ALU.add).then_inc(sum_done, 1)
                e.wait_ge(sum_done, u + 1)
                wait_ge(e, norm_done, u)
                e.reciprocal(rinv[:, :], rsum[:, :]).then_inc(rinv_done, 1)

            def next_stats(b):
                if is_step(b, 1):
                    e.wait_ge(x_in[1], 16)
                ln_stats(b, 0, stats_done, aggr_done, X[:, b, :])

            def next_norm(b):
                ln_apply(b, 0, rstd_done, xn_done, X[:, b, :], xt_done)

            def ternary(b, g):
                if is_step(b, 1):
                    signs(g)
                if is_step(b, 1) and g == 2:
                    e.tensor_scalar(half_up[:, :], wscale[:, 0:1], 0.5, None, ALU.mult).then_inc(wscale_done, 1)
                    e.tensor_tensor(ffn_scale[:, 0:1], wscale[:, 1:2], wscale[:, 2:3], ALU.mult)\
                     .then_inc(wscale_done, 1)
                    e.wait_ge(wscale_done, 2)
                    e.scalar_tensor_tensor(out=ffn_scale[:, 0:1], in0=ffn_scale[:, 0:1], scalar=half_up[:, 0:1],
                                           in1=tgates[:, 2:3], op0=ALU.mult, op1=ALU.mult)\
                     .then_inc(wscale_done, 1)

            def act_up(b, half):
                n = 2 * b + half
                e.wait_ge(tanh_done, n + 1)
                e.scalar_tensor_tensor(out=H[:, half, :], in0=H[:, half, :], scalar=1.0, in1=v_bank[:, :],
                                       op0=ALU.add, op1=ALU.mult).then_inc(act_done, 1)

            def times_gate(b, half):
                n = 2 * b + half
                e.wait_ge(act_done, n + 1)
                e.wait_ge(gate_done, n + 1)
                e.tensor_tensor(H[:, half, :], H[:, half, :], s_bank[:, :], ALU.mult).then_inc(hid_done, 1)

            def ffn_residual(b):
                e.wait_ge(down_done, b + 1)
                if is_step(b, 0):
                    e.wait_ge(wscale_done, 3)
                e.scalar_tensor_tensor(out=X[:, b, :], in0=v_bank[:, 0:D], scalar=ffn_scale[:, 0:1],
                                       in1=X[:, b, :], op0=ALU.mult, op1=ALU.add).then_inc(fres_done, 1)

            def save_pt(b, g):
                e.wait_ge(pt_done, GROUPS * b + g + 1)
                wait_ge(e, o_done, GROUPS * b + g)
                e.tensor_copy(PT[:, :], tq_bank[:, :]).then_inc(pt_saved, 1)

            def hidden_lo(b, half):
                e.wait_ge(ht_hi, 2 * b + half + 1)
                e.tensor_tensor(HTl[:, half, :], tk_bank[:, :], HTh[:, half, :].bitcast(F32),
                                ALU.subtract).then_inc(ht_lo, 1)

            def ffn_in_lo(b):
                e.wait_ge(ft_hi, b + 1)
                e.tensor_tensor(xfT[:, 1, :], tk_bank[:, 0:D], xfT[:, 0, :].bitcast(F32), ALU.subtract)\
                 .then_inc(ft_lo, 1)

            def split_lo(b, n):
                if is_step(b, B):
                    e.wait_ge(stage_hi, TERN + n + 1)
                    hi, lo, src = layer1_chunk(n)
                    e.tensor_tensor(lo, src, hi.bitcast(F32), ALU.subtract).then_inc(stage_lo, 1)

            def lnc_stats(b):
                wait_ge(e, c_rstd, b)
                e.sem_inc(waits_passed, 1)
                e.bn_stats(stats[:, 0, :], X[:, b, :]).then_inc(c_stats, 1)
                e.wait_ge(c_stats, b + 1)
                e.sem_inc(waits_passed, 1)
                e.bn_aggr(mv[:, 0, :], stats[:, 0, :]).then_inc(c_aggr, 1)

            def c_norm(b):
                e.wait_ge(c_rstd, b + 1)
                wait_ge(e, c_turned, b)
                e.tensor_scalar(xn[:, 0, :], X[:, b, :], mv[:, 0, 0:1], rstd[:, 0:1], ALU.subtract, ALU.mult)\
                 .then_inc(c_xn, 1)
                e.wait_ge(c_chi, b + 1)
                e.tensor_tensor(cT[:, 1, :], ctxT[:, b, :], cT[:, 0, :].bitcast(F32), ALU.subtract)\
                 .then_inc(c_clo, 1)

            def c_inputs(b):
                e.wait_ge(c_xhi, b + 1)
                e.tensor_tensor(xaT[:, 1, :], m1[:, 0:D], xaT[:, 0, :].bitcast(F32), ALU.subtract)\
                 .then_inc(c_xlo, 1)

            def rope(b):
                four = [P, 2 * H1, 4]
                x = qk.rearrange("p (h f c) -> p h f c", h=2 * H1, c=2)
                r = rot.rearrange("p (h f c) -> p h f c", h=2 * H1, c=2)
                s_ = sin8[:, b, :].rearrange("p (f c) -> p f c", c=2)
                e.wait_ge(qk_saved, b + 1)
                e.tensor_tensor(r[:, :, :, 0], x[:, :, :, 1],
                                s_[:, :, 0].unsqueeze(1).to_broadcast(four), ALU.mult).then_inc(rope_a, 1)
                e.tensor_tensor(r[:, :, :, 1], x[:, :, :, 0],
                                s_[:, :, 1].unsqueeze(1).to_broadcast(four), ALU.mult).then_inc(rope_a, 1)
                e.wait_ge(rope_a, 2 * b + 2)
                q3 = qk.rearrange("p (h d) -> p h d", d=D1)
                e.tensor_tensor(q3, q3, cos8[:, b, :].unsqueeze(1).to_broadcast([P, 2 * H1, D1]), ALU.mult)\
                 .then_inc(rope_b, 1)
                e.wait_ge(rope_b, b + 1)
                e.tensor_tensor(rot, rot, qk, ALU.add).then_inc(rope_done, 1)

            def stack_los(b):
                r3 = rot.rearrange("p (s h d) -> p s h d", s=2, d=D1)
                e.wait_ge(stack_hi, 2 * b + 2)
                e.tensor_tensor(SQ[:, :, 2, :], r3[:, 0], SQ[:, :, 0, :], ALU.subtract).then_inc(stack_lo, 1)
                e.tensor_tensor(SK[:, :, 1, :], r3[:, 1], SK[:, :, 0, :], ALU.subtract).then_inc(stack_lo, 1)

            def t1q_save(b):
                e.wait_ge(t1_done, b + 1)
                e.tensor_copy(QT1.rearrange("p t q -> p (t q)"), m1[:, :].bitcast(F16)).then_inc(t1q_saved, 1)

            def max_group(b, j):
                e.wait_ge(sc_done, SG * b + j + 1)
                if j == 0:
                    wait_ge(e, m_split, 4 * b)
                a = (j // HG) * HG * HG + j % HG
                e.tensor_reduce(Mx[:, a:a + HG * (HG - 1) + 1:HG], s_banks[j % 2][:, :]
                                .rearrange("p (h k) -> p h k", h=HG), AX.X, ALU.max).then_inc(smax_done, 1)

            def split_max(b):
                e.wait_ge(smax_done, SG * b + SG)
                e.tensor_scalar(SQ[:, :, 3, 0], Mx[:, :], 1.0 / 64, None, ALU.mult).then_inc(m_split, 1)
                e.wait_ge(m_split, 4 * b + 1)
                e.scalar_tensor_tensor(out=Mr[:, :], in0=Mx[:, :], scalar=1.0 / 64, in1=SQ[:, :, 3, 0],
                                       op0=ALU.mult, op1=ALU.subtract).then_inc(m_split, 1)
                e.wait_ge(m_split, 4 * b + 2)
                e.tensor_copy(SQ[:, :, 3, 1], Mr[:, :]).then_inc(m_split, 1)
                e.wait_ge(m_split, 4 * b + 3)
                e.tensor_tensor(SQ[:, :, 3, 2], Mr[:, :], SQ[:, :, 3, 1], ALU.subtract).then_inc(m_split, 1)

            def t2_save(b):
                e.wait_ge(t2_done, b + 1)
                wait_ge(e, st_done, SG * b)
                e.tensor_copy(QT2.rearrange("p t q -> p (t q)"), m2[:, :].bitcast(F16)).then_inc(t2_saved, 1)

            def attn_norm(b):
                e.wait_ge(av_done, SG * b + SG)
                ov = ov_bank[:, 0:9 * H1].rearrange("p (h c) -> p h c", h=H1)
                e.reciprocal(rz[:, :], ov[:, :, D1]).then_inc(rz_done, 1)
                e.wait_ge(rz_done, b + 1)
                wait_ge(e, ot2_done, b)
                e.tensor_tensor(On.rearrange("p (h c) -> p h c", h=H1), ov[:, :, 0:D1],
                                rz[:, :].unsqueeze(2).to_broadcast([P, H1, D1]), ALU.mult).then_inc(on_done, 1)

            def attn_out(b):
                e.wait_ge(ot2_hi, b + 1)
                e.tensor_tensor(OT2[1], m1[:, 0:D], OT2[0].bitcast(F32), ALU.subtract).then_inc(ot2_lo, 1)

            def residual(b):
                e.wait_ge(w2_done, b + 1)
                e.wait_ge(bias_added, b + 1)
                e.scalar_tensor_tensor(out=X[:, b, :], in0=m1[:, D:2 * D], scalar=tgates[:, 1:2],
                                       in1=X[:, b, :], op0=ALU.mult, op1=ALU.add).then_inc(cres_done, 1)
                e.wait_ge(cres_done, b + 1)
                wait_ge(e, d_rstd, b)
                e.sem_inc(waits_passed, 1)
                e.bn_stats(stats[:, 1, :], X[:, b, :]).then_inc(d_stats, 1)
                e.wait_ge(d_stats, b + 1)
                e.sem_inc(waits_passed, 1)
                e.bn_aggr(mv[:, 1, :], stats[:, 1, :]).then_inc(d_aggr, 1)

            def d_norm(b):
                e.wait_ge(d_rstd, b + 1)
                wait_ge(e, d_turned, b)
                e.tensor_scalar(xn[:, 1, :], X[:, b, :], mv[:, 1, 0:1], rstd[:, 1:2], ALU.subtract, ALU.mult)\
                 .then_inc(d_xn, 1)

            def d_inputs(b):
                e.wait_ge(d_xhi, b + 1)
                e.tensor_tensor(xfT[:, 1, :], m1[:, 0:D], xfT[:, 0, :].bitcast(F32), ALU.subtract)\
                 .then_inc(d_xlo, 1)

            def winners(b):
                n = 7 * b
                e.wait_ge(route_done, b + 1)
                e.tensor_copy(lg[:, :], m1[:, D:D + EX]).then_inc(route_step, 1)
                e.wait_ge(route_step, n + 1)
                e.sem_inc(waits_passed, 1)
                e.max(top[:, :], lg[:, :]).then_inc(route_step, 1)
                e.wait_ge(route_step, n + 2)
                e.sem_inc(waits_passed, 1)
                e.max_index(topi[:, :], top[:, :], lg[:, :]).then_inc(route_step, 1)
                e.wait_ge(route_step, n + 3)
                e.tensor_copy(topf[:, :], topi[:, 0:2]).then_inc(route_step, 1)
                e.tensor_tensor(gap[:, :], top[:, 1:2], top[:, 0:1], ALU.subtract).then_inc(route_step, 1)

            def first_weight(b):
                e.wait_ge(gap_exp, b + 1)
                e.tensor_scalar(rw[:, 2:3], rw[:, 1:2], 1.0, 2.0, ALU.add, ALU.mult).then_inc(route_step, 1)
                e.wait_ge(route_step, 7 * b + 6)
                e.reciprocal(rw[:, 3:4], rw[:, 2:3]).then_inc(route_step, 1)

            def hidden(b, c):
                cols = slice(c * 2 * CH, (c + 1) * 2 * CH)
                n = 4 * b + c
                e.wait_ge(g_tanh, n + 1)
                e.scalar_tensor_tensor(out=H2[:, cols], in0=H2[:, cols], scalar=1.0, in1=g_bank[:, 0:2 * CH],
                                       op0=ALU.add, op1=ALU.mult).then_inc(g_act, 1)
                e.wait_ge(g_act, n + 1)
                e.wait_ge(u2_done, n + 1)
                if c == 0:
                    e.wait_ge(wte_step, 5 * b + 5)
                for k in range(2):
                    one = slice((2 * c + k) * CH, (2 * c + k + 1) * CH)
                    ins = e.scalar_tensor_tensor(out=H2[:, one], in0=H2[:, one], scalar=w_te[:, 2 * c + k:2 * c + k + 1],
                                                 in1=u_bank[:, k * CH:(k + 1) * CH], op0=ALU.mult, op1=ALU.mult)
                ins.then_inc(h2_done, 1)

            def ht_lo2(b, c):
                a, z = CHUNK_TILES[c]
                e.wait_ge(h2t_hi, 4 * b + c + 1)
                e.tensor_tensor(HT2[1][:, a * P:z * P], m3[:, 0:(z - a) * P], HT2[0][:, a * P:z * P].bitcast(F32),
                                ALU.subtract).then_inc(h2t_lo, 1)

            def d_out(b):
                e.wait_ge(dn_done, b + 1)
                e.scalar_tensor_tensor(out=X[:, b, :], in0=g_bank[:, 0:D], scalar=tgates[:, 3:4],
                                       in1=X[:, b, :], op0=ALU.mult, op1=ALU.add).then_inc(dres_done, 1)
            def step1(i, cur, prv, old, nxt):
                split_lo(i, 0)
                if cur:
                    sum_q(i, 0)
                    sum_k(i, 0)
                    split_lo0(i, 0)
                if prv:
                    shift_scores(i - 1, 3)
                if cur:
                    scale_q(i, 0)
                    scale_k(i, 0)
                if prv:
                    out_lo(i - 1, 2)
                    row_sums(i - 1, 3)
                split_lo(i, 1)
                if cur:
                    ternary(i, 0)
                if old:
                    act_up(i - 2, 1)
                    times_gate(i - 2, 1)
                if prv:
                    save_pt(i - 1, 3)
                if old:
                    hidden_lo(i - 2, 0)
                split_lo(i, 2)
                if cur:
                    sum_q(i, 1)
                    sum_k(i, 1)
                    split_lo0(i, 1)
                    shift_scores(i, 0)
                split_lo(i, 3)
                if cur:
                    scale_q(i, 1)
                    scale_k(i, 1)
                if prv:
                    out_lo(i - 1, 3)
                if cur:
                    row_sums(i, 0)
                    ternary(i, 1)
                    save_pt(i, 0)
                if old:
                    hidden_lo(i - 2, 1)
                if prv:
                    attn_residual(i - 1)
                if cur:
                    sum_q(i, 2)
                split_lo(i, 4)
                if cur:
                    sum_k(i, 2)
                    split_lo0(i, 2)
                if prv:
                    ffn_norm(i - 1)
                if cur:
                    shift_scores(i, 1)
                    scale_q(i, 2)
                    scale_k(i, 2)
                    out_lo(i, 0)
                    row_sums(i, 1)
                split_lo(i, 5)
                if nxt:
                    next_stats(i + 1)
                if cur:
                    ternary(i, 2)
                if old:
                    ffn_residual(i - 2)
                if cur:
                    save_pt(i, 1)
                if prv:
                    ffn_in_lo(i - 1)
                if cur:
                    sum_q(i, 3)
                    sum_k(i, 3)
                    split_lo0(i, 3)
                    shift_scores(i, 2)
                split_lo(i, 6)
                if cur:
                    scale_q(i, 3)
                    scale_k(i, 3)
                    out_lo(i, 1)
                    row_sums(i, 2)
                if nxt:
                    next_norm(i + 1)
                if prv:
                    act_up(i - 1, 0)
                    times_gate(i - 1, 0)
                if nxt:
                    prep(i + 1)
                if cur:
                    save_pt(i, 2)
                if is_step(i, B + 1):
                    lnc_stats(0)
                    c_norm(0)
                    c_inputs(0)
                    rope(0)
                    stack_los(0)
                    t1q_save(0)
                    max_group(0, 0)
                    max_group(0, 1)
                    max_group(0, 2)
                    max_group(0, 3)
                    max_group(0, 4)
                    max_group(0, 5)
                    max_group(0, 6)
                    max_group(0, 7)
                    split_max(0)
                    t2_save(0)

            batches(e, step1)

            def step(i, cur, prv, nxt):
                if nxt:
                    lnc_stats(i + 1)
                    c_norm(i + 1)
                if prv:
                    hidden(i - 1, 0)
                    hidden(i - 1, 1)
                if nxt:
                    c_inputs(i + 1)
                    rope(i + 1)
                if prv:
                    ht_lo2(i - 1, 0)
                    hidden(i - 1, 2)
                if nxt:
                    stack_los(i + 1)
                if cur:
                    attn_norm(i)
                if prv:
                    ht_lo2(i - 1, 1)
                    hidden(i - 1, 3)
                if nxt:
                    t1q_save(i + 1)
                    max_group(i + 1, 0)
                if cur:
                    attn_out(i)
                if prv:
                    ht_lo2(i - 1, 2)
                if nxt:
                    max_group(i + 1, 1)
                    max_group(i + 1, 2)
                if cur:
                    residual(i)
                if prv:
                    ht_lo2(i - 1, 3)
                if nxt:
                    max_group(i + 1, 3)
                    max_group(i + 1, 4)
                if cur:
                    d_norm(i)
                if nxt:
                    max_group(i + 1, 5)
                if cur:
                    d_inputs(i)
                if nxt:
                    max_group(i + 1, 6)
                    max_group(i + 1, 7)
                    split_max(i + 1)
                if prv:
                    d_out(i - 1)
                if cur:
                    winners(i)
                if nxt:
                    t2_save(i + 1)
                if cur:
                    first_weight(i)

            steps(e, step)

        @block.tensor
        def _(e):
            def three(out, lh, ll, rh, rl, start, stop):
                e.matmul(out, lh, rh, start=start, stop=False)
                e.matmul(out, lh, rl, start=False, stop=False)
                return e.matmul(out, ll, rh, start=False, stop=stop)

            def turn(out_bank, src, n, done):
                for k in range(n):
                    ins = e.transpose(out_bank[:, k * P:(k + 1) * P], src(k), ident[:, :])
                ins.then_inc(done, 1)

            def prep(b):
                e.wait_ge(xn_done, b + 1)
                wait_ge(e, kt_saved, GROUPS * b)
                turn(tk_bank, lambda k: xn[:, 0, k * P:(k + 1) * P], KT, xt_done)

            e.wait_ge(consts, 6)
            prep(0)

            def project_q(b, g):
                t = GROUPS * b + g
                if g == 0:
                    e.wait_ge(xt_lo, b + 1)
                if is_step(b, 0):
                    e.wait_ge(stage_lo, g + 1)
                wait_ge(e, q_scaled, t)
                for kt in range(KT):
                    ins = three(q_bank[:, :], xaT[:, 0, kt * P:(kt + 1) * P], xaT[:, 1, kt * P:(kt + 1) * P],
                                W1h[:, g, kt, :], W1l[:, g, kt, :], kt == 0, kt == KT - 1)
                ins.then_inc(q_proj, 1)

            def project_k(b, g):
                if g == 0:
                    e.wait_ge(c_lo, b + 1)
                if is_step(b, 0):
                    e.wait_ge(stage_lo, g + 1)
                wait_ge(e, k_scaled, GROUPS * b + g)
                three(k_bank[:, :], cT[:, 0, :], cT[:, 1, :], W1h[:, g, 2, :], W1l[:, g, 2, :], True, True)\
                    .then_inc(k_proj, 1)

            def project_v(b, g):
                wait_ge(e, v_saved, GROUPS * b + g)
                if g == 0:
                    wait_ge(e, act_done, 2 * (b - 2) + 1)
                if g == 1:
                    wait_ge(e, act_done, 2 * (b - 2) + 2)
                if g == 3:
                    wait_ge(e, fres_done, b - 1)
                if is_step(b, 1) and g > 0:
                    e.wait_ge(low_done, 4 * (g - 1) + 1)
                three(v_bank[:, :], cT[:, 0, :], cT[:, 1, :], W1h[:, g, 3, :], W1l[:, g, 3, :], True, True)\
                    .then_inc(v_proj, 1)

            def scores(b, h):
                u = GROUPS * b + h
                e.wait_ge(qt_saved, u + 1)
                e.wait_ge(kt_saved, u + 1)
                wait_ge(e, sub_done, u)
                if h == 3:
                    wait_ge(e, hid_done, 2 * (b - 1) + 1)
                if h == 0:
                    wait_ge(e, hid_done, 2 * (b - 2) + 2)
                for k in range(HG):
                    cols = slice(k * P, (k + 1) * P)
                    ins = e.matmul(s_bank[:, cols], QT[:, h % 2, cols], KTr[:, h % 2, cols],
                                   start=True, stop=True)
                ins.then_inc(s_done, 1)

            def values(b, h):
                u = GROUPS * b + h
                e.wait_ge(pt_saved, u + 1)
                wait_ge(e, o_lo, u)
                for k in range(HG):
                    cols = slice(k * P, (k + 1) * P)
                    ins = e.matmul(o_bank[:, cols], V[:, h, cols], PT[:, cols], start=True, stop=True)
                ins.then_inc(o_done, 1)

            def out_project(b, h):
                u = GROUPS * b + h
                e.wait_ge(o_lo, u + 1)
                if h == 0:
                    wait_ge(e, res_done, b)
                if is_step(b, 0):
                    e.wait_ge(stage_lo, WO + h // 2 + 1)
                for k in range(HG):
                    cols = slice(k * P, (k + 1) * P)
                    ins = three(y_bank[:, 0:D], OTh[:, h % 2, cols], OTl[:, h % 2, cols],
                                Woh[:, h * HG + k, :], Wol[:, h * HG + k, :],
                                h == 0 and k == 0, h == GROUPS - 1 and k == HG - 1)
                ins.then_inc(w_done, 1)

            def ternary_half(b, half, out, m, done):
                for kt in range(KT):
                    w = T[:, m, kt * E0 + half * BANK:kt * E0 + (half + 1) * BANK]
                    for part in range(2):
                        ins = e.matmul(out[:, :], xfT[:, part, kt * P:(kt + 1) * P], w,
                                       start=(kt == 0 and part == 0), stop=(kt == KT - 1 and part == 1))
                ins.then_inc(done, 1)

            def up(b, half):
                e.wait_ge(ft_lo, b + 1)
                if is_step(b, 0):
                    e.wait_ge(sign_done, 1)
                e.wait_ge(v_saved, last(*((b + 1, 3), (b + 2, 0))[half]) + 1)
                wait_ge(e, act_done, 2 * b + half)
                ternary_half(b, half, v_bank, 0, up_done)

            def gate(b, half):
                if is_step(b, 0):
                    e.wait_ge(sign_done, 2)
                t = GROUPS * (b + 1 + half) + (3, 0)[half]
                e.wait_ge(sub_done, min(t, SLOTS) if isinstance(t, int) else t)
                wait_ge(e, hid_done, 2 * b + half)
                ternary_half(b, half, s_bank, 1, gate_done)

            def ffn_down(b):
                e.wait_ge(ht_lo, 2 * b + 2)
                if is_step(b, 0):
                    e.wait_ge(sign_done, 3)
                e.wait_ge(v_saved, last(b + 2, 2) + 1)
                for k in range(ET):
                    cols = slice((k % HG) * P, (k % HG + 1) * P)
                    for part, HT in enumerate((HTh, HTl)):
                        ins = e.matmul(v_bank[:, 0:D], HT[:, k // HG, cols], T[:, 2, k * D:(k + 1) * D],
                                       start=(k == 0 and part == 0), stop=(k == ET - 1 and part == 1))
                ins.then_inc(down_done, 1)

            def sum_weights(b, g):
                if is_step(b, 1):
                    e.wait_ge(wsum_done, g + 1)
                    e.wait_ge(v_saved, GROUPS * b + g + 1)
                    e.matmul(v_bank[:, D + g:D + g + 1], ones[:, :], wsum[:, g:g + 1], start=True, stop=True)\
                     .then_inc(wtot_done, 1)

            def turn_q(b, g):
                t = GROUPS * b + g
                e.wait_ge(q_scaled, t + 1)
                wait_ge(e, qt_saved, t)
                wait_ge(e, pt_saved, t - 1)
                turn(tq_bank, lambda k: Qs[:, k, :], HG, tq_done)

            def turn_k(b, g):
                t = GROUPS * b + g
                e.wait_ge(k_scaled, t + 1)
                wait_ge(e, kt_saved, t)
                if g == 0:
                    wait_ge(e, xt_lo, b + 1)
                if g in (1, 2):
                    wait_ge(e, ht_lo, 2 * (b - 2) + g)
                if g == 3:
                    wait_ge(e, ft_lo, b)
                turn(tk_bank, lambda k: Ks[:, k, :], HG, tk_done)

            def turn_hidden(b, half):
                e.wait_ge(hid_done, 2 * b + half + 1)
                wait_ge(e, ht_lo, 2 * b + half)
                e.wait_ge(kt_saved, last(b + 2, half) + 1)
                turn(tk_bank, lambda k: H[:, half, k * P:(k + 1) * P], HG, ht_done)

            def turn_ffn_in(b):
                e.wait_ge(fxn_done, b + 1)
                e.wait_ge(kt_saved, last(b + 1, 2) + 1)
                turn(tk_bank, lambda k: xn[:, 1, k * P:(k + 1) * P], KT, ft_done)

            def turn_p(b, g):
                u = GROUPS * b + g
                e.wait_ge(norm_done, u + 1)
                e.wait_ge(qt_saved, min(u + 2, SLOTS) if isinstance(u, int) else u + 2)
                wait_ge(e, pt_saved, u)
                turn(tq_bank, lambda k: Pr[:, k, :], HG, pt_done)

            def c_turn(b):
                e.wait_ge(c_xn, b + 1)
                wait_ge(e, route_step, 7 * (b - 2) + 1)
                if is_step(b, 0):
                    e.wait_ge(hid_done, 2 * B)
                turn(m1, lambda k: xn[:, 0, k * P:(k + 1) * P], KT, c_turned)

            def c_project(b):
                e.wait_ge(c_xlo, b + 1)
                e.wait_ge(c_clo, b + 1)
                wait_ge(e, t2_saved, b)
                if is_step(b, 0):
                    e.wait_ge(stage_lo, TERN + 1)
                for kt in range(KT):
                    wh, wl = w2("q", kt, D)
                    three(m1[:, D:2 * D], xaT[:, 0, kt * P:(kt + 1) * P], xaT[:, 1, kt * P:(kt + 1) * P],
                          wh, wl, kt == 0, kt == KT - 1)
                wh, wl = w2("kv", 0, 2 * D)
                three(m2[:, :], cT[:, 0, :], cT[:, 1, :], wh, wl, True, True).then_inc(qkv_done, 1)

            def t1(b):
                e.wait_ge(stack_lo, 2 * b + 2)
                e.wait_ge(qk_saved, b + 1)
                e.wait_ge(vn_saved, b + 1)
                if is_step(b, 0):
                    e.wait_ge(consts, 7 + EX + 3)
                for stack, out in ((SQ, m1), (SK, m2)):
                    flat = stack.rearrange("p h s d -> p (h s d)")
                    for k in range(SG):
                        ins = e.transpose(out[:, :].bitcast(F16)[:, k * P:(k + 1) * P],
                                          flat[:, k * P:(k + 1) * P], ident16[:, :])
                ins.then_inc(t1_done, 1)

            def t2(b):
                e.wait_ge(m_split, 4 * b + 4)
                flat = SQ.rearrange("p h s d -> p (h s d)")
                for k in range(SG):
                    ins = e.transpose(m2[:, :].bitcast(F16)[:, k * P:(k + 1) * P],
                                      flat[:, k * P:(k + 1) * P], ident16[:, :])
                ins.then_inc(t2_done, 1)

            def score_group(b, j):
                if j == 0:
                    e.wait_ge(t1q_saved, b + 1)
                    e.wait_ge(t1k_saved, b + 1)
                    wait_ge(e, e_done, SG * b)
                elif j >= 2:
                    e.wait_ge(smax_done, SG * b + j - 1)
                rows = slice(32 * (j % HG), 32 * (j % HG) + 24)
                for k in range(HG):
                    tile = HG * (j // HG) + k
                    ins = e.matmul(s_banks[j % 2][:, k * P:(k + 1) * P], QT1[rows, tile, :], KT1[rows, tile, :],
                                   start=True, stop=True)
                ins.then_inc(sc_done, 1)

            def shifted_group(b, j):
                if j == 0:
                    e.wait_ge(t2_saved, b + 1)
                elif j >= 2:
                    e.wait_ge(e_done, SG * b + j - 1)
                rows = slice(32 * (j % HG), 32 * (j % HG) + 32)
                for k in range(HG):
                    tile = HG * (j // HG) + k
                    ins = e.matmul(s_banks[j % 2][:, k * P:(k + 1) * P], KT1[rows, tile, :], QT2[rows, tile, :],
                                   start=True, stop=True)
                ins.then_inc(st_done, 1)

            def av_group(b, j):
                e.wait_ge(e_done, SG * b + j + 1)
                if j == 0:
                    e.wait_ge(va_done, b + 1)
                    if is_step(b, 0):
                        e.wait_ge(consts, 7 + EX + 4)
                    wait_ge(e, on_done, b)
                for k, h in enumerate(heads(j)):
                    ins = e.matmul(ov_bank[:, 9 * h:9 * h + 9], E2[:, j % 4, k * P:(k + 1) * P], Va[:, h, :],
                                   start=True, stop=True)
                ins.then_inc(av_done, 1)

            def ot2_turn(b, t1_of):
                e.wait_ge(on_done, b + 1)
                e.wait_ge(t1q_saved, t1_of + 1)
                turn(m1, lambda k: On[:, k * P:(k + 1) * P], KT, ot2_done)

            def attn_out(b):
                e.wait_ge(ot2_lo, b + 1)
                for kt in range(KT):
                    wh, wl = w2("out", kt, D)
                    ins = three(m1[:, D:2 * D], OT2[0][:, kt * P:(kt + 1) * P], OT2[1][:, kt * P:(kt + 1) * P],
                                wh, wl, kt == 0, kt == KT - 1)
                ins.then_inc(w2_done, 1)

            def d_turn(b):
                e.wait_ge(d_xn, b + 1)
                turn(m1, lambda k: xn[:, 1, k * P:(k + 1) * P], KT, d_turned)

            def logits(b):
                e.wait_ge(d_xlo, b + 1)
                for kt in range(KT):
                    wh, wl = w2("route", kt, EX)
                    ins = three(m1[:, D:D + EX], xfT[:, 0, kt * P:(kt + 1) * P], xfT[:, 1, kt * P:(kt + 1) * P],
                                wh, wl, kt == 0, kt == KT - 1)
                ins.then_inc(route_done, 1)

            def expert_half(b, c, m, out, done, used):
                wait_ge(e, used, 4 * b + c)
                for kt in range(KT):
                    wh, wl = w2("exp", 4 * c + 2 * m + kt, 2 * CH)
                    ins = three(out[:, 0:2 * CH], xfT[:, 0, kt * P:(kt + 1) * P], xfT[:, 1, kt * P:(kt + 1) * P],
                                wh, wl, kt == 0, kt == KT - 1)
                ins.then_inc(done, 1)

            def expert_gate(b, c):
                if c == 0:
                    e.wait_ge(d_xlo, b + 1)
                    wait_ge(e, dres_done, b)
                if is_step(b, 0):
                    e.wait_ge(stage_lo, TERN + 2 + c)
                expert_half(b, c, 0, g_bank, g2_done, g_act)

            def expert_up(b, c):
                expert_half(b, c, 1, u_bank, u2_done, h2_done)

            def hidden_turn(b, c):
                a, z = CHUNK_TILES[c]
                e.wait_ge(h2_done, 4 * b + c + 1)
                wait_ge(e, h2t_lo, 4 * b + c)
                turn(m3, lambda k: H2[:, (a + k) * P:(a + k + 1) * P], z - a, h2t_done)

            def down(b, c):
                e.wait_ge(h2t_lo, 4 * b + c + 1)
                if is_step(b, 0) and c == 0:
                    e.wait_ge(stage_lo, TERN + L1_CHUNKS)
                if c == 0:
                    e.wait_ge(g_act, 4 * b + 4)
                for k in range(*CHUNK_TILES[c]):
                    cols = slice(k * P, (k + 1) * P)
                    ins = three(g_bank[:, 0:D], HT2[0][:, cols], HT2[1][:, cols], woh[:, k * D:(k + 1) * D],
                                wol[:, k * D:(k + 1) * D], k == 0, k == F2 // P - 1)
                if c == 3:
                    ins.then_inc(dn_done, 1)

            def step1(i, cur, prv, old, nxt):
                if prv:
                    scores(i - 1, 3)
                    values(i - 1, 2)
                if cur:
                    project_q(i, 0)
                    project_k(i, 0)
                    project_v(i, 0)
                    sum_weights(i, 0)
                if old:
                    up(i - 2, 1)
                    gate(i - 2, 1)
                if cur:
                    turn_q(i, 0)
                    turn_k(i, 0)
                if prv:
                    out_project(i - 1, 2)
                if old:
                    turn_hidden(i - 2, 0)
                if prv:
                    turn_p(i - 1, 3)
                if cur:
                    project_q(i, 1)
                    project_k(i, 1)
                    project_v(i, 1)
                    scores(i, 0)
                if prv:
                    values(i - 1, 3)
                if cur:
                    sum_weights(i, 1)
                    turn_q(i, 1)
                    turn_k(i, 1)
                if prv:
                    out_project(i - 1, 3)
                if old:
                    turn_hidden(i - 2, 1)
                if cur:
                    turn_p(i, 0)
                    project_q(i, 2)
                    project_k(i, 2)
                    project_v(i, 2)
                    scores(i, 1)
                    values(i, 0)
                    sum_weights(i, 2)
                if old:
                    ffn_down(i - 2)
                if cur:
                    turn_q(i, 2)
                    turn_k(i, 2)
                    out_project(i, 0)
                if prv:
                    turn_ffn_in(i - 1)
                if cur:
                    turn_p(i, 1)
                    project_q(i, 3)
                    project_k(i, 3)
                    project_v(i, 3)
                    scores(i, 2)
                    values(i, 1)
                if prv:
                    up(i - 1, 0)
                    gate(i - 1, 0)
                if cur:
                    turn_q(i, 3)
                    turn_k(i, 3)
                    out_project(i, 1)
                if nxt:
                    prep(i + 1)
                if cur:
                    turn_p(i, 2)
                if is_step(i, B + 1):
                    c_turn(0)
                    c_project(0)
                    t1(0)
                    score_group(0, 0)
                    score_group(0, 1)
                    score_group(0, 2)
                    score_group(0, 3)
                    score_group(0, 4)
                    score_group(0, 5)
                    score_group(0, 6)
                    score_group(0, 7)
                    t2(0)

            batches(e, step1)

            def step(i, cur, prv, nxt):
                if prv:
                    expert_gate(i - 1, 0)
                if cur:
                    shifted_group(i, 0)
                    shifted_group(i, 1)
                if prv:
                    expert_up(i - 1, 0)
                if cur:
                    av_group(i, 0)
                    shifted_group(i, 2)
                    av_group(i, 1)
                    shifted_group(i, 3)
                if nxt:
                    c_turn(i + 1)
                if prv:
                    expert_gate(i - 1, 1)
                    expert_up(i - 1, 1)
                if cur:
                    av_group(i, 2)
                    shifted_group(i, 4)
                    av_group(i, 3)
                    shifted_group(i, 5)
                if prv:
                    hidden_turn(i - 1, 0)
                if nxt:
                    c_project(i + 1)
                if cur:
                    av_group(i, 4)
                    shifted_group(i, 6)
                    av_group(i, 5)
                    shifted_group(i, 7)
                if prv:
                    expert_gate(i - 1, 2)
                    expert_up(i - 1, 2)
                if cur:
                    av_group(i, 6)
                    av_group(i, 7)
                if prv:
                    hidden_turn(i - 1, 1)
                    expert_gate(i - 1, 3)
                    expert_up(i - 1, 3)
                if nxt:
                    t1(i + 1)
                if prv:
                    hidden_turn(i - 1, 2)
                    down(i - 1, 0)
                if cur:
                    ot2_turn(i, i + 1 if nxt else B - 1)
                if nxt:
                    score_group(i + 1, 0)
                    score_group(i + 1, 1)
                if prv:
                    down(i - 1, 1)
                if nxt:
                    score_group(i + 1, 2)
                if cur:
                    attn_out(i)
                if nxt:
                    score_group(i + 1, 3)
                if prv:
                    hidden_turn(i - 1, 3)
                if nxt:
                    score_group(i + 1, 4)
                if prv:
                    down(i - 1, 2)
                if nxt:
                    score_group(i + 1, 5)
                if cur:
                    d_turn(i)
                if nxt:
                    score_group(i + 1, 6)
                    score_group(i + 1, 7)
                if prv:
                    down(i - 1, 3)
                if cur:
                    logits(i)
                if nxt:
                    t2(i + 1)

            steps(e, step)


INS = {"x": "x", "ctxT": "ctx_1024", "g_xattn": "g_xattn", "g_ffn": "g_ffn", "Wq0": "L0_xattn_Wq",
       "Wk0": "L0_xattn_Wk", "Wv0": "L0_xattn_Wv", "Wo0": "L0_xattn_Wo", "gq": "L0_xattn_gq",
       "gk": "L0_xattn_gk", "WuT": "L0_ffn_W_up", "WgT": "L0_ffn_W_gate", "WdT": "L0_ffn_W_down",
       "pos": "fside_BxSx2_0", "Wq1": "L1_xattn_Wq", "Wkv1": "L1_xattn_Wkv", "Wout1": "L1_xattn_Wout",
       "bout": "L1_xattn_bout", "gwT": "L1_ffn_gate_w", "e_gate": "L1_ffn_w_gate", "e_up": "L1_ffn_w_up",
       "e_down": "L1_ffn_w_down"}
TURNED = {"ctxT": (2, 0, 1), "WuT": (1, 0), "WgT": (1, 0), "WdT": (1, 0), "gwT": (1, 0)}


def kernel(**inputs):
    import numpy as np
    import concourse.bacc as bacc
    from concourse.bass_utils import run_bass_kernel_spmd

    nc = bacc.Bacc("TRN2", target_bir_lowering=False, num_devices=1)
    arrays, io = {}, {}
    for name, source in INS.items():
        a = np.asarray(inputs[source])
        a = np.ascontiguousarray(a.transpose(TURNED[name]) if name in TURNED else a)
        arrays[f"in_{name}"] = a
        io[name] = nc.dram_tensor(f"in_{name}", a.shape, mybir.dt.from_np(a.dtype), kind="ExternalInput").ap()
    shape = np.asarray(inputs["x"]).shape
    io["out"] = nc.dram_tensor("out_x", shape, F32, kind="ExternalOutput").ap()
    build(nc, io)
    return run_bass_kernel_spmd(nc, [arrays], core_ids=[0]).results[0]["out_x"]
```

```python
import math
from contextlib import ExitStack

import concourse.bass as bass
from concourse import mybir

F32 = mybir.dt.float32
F32R = mybir.dt.float32r
F16 = mybir.dt.float16
U32 = mybir.dt.uint32
ALU = mybir.AluOpType
ACT = mybir.ActivationFunctionType
AX = mybir.AxisListType

P = 128
GROUPS = 4
HG = 4
BANK = 512


def is_batch(b, batches):
    return not isinstance(b, int) or 0 <= b < batches


def is_step(i, n):
    return isinstance(i, int) and i == n


def wait_ge(engine, semaphore, value):
    if not isinstance(value, int) or value > 0:
        engine.wait_ge(semaphore, value)


def back(b, g, n):
    return (b, g - n) if g >= n else (b - 1, g - n + GROUPS)


def build(nc, io):
    B, S, D = io["x"].shape
    C = io["ctxT"].shape[0]
    INNER = io["Wq0"].shape[1]
    KT = D // P
    E0 = io["WuT"].shape[1]
    ET = E0 // P
    assert S == P and C == P and INNER == GROUPS * BANK and E0 == 2 * BANK and KT == 2
    SLOTS = B * GROUPS
    EX, _, CH = io["e_gate"].shape
    F2 = EX * CH
    D1 = 8
    H1 = D // D1
    L1_CHUNKS = 1 + EX // 2 + 2
    assert F2 % P == 0

    with ExitStack() as ctx:
        def sb(name, shape, dt=F32):
            return ctx.enter_context(nc.sbuf_tensor(name, shape, dt))

        def sem(name):
            return ctx.enter_context(nc.semaphore(name))

        bank = [ctx.enter_context(nc.psum_tensor(f"bank{n}", [P, BANK], F32)) for n in range(8)]
        q_bank, k_bank, v_bank, tq_bank, tk_bank, s_bank, o_bank, y_bank = bank

        X = sb("X", [P, B, D])
        W1h = sb("W1h", [P, GROUPS, 4, BANK], F32R)
        W1l = sb("W1l", [P, GROUPS, 4, BANK], F32R)
        Woh = sb("Woh", [P, INNER // P, D], F32R)
        Wol = sb("Wol", [P, INNER // P, D], F32R)
        T = sb("T", [P, 3, 4 * BANK], F32R)
        stage = sb("stage", [P, 2, 4 * BANK])
        ctxT = sb("ctxT_sb", [P, B, P])

        ident = sb("ident", [P, P])
        ones = sb("ones", [P, P])
        neg_half = sb("neg_half", [P, 2 * HG])
        eps = sb("eps", [P, 1])
        p_eps = sb("p_eps", [P, 2 * HG])
        gains = sb("gains", [P, 2])
        gqk = sb("gqk", [P, 1])
        gates = sb("gates", [P, 4])
        tgates = sb("tgates", [P, 4])
        wsum = sb("wsum", [P, 3])
        wscale = sb("wscale", [P, 3])
        half_up = sb("half_up", [P, 1])
        th = sb("th", [P, 3])
        nth = sb("nth", [P, 3])
        ffn_scale = sb("ffn_scale", [P, 2])

        stats = sb("stats", [P, 2, 6])
        mv = sb("mv", [P, 2, 2])
        var = sb("var", [P, 2])
        rstd = sb("rstd", [P, 2])
        xn = sb("xn", [P, 2, D])
        xaT = sb("xaT", [P, 2, D], F32R)
        cT = sb("cT", [P, 2, P], F32R)
        ss = sb("ss", [P, 2 * HG])
        rs = sb("rs", [P, 2 * HG])
        Qs = sb("Qs", [P, HG, P])
        Ks = sb("Ks", [P, HG, P])
        QT = sb("QT", [P, 2, BANK])
        KTr = sb("KTr", [P, 2, BANK])
        V = sb("V", [P, GROUPS, BANK])
        mx = sb("mx", [P, HG])
        Pr = sb("Pr", [P, HG, P])
        rsum = sb("rsum", [P, HG])
        rinv = sb("rinv", [P, HG])
        PT = sb("PT", [P, BANK])
        OTh = sb("OTh", [P, 2, BANK], F32R)
        OTl = sb("OTl", [P, 2, BANK], F32R)
        xfT = sb("xfT", [P, 2, D], F32R)
        H = sb("H", [P, 2, BANK])
        HTh = sb("HTh", [P, 2, BANK], F32R)
        HTl = sb("HTl", [P, 2, BANK], F32R)

        ident16 = sb("ident16", [P, P], F16)
        btg = sb("btg", [P, D])
        pos = sb("pos_sb", [P, B, 2])
        ang = sb("ang", [P, 2, B, 2, 2])
        turns = sb("turns", [P, 8 * B])
        trig = sb("trig", [P, 2, B, 2, 2])
        cos8 = sb("cos8", [P, B, D1])
        sin8 = sb("sin8", [P, B, D1])
        Vn = sb("Vn", [P, D])
        Mx = sb("Mx", [P, H1])
        Mr = sb("Mr", [P, H1])
        rz = sb("rz", [P, H1])
        iota8 = sb("iota8", [P, EX])
        lg, top, w_one, w_two, w_te = (sb(n, [P, EX]) for n in ("lg", "top", "w_one", "w_two", "w_te"))
        topi = sb("topi", [P, EX], U32)
        topf = sb("topf", [P, 2])
        gap = sb("gap", [P, 1])
        rw = sb("rw", [P, 6])
        ang_flat = ang[:, :, :, :, :].rearrange("p k b s f -> p (k b s f)")

        x_in = [sem(f"x_in{n}") for n in range(2)]
        ctx_in, small_in = sem("ctx_in"), sem("small_in")
        stage_in = [sem("stage_in0"), sem("stage_in1")]
        stage_hi, stage_lo = sem("stage_hi"), sem("stage_lo")
        consts, gains_done, gates_done = sem("consts"), sem("gains_done"), sem("gates_done")
        wsum_done, wtot_done, wscale_done = sem("wsum_done"), sem("wtot_done"), sem("wscale_done")
        low_done, sign_done = sem("low_done"), sem("sign_done")
        stats_done, aggr_done, eps_done, rstd_done, xn_done = (sem(n) for n in (
            "stats_done", "aggr_done", "eps_done", "rstd_done", "xn_done"))
        fstats_done, faggr_done, feps_done, frstd_done, fxn_done = (sem(n) for n in (
            "fstats_done", "faggr_done", "feps_done", "frstd_done", "fxn_done"))
        xt_done, xt_hi, xt_lo, c_hi, c_lo = (sem(n) for n in ("xt_done", "xt_hi", "xt_lo", "c_hi", "c_lo"))
        q_proj, k_proj, v_proj, sq_done, ss_done, ms_done, rs_done = (sem(n) for n in (
            "q_proj", "k_proj", "v_proj", "sq_done", "ss_done", "ms_done", "rs_done"))
        q_scaled, k_scaled, v_saved, tq_done, tk_done, qt_saved, kt_saved = (sem(n) for n in (
            "q_scaled", "k_scaled", "v_saved", "tq_done", "tk_done", "qt_saved", "kt_saved"))
        s_done, mx_done, sub_done, exp_done, sum_done, rinv_done, norm_done = (sem(n) for n in (
            "s_done", "mx_done", "sub_done", "exp_done", "sum_done", "rinv_done", "norm_done"))
        pt_done, pt_saved, o_done, o_hi, o_lo, w_done, res_done = (sem(n) for n in (
            "pt_done", "pt_saved", "o_done", "o_hi", "o_lo", "w_done", "res_done"))
        ft_done, ft_hi, ft_lo, up_done, gate_done, tanh_done, act_done, hid_done = (sem(n) for n in (
            "ft_done", "ft_hi", "ft_lo", "up_done", "gate_done", "tanh_done", "act_done", "hid_done"))
        ht_done, ht_hi, ht_lo, down_done, fres_done = (sem(n) for n in (
            "ht_done", "ht_hi", "ht_lo", "down_done", "fres_done"))
        pos_in, ang_step, ang_done, trig_done, c_stats, c_aggr = (sem(n) for n in (
            "pos_in", "ang_step", "ang_done", "trig_done", "c_stats", "c_aggr"))
        c_eps, c_rstd, c_xn, c_turned, c_chi, c_clo = (sem(n) for n in (
            "c_eps", "c_rstd", "c_xn", "c_turned", "c_chi", "c_clo"))
        c_xhi, c_xlo, qkv_done, qk_saved, vn_saved, va_done = (sem(n) for n in (
            "c_xhi", "c_xlo", "qkv_done", "qk_saved", "vn_saved", "va_done"))
        rope_a, rope_b, rope_done, stack_hi, stack_lo, t1_done = (sem(n) for n in (
            "rope_a", "rope_b", "rope_done", "stack_hi", "stack_lo", "t1_done"))
        t1q_saved, sc_done, smax_done, m_split, t2_done, t2_saved = (sem(n) for n in (
            "t1q_saved", "sc_done", "smax_done", "m_split", "t2_done", "t2_saved"))
        t1k_saved, st_done, e_done, av_done, rz_done, on_done = (sem(n) for n in (
            "t1k_saved", "st_done", "e_done", "av_done", "rz_done", "on_done"))
        ot2_done, ot2_hi, ot2_lo, w2_done, bias_added, cres_done = (sem(n) for n in (
            "ot2_done", "ot2_hi", "ot2_lo", "w2_done", "bias_added", "cres_done"))
        d_stats, d_aggr, d_eps, d_rstd, d_xn, d_turned = (sem(n) for n in (
            "d_stats", "d_aggr", "d_eps", "d_rstd", "d_xn", "d_turned"))
        d_xhi, d_xlo, route_done, route_step, gap_exp, g2_done = (sem(n) for n in (
            "d_xhi", "d_xlo", "route_done", "route_step", "gap_exp", "g2_done"))
        u2_done, g_tanh, g_act, h2_done, wte_step, h2t_done = (sem(n) for n in (
            "u2_done", "g_tanh", "g_act", "h2_done", "wte_step", "h2t_done"))
        h2t_hi, h2t_lo, dn_done, dres_done = (sem(n) for n in (
            "h2t_hi", "h2t_lo", "dn_done", "dres_done"))
        out_done = sem("out_done")
        waits_passed = sem("waits_passed")

        w1h, w1l = (w[:, :, :, :].rearrange("p g m n -> p (g m n)") for w in (W1h, W1l))
        woh, wol = (w[:, :, :].rearrange("p t n -> p (t n)") for w in (Woh, Wol))
        at = 0
        place = {}
        for name, size in (("q", KT * D), ("kv", 2 * D), ("out", KT * D), ("route", KT * EX),
                           ("exp", EX * 4 * CH)):
            place[name] = at
            at += size
        assert at + D <= GROUPS * 4 * BANK

        def w2(name, n, size):
            a = place[name] + n * size
            return w1h[:, a:a + size], w1l[:, a:a + size]

        t_flat = T[:, :, :].rearrange("p m n -> p (m n)")
        HT2 = [t_flat[:, n * F2:(n + 1) * F2] for n in range(2)]
        OT2 = [w[:, at:at + D] for w in (w1h, w1l)]
        E2 = V
        QT1 = QT[:, 0, :].bitcast(F16).rearrange("p (t q) -> p t q", q=P)
        QT2 = QT[:, 1, :].bitcast(F16).rearrange("p (t q) -> p t q", q=P)
        KT1 = KTr[:, 0, :].bitcast(F16).rearrange("p (t q) -> p t q", q=P)
        qk = Qs[:, :, :].rearrange("p h d -> p (h d)")
        rot = Ks[:, :, :].rearrange("p h d -> p (h d)")
        SQ = PT[:, :].bitcast(F16).rearrange("p (h s d) -> p h s d", h=H1, s=4)
        SK = Pr[:, :, :].rearrange("p h d -> p (h d)").bitcast(F16).rearrange("p (h s d) -> p h s d", h=H1, s=4)
        Va = KTr[:, 1, 0:9 * H1].rearrange("p (h c) -> p h c", h=H1)
        On = qk[:, 0:D]
        H2 = stage[:, 0, 0:F2]
        m1, m2, g_bank, sb_bank, m3, u_bank, sa_bank, ov_bank = bank
        s_banks = (sa_bank, sb_bank)
        SG = 2 * HG

        def heads(j):
            return [HG * (HG * (j // HG) + k) + j % HG for k in range(HG)]

        CHUNK_TILES = ((0, 2), (2, 5), (5, 8), (8, 11))

        def layer1_chunk(n):
            src = stage[:, (CHUNKS + n) % 2, :]
            if n <= EX // 2:
                a = 0 if n == 0 else place["exp"] + (n - 1) * 4 * 2 * CH
                size = place["exp"] if n == 0 else 4 * 2 * CH
                return w1h[:, a:a + size], w1l[:, a:a + size], src[:, 0:size]
            a, z = ((0, 6), (6, F2 // P))[n - 1 - EX // 2]
            return woh[:, a * D:z * D], wol[:, a * D:z * D], src[:, 0:(z - a) * D]

        block = ctx.enter_context(nc.Block())

        WO, TERN = GROUPS, GROUPS + 2
        CHUNKS = TERN + 3

        def chunk_half(c, half):
            if c < WO:
                hi, lo = (w[:, c, 2 * half:2 * half + 2, :] for w in (W1h, W1l))
            else:
                a = (2 * (c - WO) + half) * (INNER // P // 4)
                hi, lo = (w[:, a:a + INNER // P // 4, :] for w in (Woh, Wol))
            src = stage[:, c % 2, half * 2 * BANK:(half + 1) * 2 * BANK]
            return hi, lo, src.rearrange("p (t n) -> p t n", n=hi.shape[2])

        def chunk_ready(e, c):
            e.wait_ge(stage_in[c % 2], 64 * (c // 2 + 1))

        def last(b, g):
            t = GROUPS * b + g
            return min(t, SLOTS - 1) if isinstance(t, int) else t

        def batches(e, step):
            for i in range(3):
                step(i, True, i > 0, i > 1, True)
            with e.Fori(3, B - 1) as i:
                step(i, True, True, True, True)
            for i in range(B - 1, B + 2):
                step(i, i < B, i <= B, True, False)

        def steps(e, step):
            for i in range(1, B + 1):
                step(i, i < B, True, i < B - 1)

        @block.sync
        def _(e):
            xd = io["x"].rearrange("b p d -> p b d")
            e.dma_start(X[:, 0:1, :], xd[:, 0:1, :]).then_inc(x_in[0], 16)
            e.dma_start(ctxT[:, :, :], io["ctxT"]).then_inc(ctx_in, 16)

            def load1(n, s, done):
                if n == 0:
                    for name, w in (("q", "Wq1"), ("kv", "Wkv1"), ("out", "Wout1"), ("route", "gwT")):
                        src = io[w].rearrange("(t p) n -> p t n", p=P)
                        size = src.shape[1] * src.shape[2]
                        e.dma_start(s[:, place[name]:place[name] + size].rearrange("p (t n) -> p t n", n=src.shape[2]),
                                    src).then_inc(done, 16)
                elif n <= EX // 2:
                    for m, w in enumerate(("e_gate", "e_up")):
                        for kt in range(KT):
                            a = (2 * m + kt) * 2 * CH
                            src = io[w][2 * n - 2:2 * n, kt * P:(kt + 1) * P, :].rearrange("e p f -> p e f")
                            e.dma_start(s[:, a:a + 2 * CH].rearrange("p (e f) -> p e f", f=CH), src).then_inc(done, 16)
                else:
                    a, z = ((0, 6), (6, F2 // P))[n - 1 - EX // 2]
                    src = io["e_down"].rearrange("e f d -> (e f) d").rearrange("(t p) d -> p t d", p=P)
                    e.dma_start(s[:, 0:(z - a) * D].rearrange("p (t d) -> p t d", d=D), src[:, a:z, :])\
                     .then_inc(done, 64)

            def load(c):
                s = stage[:, c % 2, :]
                if c >= 2:
                    if c - 2 < TERN:
                        e.wait_ge(stage_lo, 2 * (c - 1))
                    elif c - 2 < CHUNKS:
                        e.wait_ge(sign_done, 2 * (c - 2 - TERN + 1))
                    else:
                        e.wait_ge(stage_lo, 2 * TERN + c - 2 - CHUNKS + 1)
                if c < WO:
                    cols = slice(c * BANK, (c + 1) * BANK)
                    for kt in range(KT):
                        e.dma_start(s[:, kt * BANK:(kt + 1) * BANK],
                                    io["Wq0"][kt * P:(kt + 1) * P, cols]).then_inc(stage_in[c % 2], 16)
                    e.dma_start(s[:, 2 * BANK:3 * BANK], io["Wk0"][:, cols]).then_inc(stage_in[c % 2], 16)
                    e.dma_start(s[:, 3 * BANK:4 * BANK], io["Wv0"][:, cols]).then_inc(stage_in[c % 2], 16)
                elif c < TERN:
                    n = INNER // P // 2
                    src = io["Wo0"].rearrange("(t p) n -> p t n", p=P)[:, (c - WO) * n:(c - WO + 1) * n, :]
                    e.dma_start(s.rearrange("p (t n) -> p t n", n=D), src).then_inc(stage_in[c % 2], 64)
                elif c >= CHUNKS:
                    load1(c - CHUNKS, s, stage_in[c % 2])
                else:
                    src = io[("WuT", "WgT", "WdT")[c - TERN]].rearrange("(t p) n -> p t n", p=P)
                    e.dma_start(s.rearrange("p (t n) -> p t n", n=src.shape[2]), src)\
                     .then_inc(stage_in[c % 2], 64)

            load(0)
            load(1)
            e.dma_start(X[:, 1:B, :], xd[:, 1:B, :]).then_inc(x_in[1], 16)
            for c in range(2, CHUNKS):
                load(c)
            for c in range(CHUNKS, CHUNKS + L1_CHUNKS):
                load(c)

            def store(i, cur, prv, nxt):
                if prv:
                    e.wait_ge(dres_done, i)
                    e.dma_start(io["out"][i - 1], X[:, i - 1, :]).then_inc(out_done, 16)

            steps(e, store)
            e.wait_ge(out_done, 16 * B)

        @block.gpsimd
        def _(e):
            e.memset(ident[:, :], 0.0).then_inc(consts, 1)
            e.memset(ones[:, :], 1.0).then_inc(consts, 1)
            e.memset(neg_half[:, :], -0.5).then_inc(consts, 1)
            e.memset(eps[:, :], 1e-5).then_inc(consts, 1)
            e.memset(p_eps[:, :], 1e-5 * P).then_inc(consts, 1)
            e.wait_ge(consts, 5)
            e.affine_select(out=ident[:, :], in_=ident[:, :], compare_op=ALU.not_equal, fill=1.0,
                            base=0, pattern=[[-1, P]], channel_multiplier=1).then_inc(consts, 1)
            e.wait_ge(consts, 6)
            e.tensor_copy(ident16[:, :], ident[:, :]).then_inc(consts, 1)

            def ln_rstd(b, n, aggr, added, done, used):
                e.wait_ge(aggr, b + 1)
                wait_ge(e, used, b)
                e.tensor_tensor(var[:, n:n + 1], mv[:, n, 1:2], eps[:, :], ALU.add).then_inc(added, 1)
                e.wait_ge(added, b + 1)
                e.tensor_tensor(rstd[:, n:n + 1], var[:, n:n + 1], neg_half[:, 0:1], ALU.pow).then_inc(done, 1)

            ln_rstd(0, 0, aggr_done, eps_done, rstd_done, xn_done)

            def ln_a(b):
                ln_rstd(b, 0, aggr_done, eps_done, rstd_done, xn_done)

            def ln_f(b):
                ln_rstd(b, 1, faggr_done, feps_done, frstd_done, fxn_done)

            def rms(b, g, k, used):
                t = GROUPS * b + g
                cols = slice(k * HG, (k + 1) * HG)
                e.wait_ge(ss_done, 2 * t + k + 1)
                wait_ge(e, used, t)
                e.tensor_tensor(rs[:, cols], ss[:, cols], p_eps[:, cols], ALU.add).then_inc(ms_done, 1)
                e.wait_ge(ms_done, 2 * t + k + 1)
                e.tensor_tensor(rs[:, cols], rs[:, cols], neg_half[:, cols], ALU.pow).then_inc(rs_done, 1)

            def rms_q(b, g):
                rms(b, g, 0, q_scaled)

            def rms_k(b, g):
                rms(b, g, 1, k_scaled)

            def normalise(b, g):
                e.wait_ge(rinv_done, GROUPS * b + g + 1)
                e.tensor_tensor(Pr[:, :, :], Pr[:, :, :], rinv[:, :].unsqueeze(2).to_broadcast([P, HG, P]),
                                ALU.mult).then_inc(norm_done, 1)

            def ln_c(b):
                ln_rstd(b, 0, c_aggr, c_eps, c_rstd, c_xn)

            def ln_d(b):
                ln_rstd(b, 1, d_aggr, d_eps, d_rstd, d_xn)

            def add_bias(b):
                e.wait_ge(c_xn, b + 1)
                e.tensor_tensor(X[:, b, :], X[:, b, :], btg[:, :], ALU.add).then_inc(bias_added, 1)

            def weights(b):
                n = 5 * b
                e.wait_ge(route_step, 7 * b + 7)
                e.tensor_tensor(rw[:, 5:6], rw[:, 1:2], rw[:, 3:4], ALU.mult).then_inc(wte_step, 1)
                e.tensor_scalar(w_one[:, :], iota8[:, :], topf[:, 0:1], rw[:, 3:4], ALU.is_equal, ALU.mult)\
                 .then_inc(wte_step, 1)
                e.tensor_scalar(w_two[:, :], iota8[:, :], topf[:, 1:2], None, ALU.is_equal).then_inc(wte_step, 1)
                e.wait_ge(wte_step, n + 3)
                e.tensor_tensor(w_two[:, :], w_two[:, :], rw[:, 5:6].to_broadcast([P, EX]), ALU.mult)\
                 .then_inc(wte_step, 1)
                e.wait_ge(wte_step, n + 4)
                wait_ge(e, h2_done, 4 * b)
                e.tensor_tensor(w_te[:, :], w_one[:, :], w_two[:, :], ALU.add).then_inc(wte_step, 1)

            def ready_layer1(b):
                if is_step(b, B):
                    for k in range(EX):
                        e.memset(iota8[:, k:k + 1], float(k)).then_inc(consts, 1)
                    e.wait_ge(o_done, SLOTS)
                    e.memset(SQ[:, :, 3, :], 0.0).then_inc(consts, 1)
                    e.memset(SK[:, :, 3, 3:D1], 0.0).then_inc(consts, 1)
                    e.memset(SK[:, :, 3, 0:3], -64.0).then_inc(consts, 1)
                    e.memset(Va[:, :, D1:D1 + 1], 1.0).then_inc(consts, 1)

            def layer0_step(i, cur, prv, old, nxt):
                if cur:
                    rms_q(i, 0)
                    rms_k(i, 0)
                if prv:
                    normalise(i - 1, 3)
                if is_step(i, B):
                    ln_c(0)
                    add_bias(0)
                ready_layer1(i)
                if cur:
                    rms_q(i, 1)
                    rms_k(i, 1)
                    normalise(i, 0)
                if nxt:
                    ln_a(i + 1)
                if cur:
                    rms_q(i, 2)
                    rms_k(i, 2)
                    normalise(i, 1)
                if prv:
                    ln_f(i - 1)
                if cur:
                    rms_q(i, 3)
                if is_step(i, B + 1):
                    ln_c(1)
                    add_bias(1)
                if cur:
                    rms_k(i, 3)
                    normalise(i, 2)
                if is_step(i, B + 1):
                    ln_d(0)
                    weights(0)

            batches(e, layer0_step)

            def layer1_step(i, cur, prv, nxt):
                if nxt:
                    ln_c(i + 1)
                if cur:
                    ln_d(i)
                if nxt:
                    add_bias(i + 1)
                if cur:
                    weights(i)

            steps(e, layer1_step)

        @block.scalar
        def _(e):
            def split_chunk_hi(c, half):
                chunk_ready(e, c)
                hi, _, src = chunk_half(c, half)
                e.activation(hi, src, ACT.Copy).then_inc(stage_hi, 1)

            def prep(b):
                wait_ge(e, v_proj, GROUPS * b)
                e.activation(cT[:, 0, :], ctxT[:, b, :], ACT.Copy).then_inc(c_hi, 1)
                e.wait_ge(xt_done, b + 1)
                e.activation(xaT[:, 0, :], tk_bank[:, 0:D], ACT.Copy).then_inc(xt_hi, 1)

            e.dma_start(pos[:, :, :], io["pos"].rearrange("b p a -> p b a")).then_inc(pos_in, 16)
            e.dma_start(gains[:, 0:1], io["gq"].rearrange("(p a) -> p a", a=1)).then_inc(small_in, 16)
            e.dma_start(gains[:, 1:2], io["gk"].rearrange("(p a) -> p a", a=1)).then_inc(small_in, 16)
            e.dma_start(gates[:, 0:2], io["g_xattn"].rearrange("(a n) -> a n", a=1).to_broadcast([P, 2]))\
             .then_inc(small_in, 16)
            e.dma_start(gates[:, 2:4], io["g_ffn"].rearrange("(a n) -> a n", a=1).to_broadcast([P, 2]))\
             .then_inc(small_in, 16)
            e.dma_start(btg[:, :], io["bout"].rearrange("(a n) -> a n", a=1).to_broadcast([P, D])).then_inc(pos_in, 32)
            e.wait_ge(small_in, 64)
            e.activation(tgates[:, :], gates[:, :], ACT.Tanh).then_inc(gates_done, 1)
            e.wait_ge(ang_done, 1)
            e.activation(trig[:, :, :, :, :], ang[:, :, :, :, :], ACT.Sin).then_inc(trig_done, 1)
            e.wait_ge(ctx_in, 16)
            prep(0)
            split_chunk_hi(0, 0)
            split_chunk_hi(0, 1)

            def square_q(b, g):
                t = GROUPS * b + g
                e.wait_ge(q_proj, t + 1)
                wait_ge(e, tq_done, t)
                e.activation(Qs[:, :, :], q_bank[:, :].rearrange("p (h d) -> p h d", h=HG), ACT.Square)\
                 .then_inc(sq_done, 1)

            def square_k(b, g):
                t = GROUPS * b + g
                e.wait_ge(k_proj, t + 1)
                wait_ge(e, tk_done, t)
                e.activation(Ks[:, :, :], k_bank[:, :].rearrange("p (h d) -> p h d", h=HG), ACT.Square)\
                 .then_inc(sq_done, 1)

            def save_v(b, g):
                t = GROUPS * b + g
                e.wait_ge(v_proj, t + 1)
                wait_ge(e, o_done, t - 3)
                e.activation(V[:, g, :], v_bank[:, :], ACT.Copy).then_inc(v_saved, 1)

            def split_hi0(b, c, half):
                if is_step(b, 0):
                    split_chunk_hi(c, half)

            def out_hi(b, g):
                u = GROUPS * b + g
                e.wait_ge(o_done, u + 1)
                wait_ge(e, w_done, u - 1)
                e.activation(OTh[:, g % 2, :], o_bank[:, :], ACT.Copy).then_inc(o_hi, 1)

            def exponentials(b, g):
                e.wait_ge(sub_done, GROUPS * b + g + 1)
                e.activation(Pr[:, :, :], Pr[:, :, :], ACT.Exp, scale=float(P) ** 0.5).then_inc(exp_done, 1)

            def tanh_up(b, half):
                if half == 0 and is_step(b, 0):
                    e.wait_ge(wscale_done, 1)
                e.wait_ge(up_done, 2 * b + half + 1)
                wait_ge(e, ht_done, 2 * b + half - 1)
                e.activation(H[:, half, :], v_bank[:, :], ACT.Tanh, scale=half_up[:, 0:1]).then_inc(tanh_done, 1)

            def save_qt(b, g):
                t = GROUPS * b + g
                e.wait_ge(tq_done, t + 1)
                wait_ge(e, s_done, t - 1)
                e.activation(QT[:, g % 2, :], tq_bank[:, :], ACT.Copy).then_inc(qt_saved, 1)

            def save_kt(b, g):
                t = GROUPS * b + g
                e.wait_ge(tk_done, t + 1)
                wait_ge(e, s_done, t - 1)
                if is_step(b, 0) and g == 0:
                    e.wait_ge(gains_done, 1)
                e.activation(KTr[:, g % 2, :], tk_bank[:, :], ACT.Copy, scale=gqk[:, 0:1]).then_inc(kt_saved, 1)

            def hidden_hi(b, half):
                e.wait_ge(ht_done, 2 * b + half + 1)
                wait_ge(e, down_done, b)
                e.activation(HTh[:, half, :], tk_bank[:, :], ACT.Copy).then_inc(ht_hi, 1)

            def ffn_in_hi(b):
                e.wait_ge(ft_done, b + 1)
                wait_ge(e, gate_done, 2 * b)
                e.activation(xfT[:, 0, :], tk_bank[:, 0:D], ACT.Copy).then_inc(ft_hi, 1)

            def split_hi(b, n):
                if is_step(b, B + (n > 0)):
                    if n == 0:
                        e.wait_ge(v_proj, SLOTS)
                    if n == EX // 2 + 1:
                        e.wait_ge(w_done, SLOTS)
                    chunk_ready(e, CHUNKS + n)
                    hi, lo, src = layer1_chunk(n)
                    e.activation(hi, src, ACT.Copy).then_inc(stage_hi, 1)

            def c_ctx(b):
                wait_ge(e, qkv_done, b)
                e.activation(cT[:, 0, :], ctxT[:, b, :], ACT.Copy).then_inc(c_chi, 1)

            def c_inputs(b):
                e.wait_ge(c_turned, b + 1)
                e.activation(xaT[:, 0, :], m1[:, 0:D], ACT.Copy).then_inc(c_xhi, 1)

            def c_save(b):
                e.wait_ge(qkv_done, b + 1)
                wait_ge(e, ot2_done, b - 1)
                e.activation(qk[:, 0:D], m1[:, D:2 * D], ACT.Copy)
                e.activation(qk[:, D:2 * D], m2[:, 0:D], ACT.Copy).then_inc(qk_saved, 1)
                e.activation(Vn[:, :], m2[:, D:2 * D], ACT.Copy).then_inc(vn_saved, 1)

            def move_v(b):
                e.wait_ge(vn_saved, b + 1)
                wait_ge(e, av_done, SG * b)
                e.activation(Va[:, :, 0:D1], Vn[:, :].rearrange("p (h d) -> p h d", h=H1), ACT.Copy).then_inc(va_done, 1)

            def c_stack(b):
                r3 = rot.rearrange("p (s h d) -> p s h d", s=2, d=D1)
                e.wait_ge(rope_done, b + 1)
                if is_step(b, 0):
                    e.wait_ge(o_done, SLOTS)
                wait_ge(e, t2_done, b)
                two = [P, H1, 2, D1]
                e.activation(SQ[:, :, 0:2, :], r3[:, 0].unsqueeze(2).to_broadcast(two), ACT.Copy).then_inc(stack_hi, 1)
                e.activation(SK[:, :, 0:3:2, :], r3[:, 1].unsqueeze(2).to_broadcast(two), ACT.Copy)\
                 .then_inc(stack_hi, 1)

            def t1k_save(b):
                e.wait_ge(t1_done, b + 1)
                wait_ge(e, st_done, SG * b)
                e.activation(KT1.rearrange("p t q -> p (t q)"), m2[:, :].bitcast(F16), ACT.Copy)\
                 .then_inc(t1k_saved, 1)

            def exp_group(b, j):
                e.wait_ge(st_done, SG * b + j + 1)
                wait_ge(e, av_done, SG * b + j - 3)
                e.activation(E2[:, j % 4, :], s_banks[j % 2][:, :], ACT.Exp, scale=float(D1) ** -0.5)\
                 .then_inc(e_done, 1)

            def ot2_save(b):
                e.wait_ge(ot2_done, b + 1)
                e.activation(OT2[0], m1[:, 0:D], ACT.Copy).then_inc(ot2_hi, 1)

            def d_inputs(b):
                e.wait_ge(d_turned, b + 1)
                wait_ge(e, u2_done, 4 * b)
                e.activation(xfT[:, 0, :], m1[:, 0:D], ACT.Copy).then_inc(d_xhi, 1)

            def route(b):
                e.wait_ge(route_step, 7 * b + 5)
                e.activation(rw[:, 1:2], gap[:, :], ACT.Exp).then_inc(gap_exp, 1)

            def tanh_chunk(b, c):
                n = 4 * b + c
                e.wait_ge(g2_done, n + 1)
                if is_step(b, 0) and c == 0:
                    e.wait_ge(stage_lo, 2 * TERN + L1_CHUNKS)
                if c == 3:
                    wait_ge(e, h2t_done, 4 * b)
                else:
                    wait_ge(e, h2t_done, 4 * (b - 1) + c + 2)
                e.activation(H2[:, c * 2 * CH:(c + 1) * 2 * CH], g_bank[:, 0:2 * CH], ACT.Tanh, scale=0.5)\
                 .then_inc(g_tanh, 1)

            def ht_hi2(b, c):
                a, z = CHUNK_TILES[c]
                e.wait_ge(h2t_done, 4 * b + c + 1)
                wait_ge(e, dn_done, b)
                e.activation(HT2[0][:, a * P:z * P], m3[:, 0:(z - a) * P], ACT.Copy).then_inc(h2t_hi, 1)
            def layer0_step(i, cur, prv, old, nxt):
                if cur:
                    square_q(i, 0)
                    square_k(i, 0)
                if prv:
                    exponentials(i - 1, 3)
                split_hi(i, 0)
                if cur:
                    save_v(i, 0)
                if is_step(i, B):
                    c_ctx(0)
                if cur:
                    split_hi0(i, 1, 0)
                if prv:
                    out_hi(i - 1, 2)
                if is_step(i, B):
                    c_inputs(0)
                if cur:
                    split_hi0(i, 1, 1)
                    save_qt(i, 0)
                    split_hi0(i, 2, 0)
                    save_kt(i, 0)
                if old:
                    tanh_up(i - 2, 1)
                if is_step(i, B):
                    c_save(0)
                if is_step(i, B + 1):
                    exp_group(0, 0)
                if cur:
                    split_hi0(i, 2, 1)
                if is_step(i, B + 1):
                    c_ctx(1)
                    exp_group(0, 1)
                    exp_group(0, 2)
                if old:
                    hidden_hi(i - 2, 0)
                if cur:
                    square_q(i, 1)
                    square_k(i, 1)
                    save_v(i, 1)
                    exponentials(i, 0)
                if prv:
                    out_hi(i - 1, 3)
                if is_step(i, B):
                    c_stack(0)
                if cur:
                    split_hi0(i, 3, 0)
                    split_hi0(i, 3, 1)
                if is_step(i, B):
                    move_v(0)
                if cur:
                    save_kt(i, 1)
                    save_qt(i, 1)
                if old:
                    hidden_hi(i - 2, 1)
                if is_step(i, B):
                    t1k_save(0)
                if cur:
                    split_hi0(i, 4, 0)
                    square_q(i, 2)
                    square_k(i, 2)
                    exponentials(i, 1)
                    save_v(i, 2)
                    split_hi0(i, 4, 1)
                    out_hi(i, 0)
                    save_kt(i, 2)
                    save_qt(i, 2)
                    split_hi0(i, 5, 0)
                if prv:
                    ffn_in_hi(i - 1)
                if cur:
                    square_q(i, 3)
                    square_k(i, 3)
                if nxt:
                    prep(i + 1)
                if cur:
                    save_v(i, 3)
                    exponentials(i, 2)
                if is_step(i, B + 1):
                    exp_group(0, 3)
                if cur:
                    out_hi(i, 1)
                    save_qt(i, 3)
                    split_hi0(i, 5, 1)
                if is_step(i, B + 1):
                    exp_group(0, 4)
                if cur:
                    save_kt(i, 3)
                split_hi(i, 1)
                if is_step(i, B + 1):
                    exp_group(0, 5)
                split_hi(i, 2)
                if is_step(i, B + 1):
                    c_inputs(1)
                split_hi(i, 3)
                if prv:
                    tanh_up(i - 1, 0)
                if is_step(i, B + 1):
                    exp_group(0, 6)
                    c_save(1)
                    exp_group(0, 7)
                    c_stack(1)
                    move_v(1)
                    t1k_save(1)
                    ot2_save(0)
                    d_inputs(0)
                    route(0)
                split_hi(i, 4)
                split_hi(i, 5)
                split_hi(i, 6)

            batches(e, layer0_step)

            def layer1_step(i, cur, prv, nxt):
                if nxt:
                    c_ctx(i + 1)
                if cur:
                    exp_group(i, 0)
                if prv:
                    tanh_chunk(i - 1, 0)
                if cur:
                    exp_group(i, 1)
                    exp_group(i, 2)
                    exp_group(i, 3)
                    exp_group(i, 4)
                if prv:
                    tanh_chunk(i - 1, 1)
                if nxt:
                    c_inputs(i + 1)
                if cur:
                    exp_group(i, 5)
                    exp_group(i, 6)
                if nxt:
                    c_save(i + 1)
                if prv:
                    ht_hi2(i - 1, 0)
                if cur:
                    exp_group(i, 7)
                if prv:
                    tanh_chunk(i - 1, 2)
                if nxt:
                    c_stack(i + 1)
                    move_v(i + 1)
                if prv:
                    ht_hi2(i - 1, 1)
                    tanh_chunk(i - 1, 3)
                if nxt:
                    t1k_save(i + 1)
                if cur:
                    ot2_save(i)
                if prv:
                    ht_hi2(i - 1, 2)
                    ht_hi2(i - 1, 3)
                if cur:
                    d_inputs(i)
                    route(i)

            steps(e, layer1_step)

        @block.vector
        def _(e):
            def split_chunk_lo(c, half):
                e.wait_ge(stage_hi, 2 * c + half + 1)
                hi, lo, src = chunk_half(c, half)
                e.tensor_tensor(lo, src, hi.bitcast(F32), ALU.subtract).then_inc(stage_lo, 1)

            def abs_sum(b, n):
                if is_step(b, 1):
                    chunk_ready(e, TERN + n)
                    e.tensor_reduce(wsum[:, n:n + 1], stage[:, (TERN + n) % 2, :], AX.X, ALU.add,
                                    apply_absolute_value=True).then_inc(wsum_done, 1)

            def scale(b, n):
                if is_step(b, 1):
                    e.wait_ge(wtot_done, n + 1)
                    e.tensor_scalar(wscale[:, n:n + 1], y_sum[:, n:n + 1], 1.0 / (4 * BANK * P), 1e-8,
                                    ALU.mult, ALU.add).then_inc(low_done, 1)
                    e.wait_ge(low_done, 5 * n + 1)
                    e.tensor_scalar(th[:, n:n + 1], wscale[:, n:n + 1], 0.5, None, ALU.mult).then_inc(low_done, 1)
                    e.tensor_scalar(nth[:, n:n + 1], wscale[:, n:n + 1], -0.5, None, ALU.mult).then_inc(low_done, 1)

            def signs(b, n, half):
                if is_step(b, 1):
                    cols = slice(half * 2 * BANK, (half + 1) * 2 * BANK)
                    w, t = stage[:, (TERN + n) % 2, cols], T[:, n, cols]
                    e.wait_ge(low_done, 5 * n + 3)
                    e.tensor_scalar(t, w, nth[:, n:n + 1], None, ALU.is_lt).then_inc(low_done, 1)
                    e.wait_ge(low_done, 5 * n + 4 + half)
                    e.scalar_tensor_tensor(out=t, in0=w, scalar=th[:, n:n + 1], in1=t.bitcast(F32),
                                           op0=ALU.is_gt, op1=ALU.subtract).then_inc(sign_done, 1)

            y_sum = v_bank[:, D:D + 3]

            def ln_stats(b, n, stats_sem, aggr_sem, src):
                wait_ge(e, (rstd_done, frstd_done)[n], b)
                e.sem_inc(waits_passed, 1)
                e.bn_stats(stats[:, n, :], src).then_inc(stats_sem, 1)
                e.wait_ge(stats_sem, b + 1)
                e.sem_inc(waits_passed, 1)
                e.bn_aggr(mv[:, n, :], stats[:, n, :]).then_inc(aggr_sem, 1)

            def ln_apply(b, n, rstd_sem, done, src, turned):
                e.wait_ge(rstd_sem, b + 1)
                wait_ge(e, turned, b)
                e.tensor_scalar(xn[:, n, :], src, mv[:, n, 0:1], rstd[:, n:n + 1], ALU.subtract, ALU.mult)\
                 .then_inc(done, 1)

            def prep(b):
                e.wait_ge(c_hi, b + 1)
                e.tensor_tensor(cT[:, 1, :], ctxT[:, b, :], cT[:, 0, :].bitcast(F32), ALU.subtract)\
                 .then_inc(c_lo, 1)
                e.wait_ge(xt_hi, b + 1)
                e.tensor_tensor(xaT[:, 1, :], tk_bank[:, 0:D], xaT[:, 0, :].bitcast(F32), ALU.subtract)\
                 .then_inc(xt_lo, 1)

            def angles():
                n = [0]
                def step(ins):
                    n[0] += 1
                    ins.then_inc(ang_step, 1)
                    e.wait_ge(ang_step, n[0])
                e.wait_ge(pos_in, 48)
                e.wait_ge(gates_done, 1)
                step(e.tensor_tensor(btg[:, :], btg[:, :], tgates[:, 1:2].to_broadcast([P, D]), ALU.mult))
                for f in range(2):
                    step(e.tensor_scalar(ang[:, 0, :, :, f], pos[:, :, :], 10000.0 ** (-f / 2.0), None, ALU.mult))
                step(e.tensor_scalar(ang[:, 1], ang[:, 0], math.pi / 2, None, ALU.add))
                step(e.tensor_scalar(turns[:, :], ang_flat, 1 / (2 * math.pi), 1.5 * 2 ** 23, ALU.mult, ALU.add))
                step(e.tensor_scalar(turns[:, :], turns[:, :], 1.5 * 2 ** 23, None, ALU.subtract))
                step(e.scalar_tensor_tensor(out=ang_flat, in0=turns[:, :], scalar=-6.28125, in1=ang_flat,
                                            op0=ALU.mult, op1=ALU.add))
                step(e.scalar_tensor_tensor(out=ang_flat, in0=turns[:, :], scalar=-(2 * math.pi - 6.28125),
                                            in1=ang_flat, op0=ALU.mult, op1=ALU.add))
                e.tensor_scalar(ang_flat, ang_flat, 3.1415925, -3.1415925, ALU.min, ALU.max).then_inc(ang_done, 1)
                e.wait_ge(trig_done, 1)
                four = [P, B, 4]
                s3, c3 = (trig[:, k].rearrange("p b s f -> p b (s f)") for k in (0, 1))
                s8, c8 = (t.rearrange("p b (f c) -> p b f c", c=2) for t in (sin8[:, :, :], cos8[:, :, :]))
                step(e.tensor_copy(c8[:, :, :, 0], c3))
                step(e.tensor_copy(c8[:, :, :, 1], c3))
                step(e.tensor_copy(s8[:, :, :, 1], s3))
                step(e.tensor_scalar(s8[:, :, :, 0], s3, -1.0, None, ALU.mult))

            e.wait_ge(x_in[0], 16)
            ln_stats(0, 0, stats_done, aggr_done, X[:, 0, :])
            e.wait_ge(small_in, 64)
            e.tensor_tensor(gqk[:, :], gains[:, 0:1], gains[:, 1:2], ALU.mult).then_inc(gains_done, 1)
            ln_apply(0, 0, rstd_done, xn_done, X[:, 0, :], xt_done)
            angles()
            prep(0)
            split_chunk_lo(0, 0)
            split_chunk_lo(0, 1)

            def attn_residual(b):
                e.wait_ge(w_done, GROUPS * b + GROUPS)
                e.scalar_tensor_tensor(out=X[:, b, :], in0=y_bank[:, 0:D], scalar=tgates[:, 0:1],
                                       in1=X[:, b, :], op0=ALU.mult, op1=ALU.add).then_inc(res_done, 1)
                e.wait_ge(res_done, b + 1)
                ln_stats(b, 1, fstats_done, faggr_done, X[:, b, :])

            def sum_q(b, g):
                t = GROUPS * b + g
                wait_ge(e, rs_done, 2 * t - 1)
                e.wait_ge(sq_done, 2 * t + 1)
                e.tensor_reduce(ss[:, 0:HG], Qs[:, :, :], AX.X, ALU.add).then_inc(ss_done, 1)

            def sum_k(b, g):
                wait_ge(e, rs_done, 2 * (GROUPS * b + g))
                e.wait_ge(sq_done, 2 * (GROUPS * b + g) + 2)
                e.tensor_reduce(ss[:, HG:2 * HG], Ks[:, :, :], AX.X, ALU.add).then_inc(ss_done, 1)

            def split_lo0(b, c, half):
                if is_step(b, 0):
                    split_chunk_lo(c, half)

            def ffn_norm(b):
                ln_apply(b, 1, frstd_done, fxn_done, X[:, b, :], ft_done)

            def shift_scores(b, g):
                u = GROUPS * b + g
                sc = s_bank[:, :].rearrange("p (h k) -> p h k", h=HG)
                e.wait_ge(s_done, u + 1)
                e.tensor_reduce(mx[:, :], sc, AX.X, ALU.max).then_inc(mx_done, 1)
                e.wait_ge(mx_done, u + 1)
                wait_ge(e, pt_done, u)
                e.tensor_tensor(Pr[:, :, :], sc, mx[:, :].unsqueeze(2).to_broadcast([P, HG, P]),
                                ALU.subtract).then_inc(sub_done, 1)

            def scale_q(b, g):
                e.wait_ge(rs_done, 2 * (GROUPS * b + g) + 1)
                e.tensor_tensor(Qs[:, :, :], q_bank[:, :].rearrange("p (h d) -> p h d", h=HG),
                                rs[:, 0:HG].unsqueeze(2).to_broadcast([P, HG, P]), ALU.mult).then_inc(q_scaled, 1)

            def scale_k(b, g):
                e.wait_ge(rs_done, 2 * (GROUPS * b + g) + 2)
                e.tensor_tensor(Ks[:, :, :], k_bank[:, :].rearrange("p (h d) -> p h d", h=HG),
                                rs[:, HG:2 * HG].unsqueeze(2).to_broadcast([P, HG, P]), ALU.mult)\
                 .then_inc(k_scaled, 1)

            def out_lo(b, g):
                e.wait_ge(o_hi, GROUPS * b + g + 1)
                e.tensor_tensor(OTl[:, g % 2, :], o_bank[:, :], OTh[:, g % 2, :].bitcast(F32),
                                ALU.subtract).then_inc(o_lo, 1)

            def row_sums(b, g):
                u = GROUPS * b + g
                e.wait_ge(exp_done, u + 1)
                e.tensor_reduce(rsum[:, :], Pr[:, :, :], AX.X, ALU.add).then_inc(sum_done, 1)
                e.wait_ge(sum_done, u + 1)
                wait_ge(e, norm_done, u)
                e.reciprocal(rinv[:, :], rsum[:, :]).then_inc(rinv_done, 1)

            def next_stats(b):
                if is_step(b, 1):
                    e.wait_ge(x_in[1], 16)
                ln_stats(b, 0, stats_done, aggr_done, X[:, b, :])

            def next_norm(b):
                ln_apply(b, 0, rstd_done, xn_done, X[:, b, :], xt_done)

            def scales(b):
                if is_step(b, 1):
                    e.wait_ge(low_done, 11)
                    e.tensor_scalar(half_up[:, :], wscale[:, 0:1], 0.5, None, ALU.mult).then_inc(wscale_done, 1)
                    e.tensor_tensor(ffn_scale[:, 0:1], wscale[:, 1:2], wscale[:, 2:3], ALU.mult)\
                     .then_inc(wscale_done, 1)
                    e.wait_ge(wscale_done, 2)
                    e.scalar_tensor_tensor(out=ffn_scale[:, 0:1], in0=ffn_scale[:, 0:1], scalar=half_up[:, 0:1],
                                           in1=tgates[:, 2:3], op0=ALU.mult, op1=ALU.mult)\
                     .then_inc(wscale_done, 1)

            def act_up(b, half):
                n = 2 * b + half
                e.wait_ge(tanh_done, n + 1)
                e.scalar_tensor_tensor(out=H[:, half, :], in0=H[:, half, :], scalar=1.0, in1=v_bank[:, :],
                                       op0=ALU.add, op1=ALU.mult).then_inc(act_done, 1)

            def times_gate(b, half):
                n = 2 * b + half
                e.wait_ge(act_done, n + 1)
                e.wait_ge(gate_done, n + 1)
                e.tensor_tensor(H[:, half, :], H[:, half, :], s_bank[:, :], ALU.mult).then_inc(hid_done, 1)

            def ffn_residual(b):
                e.wait_ge(down_done, b + 1)
                if is_step(b, 0):
                    e.wait_ge(wscale_done, 3)
                e.scalar_tensor_tensor(out=X[:, b, :], in0=v_bank[:, 0:D], scalar=ffn_scale[:, 0:1],
                                       in1=X[:, b, :], op0=ALU.mult, op1=ALU.add).then_inc(fres_done, 1)

            def save_pt(b, g):
                e.wait_ge(pt_done, GROUPS * b + g + 1)
                wait_ge(e, o_done, GROUPS * b + g)
                e.tensor_copy(PT[:, :], tq_bank[:, :]).then_inc(pt_saved, 1)

            def hidden_lo(b, half):
                e.wait_ge(ht_hi, 2 * b + half + 1)
                e.tensor_tensor(HTl[:, half, :], tk_bank[:, :], HTh[:, half, :].bitcast(F32),
                                ALU.subtract).then_inc(ht_lo, 1)

            def ffn_in_lo(b):
                e.wait_ge(ft_hi, b + 1)
                e.tensor_tensor(xfT[:, 1, :], tk_bank[:, 0:D], xfT[:, 0, :].bitcast(F32), ALU.subtract)\
                 .then_inc(ft_lo, 1)

            def split_lo(b, n):
                if is_step(b, B + (n > 0)):
                    e.wait_ge(stage_hi, 2 * TERN + n + 1)
                    hi, lo, src = layer1_chunk(n)
                    e.tensor_tensor(lo, src, hi.bitcast(F32), ALU.subtract).then_inc(stage_lo, 1)

            def lnc_stats(b):
                wait_ge(e, c_rstd, b)
                e.sem_inc(waits_passed, 1)
                e.bn_stats(stats[:, 0, :], X[:, b, :]).then_inc(c_stats, 1)
                e.wait_ge(c_stats, b + 1)
                e.sem_inc(waits_passed, 1)
                e.bn_aggr(mv[:, 0, :], stats[:, 0, :]).then_inc(c_aggr, 1)

            def c_norm(b):
                e.wait_ge(c_rstd, b + 1)
                wait_ge(e, c_turned, b)
                e.tensor_scalar(xn[:, 0, :], X[:, b, :], mv[:, 0, 0:1], rstd[:, 0:1], ALU.subtract, ALU.mult)\
                 .then_inc(c_xn, 1)
                e.wait_ge(c_chi, b + 1)
                e.tensor_tensor(cT[:, 1, :], ctxT[:, b, :], cT[:, 0, :].bitcast(F32), ALU.subtract)\
                 .then_inc(c_clo, 1)

            def c_inputs(b):
                e.wait_ge(c_xhi, b + 1)
                e.tensor_tensor(xaT[:, 1, :], m1[:, 0:D], xaT[:, 0, :].bitcast(F32), ALU.subtract)\
                 .then_inc(c_xlo, 1)

            def rope(b):
                four = [P, 2 * H1, 4]
                x = qk.rearrange("p (h f c) -> p h f c", h=2 * H1, c=2)
                r = rot.rearrange("p (h f c) -> p h f c", h=2 * H1, c=2)
                s_ = sin8[:, b, :].rearrange("p (f c) -> p f c", c=2)
                e.wait_ge(qk_saved, b + 1)
                e.tensor_tensor(r[:, :, :, 0], x[:, :, :, 1],
                                s_[:, :, 0].unsqueeze(1).to_broadcast(four), ALU.mult).then_inc(rope_a, 1)
                e.tensor_tensor(r[:, :, :, 1], x[:, :, :, 0],
                                s_[:, :, 1].unsqueeze(1).to_broadcast(four), ALU.mult).then_inc(rope_a, 1)
                e.wait_ge(rope_a, 2 * b + 2)
                q3 = qk.rearrange("p (h d) -> p h d", d=D1)
                e.tensor_tensor(q3, q3, cos8[:, b, :].unsqueeze(1).to_broadcast([P, 2 * H1, D1]), ALU.mult)\
                 .then_inc(rope_b, 1)
                e.wait_ge(rope_b, b + 1)
                e.tensor_tensor(rot, rot, qk, ALU.add).then_inc(rope_done, 1)

            def stack_los(b):
                r3 = rot.rearrange("p (s h d) -> p s h d", s=2, d=D1)
                e.wait_ge(stack_hi, 2 * b + 2)
                e.tensor_tensor(SQ[:, :, 2, :], r3[:, 0], SQ[:, :, 0, :], ALU.subtract).then_inc(stack_lo, 1)
                e.tensor_tensor(SK[:, :, 1, :], r3[:, 1], SK[:, :, 0, :], ALU.subtract).then_inc(stack_lo, 1)

            def t1q_save(b):
                e.wait_ge(t1_done, b + 1)
                e.tensor_copy(QT1.rearrange("p t q -> p (t q)"), m1[:, :].bitcast(F16)).then_inc(t1q_saved, 1)

            def max_group(b, j):
                e.wait_ge(sc_done, SG * b + j + 1)
                if j == 0:
                    wait_ge(e, m_split, 4 * b)
                a = (j // HG) * HG * HG + j % HG
                e.tensor_reduce(Mx[:, a:a + HG * (HG - 1) + 1:HG], s_banks[j % 2][:, :]
                                .rearrange("p (h k) -> p h k", h=HG), AX.X, ALU.max).then_inc(smax_done, 1)

            def split_max(b):
                e.wait_ge(smax_done, SG * b + SG)
                e.tensor_scalar(SQ[:, :, 3, 0], Mx[:, :], 1.0 / 64, None, ALU.mult).then_inc(m_split, 1)
                e.wait_ge(m_split, 4 * b + 1)
                e.scalar_tensor_tensor(out=Mr[:, :], in0=Mx[:, :], scalar=1.0 / 64, in1=SQ[:, :, 3, 0],
                                       op0=ALU.mult, op1=ALU.subtract).then_inc(m_split, 1)
                e.wait_ge(m_split, 4 * b + 2)
                e.tensor_copy(SQ[:, :, 3, 1], Mr[:, :]).then_inc(m_split, 1)
                e.wait_ge(m_split, 4 * b + 3)
                e.tensor_tensor(SQ[:, :, 3, 2], Mr[:, :], SQ[:, :, 3, 1], ALU.subtract).then_inc(m_split, 1)

            def t2_save(b):
                e.wait_ge(t2_done, b + 1)
                wait_ge(e, st_done, SG * b)
                e.tensor_copy(QT2.rearrange("p t q -> p (t q)"), m2[:, :].bitcast(F16)).then_inc(t2_saved, 1)

            def attn_norm(b):
                e.wait_ge(av_done, SG * b + SG)
                ov = ov_bank[:, 0:9 * H1].rearrange("p (h c) -> p h c", h=H1)
                e.reciprocal(rz[:, :], ov[:, :, D1]).then_inc(rz_done, 1)
                e.wait_ge(rz_done, b + 1)
                wait_ge(e, ot2_done, b)
                e.tensor_tensor(On.rearrange("p (h c) -> p h c", h=H1), ov[:, :, 0:D1],
                                rz[:, :].unsqueeze(2).to_broadcast([P, H1, D1]), ALU.mult).then_inc(on_done, 1)

            def attn_out(b):
                e.wait_ge(ot2_hi, b + 1)
                e.tensor_tensor(OT2[1], m1[:, 0:D], OT2[0].bitcast(F32), ALU.subtract).then_inc(ot2_lo, 1)

            def residual(b):
                e.wait_ge(w2_done, b + 1)
                e.wait_ge(bias_added, b + 1)
                e.scalar_tensor_tensor(out=X[:, b, :], in0=m1[:, D:2 * D], scalar=tgates[:, 1:2],
                                       in1=X[:, b, :], op0=ALU.mult, op1=ALU.add).then_inc(cres_done, 1)
                e.wait_ge(cres_done, b + 1)
                wait_ge(e, d_rstd, b)
                e.sem_inc(waits_passed, 1)
                e.bn_stats(stats[:, 1, :], X[:, b, :]).then_inc(d_stats, 1)
                e.wait_ge(d_stats, b + 1)
                e.sem_inc(waits_passed, 1)
                e.bn_aggr(mv[:, 1, :], stats[:, 1, :]).then_inc(d_aggr, 1)

            def d_norm(b):
                e.wait_ge(d_rstd, b + 1)
                wait_ge(e, d_turned, b)
                e.tensor_scalar(xn[:, 1, :], X[:, b, :], mv[:, 1, 0:1], rstd[:, 1:2], ALU.subtract, ALU.mult)\
                 .then_inc(d_xn, 1)

            def d_inputs(b):
                e.wait_ge(d_xhi, b + 1)
                e.tensor_tensor(xfT[:, 1, :], m1[:, 0:D], xfT[:, 0, :].bitcast(F32), ALU.subtract)\
                 .then_inc(d_xlo, 1)

            def winners(b):
                n = 7 * b
                e.wait_ge(route_done, b + 1)
                e.tensor_copy(lg[:, :], m1[:, D:D + EX]).then_inc(route_step, 1)
                e.wait_ge(route_step, n + 1)
                e.sem_inc(waits_passed, 1)
                e.max(top[:, :], lg[:, :]).then_inc(route_step, 1)
                e.wait_ge(route_step, n + 2)
                e.sem_inc(waits_passed, 1)
                e.max_index(topi[:, :], top[:, :], lg[:, :]).then_inc(route_step, 1)
                e.wait_ge(route_step, n + 3)
                e.tensor_copy(topf[:, :], topi[:, 0:2]).then_inc(route_step, 1)
                e.tensor_tensor(gap[:, :], top[:, 1:2], top[:, 0:1], ALU.subtract).then_inc(route_step, 1)

            def first_weight(b):
                e.wait_ge(gap_exp, b + 1)
                e.tensor_scalar(rw[:, 2:3], rw[:, 1:2], 1.0, 2.0, ALU.add, ALU.mult).then_inc(route_step, 1)
                e.wait_ge(route_step, 7 * b + 6)
                e.reciprocal(rw[:, 3:4], rw[:, 2:3]).then_inc(route_step, 1)

            def hidden(b, c):
                cols = slice(c * 2 * CH, (c + 1) * 2 * CH)
                n = 4 * b + c
                e.wait_ge(g_tanh, n + 1)
                e.scalar_tensor_tensor(out=H2[:, cols], in0=H2[:, cols], scalar=1.0, in1=g_bank[:, 0:2 * CH],
                                       op0=ALU.add, op1=ALU.mult).then_inc(g_act, 1)
                e.wait_ge(g_act, n + 1)
                e.wait_ge(u2_done, n + 1)
                if c == 0:
                    e.wait_ge(wte_step, 5 * b + 5)
                for k in range(2):
                    one = slice((2 * c + k) * CH, (2 * c + k + 1) * CH)
                    ins = e.scalar_tensor_tensor(out=H2[:, one], in0=H2[:, one], scalar=w_te[:, 2 * c + k:2 * c + k + 1],
                                                 in1=u_bank[:, k * CH:(k + 1) * CH], op0=ALU.mult, op1=ALU.mult)
                ins.then_inc(h2_done, 1)

            def ht_lo2(b, c):
                a, z = CHUNK_TILES[c]
                e.wait_ge(h2t_hi, 4 * b + c + 1)
                e.tensor_tensor(HT2[1][:, a * P:z * P], m3[:, 0:(z - a) * P], HT2[0][:, a * P:z * P].bitcast(F32),
                                ALU.subtract).then_inc(h2t_lo, 1)

            def d_out(b):
                e.wait_ge(dn_done, b + 1)
                e.scalar_tensor_tensor(out=X[:, b, :], in0=g_bank[:, 0:D], scalar=tgates[:, 3:4],
                                       in1=X[:, b, :], op0=ALU.mult, op1=ALU.add).then_inc(dres_done, 1)
            def layer0_step(i, cur, prv, old, nxt):
                if cur:
                    sum_q(i, 0)
                    sum_k(i, 0)
                if prv:
                    shift_scores(i - 1, 3)
                if is_step(i, B):
                    lnc_stats(0)
                if cur:
                    scale_q(i, 0)
                    scale_k(i, 0)
                if prv:
                    row_sums(i - 1, 3)
                    out_lo(i - 1, 2)
                if is_step(i, B):
                    c_norm(0)
                split_lo(i, 0)
                if is_step(i, B):
                    c_inputs(0)
                if old:
                    act_up(i - 2, 1)
                if cur:
                    split_lo0(i, 1, 0)
                    split_lo0(i, 1, 1)
                    split_lo0(i, 2, 0)
                    split_lo0(i, 2, 1)
                    abs_sum(i, 0)
                if is_step(i, B + 1):
                    lnc_stats(1)
                    c_norm(1)
                if old:
                    times_gate(i - 2, 1)
                if cur:
                    scale(i, 0)
                    signs(i, 0, 0)
                    signs(i, 0, 1)
                if prv:
                    save_pt(i - 1, 3)
                if is_step(i, B):
                    rope(0)
                if old:
                    hidden_lo(i - 2, 0)
                if cur:
                    sum_q(i, 1)
                    sum_k(i, 1)
                    shift_scores(i, 0)
                    scale_q(i, 1)
                    scale_k(i, 1)
                if is_step(i, B):
                    stack_los(0)
                if cur:
                    row_sums(i, 0)
                if nxt:
                    next_stats(i + 1)
                if cur:
                    abs_sum(i, 1)
                if prv:
                    out_lo(i - 1, 3)
                if cur:
                    split_lo0(i, 3, 0)
                if old:
                    hidden_lo(i - 2, 1)
                if is_step(i, B):
                    t1q_save(0)
                if cur:
                    save_pt(i, 0)
                    scale(i, 1)
                    signs(i, 1, 0)
                    signs(i, 1, 1)
                    split_lo0(i, 3, 1)
                    sum_q(i, 2)
                    sum_k(i, 2)
                    shift_scores(i, 1)
                    scale_q(i, 2)
                    scale_k(i, 2)
                    row_sums(i, 1)
                    split_lo0(i, 4, 0)
                    split_lo0(i, 4, 1)
                if prv:
                    attn_residual(i - 1)
                if old:
                    ffn_residual(i - 2)
                if prv:
                    ffn_norm(i - 1)
                if cur:
                    abs_sum(i, 2)
                if is_step(i, B):
                    max_group(0, 0)
                    max_group(0, 1)
                    max_group(0, 2)
                    max_group(0, 3)
                if nxt:
                    next_norm(i + 1)
                if cur:
                    save_pt(i, 1)
                    scale(i, 2)
                    signs(i, 2, 0)
                    signs(i, 2, 1)
                    out_lo(i, 0)
                    scales(i)
                    sum_q(i, 3)
                if is_step(i, B):
                    max_group(0, 4)
                    max_group(0, 5)
                if prv:
                    ffn_in_lo(i - 1)
                if is_step(i, B):
                    max_group(0, 6)
                if cur:
                    sum_k(i, 3)
                if is_step(i, B):
                    max_group(0, 7)
                    split_max(0)
                    t2_save(0)
                if cur:
                    shift_scores(i, 2)
                    scale_q(i, 3)
                    scale_k(i, 3)
                    out_lo(i, 1)
                    row_sums(i, 2)
                if nxt:
                    prep(i + 1)
                if cur:
                    split_lo0(i, 5, 0)
                if prv:
                    act_up(i - 1, 0)
                if cur:
                    split_lo0(i, 5, 1)
                if prv:
                    times_gate(i - 1, 0)
                split_lo(i, 1)
                if is_step(i, B + 1):
                    c_inputs(1)
                split_lo(i, 2)
                if cur:
                    save_pt(i, 2)
                if is_step(i, B + 1):
                    rope(1)
                split_lo(i, 3)
                if is_step(i, B + 1):
                    attn_norm(0)
                    stack_los(1)
                    t1q_save(1)
                    max_group(1, 0)
                    attn_out(0)
                    max_group(1, 1)
                    max_group(1, 2)
                    residual(0)
                    max_group(1, 3)
                    max_group(1, 4)
                    d_norm(0)
                    max_group(1, 5)
                    d_inputs(0)
                    max_group(1, 6)
                    max_group(1, 7)
                    split_max(1)
                    winners(0)
                    first_weight(0)
                split_lo(i, 4)
                if is_step(i, B + 1):
                    t2_save(1)
                split_lo(i, 5)
                split_lo(i, 6)

            batches(e, layer0_step)

            def layer1_step(i, cur, prv, nxt):
                if nxt:
                    lnc_stats(i + 1)
                if prv:
                    hidden(i - 1, 0)
                if nxt:
                    c_norm(i + 1)
                if prv:
                    hidden(i - 1, 1)
                if nxt:
                    c_inputs(i + 1)
                    rope(i + 1)
                if prv:
                    ht_lo2(i - 1, 0)
                    hidden(i - 1, 2)
                if cur:
                    attn_norm(i)
                if nxt:
                    stack_los(i + 1)
                if prv:
                    ht_lo2(i - 1, 1)
                    hidden(i - 1, 3)
                if nxt:
                    t1q_save(i + 1)
                    max_group(i + 1, 0)
                if cur:
                    attn_out(i)
                if nxt:
                    max_group(i + 1, 1)
                if prv:
                    ht_lo2(i - 1, 2)
                if nxt:
                    max_group(i + 1, 2)
                if cur:
                    residual(i)
                if prv:
                    ht_lo2(i - 1, 3)
                if nxt:
                    max_group(i + 1, 3)
                    max_group(i + 1, 4)
                if cur:
                    d_norm(i)
                if nxt:
                    max_group(i + 1, 5)
                if cur:
                    d_inputs(i)
                if nxt:
                    max_group(i + 1, 6)
                    max_group(i + 1, 7)
                if prv:
                    d_out(i - 1)
                if nxt:
                    split_max(i + 1)
                if cur:
                    winners(i)
                if nxt:
                    t2_save(i + 1)
                if cur:
                    first_weight(i)

            steps(e, layer1_step)

        @block.tensor
        def _(e):
            def three(out, lh, ll, rh, rl, start, stop):
                e.matmul(out, lh, rh, start=start, stop=False)
                e.matmul(out, lh, rl, start=False, stop=False)
                return e.matmul(out, ll, rh, start=False, stop=stop)

            def turn(out_bank, src, n, done):
                for k in range(n):
                    ins = e.transpose(out_bank[:, k * P:(k + 1) * P], src(k), ident[:, :])
                ins.then_inc(done, 1)

            def prep(b):
                e.wait_ge(xn_done, b + 1)
                wait_ge(e, kt_saved, GROUPS * b - 1)
                wait_ge(e, ft_lo, b - 1)
                turn(tk_bank, lambda k: xn[:, 0, k * P:(k + 1) * P], KT, xt_done)

            e.wait_ge(consts, 6)
            prep(0)

            def project_q(b, g):
                t = GROUPS * b + g
                if g == 0:
                    e.wait_ge(xt_lo, b + 1)
                if is_step(b, 0):
                    e.wait_ge(stage_lo, 2 * g + 1)
                wait_ge(e, q_scaled, t)
                for kt in range(KT):
                    ins = three(q_bank[:, :], xaT[:, 0, kt * P:(kt + 1) * P], xaT[:, 1, kt * P:(kt + 1) * P],
                                W1h[:, g, kt, :], W1l[:, g, kt, :], kt == 0, kt == KT - 1)
                ins.then_inc(q_proj, 1)

            def project_k(b, g):
                if g == 0:
                    e.wait_ge(c_lo, b + 1)
                if is_step(b, 0):
                    e.wait_ge(stage_lo, 2 * g + 2)
                wait_ge(e, k_scaled, GROUPS * b + g)
                three(k_bank[:, :], cT[:, 0, :], cT[:, 1, :], W1h[:, g, 2, :], W1l[:, g, 2, :], True, True)\
                    .then_inc(k_proj, 1)

            def project_v(b, g):
                wait_ge(e, v_saved, GROUPS * b + g)
                if g == 0:
                    wait_ge(e, act_done, 2 * (b - 2) + 1)
                if g == 1:
                    wait_ge(e, act_done, 2 * (b - 2) + 2)
                if g == 3:
                    wait_ge(e, fres_done, b - 1)
                if is_step(b, 1) and g > 0:
                    e.wait_ge(low_done, 5 * (g - 1) + 1)
                three(v_bank[:, :], cT[:, 0, :], cT[:, 1, :], W1h[:, g, 3, :], W1l[:, g, 3, :], True, True)\
                    .then_inc(v_proj, 1)

            def scores(b, h):
                u = GROUPS * b + h
                e.wait_ge(qt_saved, u + 1)
                e.wait_ge(kt_saved, u + 1)
                wait_ge(e, sub_done, u)
                if h == 3:
                    wait_ge(e, hid_done, 2 * (b - 1) + 1)
                if h == 0:
                    wait_ge(e, hid_done, 2 * (b - 2) + 2)
                for k in range(HG):
                    cols = slice(k * P, (k + 1) * P)
                    ins = e.matmul(s_bank[:, cols], QT[:, h % 2, cols], KTr[:, h % 2, cols],
                                   start=True, stop=True)
                ins.then_inc(s_done, 1)

            def values(b, h):
                u = GROUPS * b + h
                e.wait_ge(pt_saved, u + 1)
                wait_ge(e, o_lo, u)
                for k in range(HG):
                    cols = slice(k * P, (k + 1) * P)
                    ins = e.matmul(o_bank[:, cols], V[:, h, cols], PT[:, cols], start=True, stop=True)
                ins.then_inc(o_done, 1)

            def out_project(b, h):
                u = GROUPS * b + h
                e.wait_ge(o_lo, u + 1)
                if h == 0:
                    wait_ge(e, res_done, b)
                if is_step(b, 0):
                    e.wait_ge(stage_lo, 2 * WO + h + 1)
                for k in range(HG):
                    cols = slice(k * P, (k + 1) * P)
                    ins = three(y_bank[:, 0:D], OTh[:, h % 2, cols], OTl[:, h % 2, cols],
                                Woh[:, h * HG + k, :], Wol[:, h * HG + k, :],
                                h == 0 and k == 0, h == GROUPS - 1 and k == HG - 1)
                ins.then_inc(w_done, 1)

            def ternary_half(b, half, out, m, done):
                for kt in range(KT):
                    w = T[:, m, kt * E0 + half * BANK:kt * E0 + (half + 1) * BANK]
                    for part in range(2):
                        ins = e.matmul(out[:, :], xfT[:, part, kt * P:(kt + 1) * P], w,
                                       start=(kt == 0 and part == 0), stop=(kt == KT - 1 and part == 1))
                ins.then_inc(done, 1)

            def up(b, half):
                e.wait_ge(ft_lo, b + 1)
                if is_step(b, 0):
                    e.wait_ge(sign_done, 2)
                e.wait_ge(v_saved, last(*((b + 1, 3), (b + 2, 0))[half]) + 1)
                wait_ge(e, act_done, 2 * b + half)
                ternary_half(b, half, v_bank, 0, up_done)

            def gate(b, half):
                if is_step(b, 0):
                    e.wait_ge(sign_done, 4)
                t = GROUPS * (b + 1 + half) + (3, 0)[half]
                e.wait_ge(sub_done, min(t, SLOTS) if isinstance(t, int) else t)
                wait_ge(e, hid_done, 2 * b + half)
                ternary_half(b, half, s_bank, 1, gate_done)

            def ffn_down(b):
                e.wait_ge(ht_lo, 2 * b + 2)
                if is_step(b, 0):
                    e.wait_ge(sign_done, 6)
                e.wait_ge(v_saved, last(b + 2, 2) + 1)
                for k in range(ET):
                    cols = slice((k % HG) * P, (k % HG + 1) * P)
                    for part, HT in enumerate((HTh, HTl)):
                        ins = e.matmul(v_bank[:, 0:D], HT[:, k // HG, cols], T[:, 2, k * D:(k + 1) * D],
                                       start=(k == 0 and part == 0), stop=(k == ET - 1 and part == 1))
                ins.then_inc(down_done, 1)

            def sum_weights(b, g):
                if is_step(b, 1):
                    e.wait_ge(wsum_done, g + 1)
                    e.wait_ge(v_saved, GROUPS * b + g + 1)
                    e.matmul(v_bank[:, D + g:D + g + 1], ones[:, :], wsum[:, g:g + 1], start=True, stop=True)\
                     .then_inc(wtot_done, 1)

            def turn_q(b, g):
                t = GROUPS * b + g
                e.wait_ge(q_scaled, t + 1)
                wait_ge(e, qt_saved, t)
                wait_ge(e, pt_saved, t - 1)
                turn(tq_bank, lambda k: Qs[:, k, :], HG, tq_done)

            def turn_k(b, g):
                t = GROUPS * b + g
                e.wait_ge(k_scaled, t + 1)
                wait_ge(e, kt_saved, t)
                if g in (1, 2):
                    wait_ge(e, ht_lo, 2 * (b - 2) + g)
                if g == 3 and is_batch(b + 1, B):
                    e.wait_ge(xt_lo, b + 2)
                elif g == 3:
                    wait_ge(e, ft_lo, b)
                turn(tk_bank, lambda k: Ks[:, k, :], HG, tk_done)

            def turn_hidden(b, half):
                e.wait_ge(hid_done, 2 * b + half + 1)
                wait_ge(e, ht_lo, 2 * b + half)
                e.wait_ge(kt_saved, last(b + 2, half) + 1)
                turn(tk_bank, lambda k: H[:, half, k * P:(k + 1) * P], HG, ht_done)

            def turn_ffn_in(b):
                e.wait_ge(fxn_done, b + 1)
                e.wait_ge(kt_saved, last(b + 1, 2) + 1)
                turn(tk_bank, lambda k: xn[:, 1, k * P:(k + 1) * P], KT, ft_done)

            def turn_p(b, g):
                u = GROUPS * b + g
                e.wait_ge(norm_done, u + 1)
                e.wait_ge(qt_saved, min(u + 2, SLOTS) if isinstance(u, int) else u + 2)
                wait_ge(e, pt_saved, u)
                turn(tq_bank, lambda k: Pr[:, k, :], HG, pt_done)

            def c_turn(b):
                e.wait_ge(c_xn, b + 1)
                wait_ge(e, route_step, 7 * (b - 2) + 1)
                if is_step(b, 0):
                    e.wait_ge(q_scaled, SLOTS)
                turn(m1, lambda k: xn[:, 0, k * P:(k + 1) * P], KT, c_turned)

            def c_project(b):
                e.wait_ge(c_xlo, b + 1)
                e.wait_ge(c_clo, b + 1)
                wait_ge(e, t2_saved, b)
                if is_step(b, 0):
                    e.wait_ge(stage_lo, 2 * TERN + 1)
                    e.wait_ge(k_scaled, SLOTS)
                for kt in range(KT):
                    wh, wl = w2("q", kt, D)
                    three(m1[:, D:2 * D], xaT[:, 0, kt * P:(kt + 1) * P], xaT[:, 1, kt * P:(kt + 1) * P],
                          wh, wl, kt == 0, kt == KT - 1)
                wh, wl = w2("kv", 0, 2 * D)
                three(m2[:, :], cT[:, 0, :], cT[:, 1, :], wh, wl, True, True).then_inc(qkv_done, 1)

            def t1(b):
                e.wait_ge(stack_lo, 2 * b + 2)
                e.wait_ge(qk_saved, b + 1)
                e.wait_ge(vn_saved, b + 1)
                if is_step(b, 0):
                    e.wait_ge(consts, 7 + EX + 3)
                for stack, out in ((SQ, m1), (SK, m2)):
                    flat = stack.rearrange("p h s d -> p (h s d)")
                    for k in range(SG):
                        ins = e.transpose(out[:, :].bitcast(F16)[:, k * P:(k + 1) * P],
                                          flat[:, k * P:(k + 1) * P], ident16[:, :])
                ins.then_inc(t1_done, 1)

            def t2(b):
                e.wait_ge(m_split, 4 * b + 4)
                flat = SQ.rearrange("p h s d -> p (h s d)")
                for k in range(SG):
                    ins = e.transpose(m2[:, :].bitcast(F16)[:, k * P:(k + 1) * P],
                                      flat[:, k * P:(k + 1) * P], ident16[:, :])
                ins.then_inc(t2_done, 1)

            def score_group(b, j):
                if j == 0:
                    e.wait_ge(t1q_saved, b + 1)
                    e.wait_ge(t1k_saved, b + 1)
                    wait_ge(e, e_done, SG * b)
                elif j >= 2:
                    e.wait_ge(smax_done, SG * b + j - 1)
                if is_step(b, 0) and j < 2:
                    e.wait_ge((o_lo, pt_saved)[j], SLOTS)
                rows = slice(32 * (j % HG), 32 * (j % HG) + 24)
                for k in range(HG):
                    tile = HG * (j // HG) + k
                    ins = e.matmul(s_banks[j % 2][:, k * P:(k + 1) * P], QT1[rows, tile, :], KT1[rows, tile, :],
                                   start=True, stop=True)
                ins.then_inc(sc_done, 1)

            def shifted_group(b, j):
                if j == 0:
                    e.wait_ge(t2_saved, b + 1)
                elif j >= 2:
                    e.wait_ge(e_done, SG * b + j - 1)
                rows = slice(32 * (j % HG), 32 * (j % HG) + 32)
                for k in range(HG):
                    tile = HG * (j // HG) + k
                    ins = e.matmul(s_banks[j % 2][:, k * P:(k + 1) * P], KT1[rows, tile, :], QT2[rows, tile, :],
                                   start=True, stop=True)
                ins.then_inc(st_done, 1)

            def av_group(b, j):
                e.wait_ge(e_done, SG * b + j + 1)
                if j == 0:
                    e.wait_ge(va_done, b + 1)
                    if is_step(b, 0):
                        e.wait_ge(consts, 7 + EX + 4)
                        e.wait_ge(res_done, B)
                    wait_ge(e, on_done, b)
                for k, h in enumerate(heads(j)):
                    ins = e.matmul(ov_bank[:, 9 * h:9 * h + 9], E2[:, j % 4, k * P:(k + 1) * P], Va[:, h, :],
                                   start=True, stop=True)
                ins.then_inc(av_done, 1)

            def ot2_turn(b, t1_of):
                e.wait_ge(on_done, b + 1)
                e.wait_ge(t1q_saved, t1_of + 1)
                turn(m1, lambda k: On[:, k * P:(k + 1) * P], KT, ot2_done)

            def attn_out(b):
                e.wait_ge(ot2_lo, b + 1)
                for kt in range(KT):
                    wh, wl = w2("out", kt, D)
                    ins = three(m1[:, D:2 * D], OT2[0][:, kt * P:(kt + 1) * P], OT2[1][:, kt * P:(kt + 1) * P],
                                wh, wl, kt == 0, kt == KT - 1)
                ins.then_inc(w2_done, 1)

            def d_turn(b):
                e.wait_ge(d_xn, b + 1)
                turn(m1, lambda k: xn[:, 1, k * P:(k + 1) * P], KT, d_turned)

            def logits(b):
                e.wait_ge(d_xlo, b + 1)
                for kt in range(KT):
                    wh, wl = w2("route", kt, EX)
                    ins = three(m1[:, D:D + EX], xfT[:, 0, kt * P:(kt + 1) * P], xfT[:, 1, kt * P:(kt + 1) * P],
                                wh, wl, kt == 0, kt == KT - 1)
                ins.then_inc(route_done, 1)

            def expert_half(b, c, m, out, done, used):
                wait_ge(e, used, 4 * b + c)
                for kt in range(KT):
                    wh, wl = w2("exp", 4 * c + 2 * m + kt, 2 * CH)
                    ins = three(out[:, 0:2 * CH], xfT[:, 0, kt * P:(kt + 1) * P], xfT[:, 1, kt * P:(kt + 1) * P],
                                wh, wl, kt == 0, kt == KT - 1)
                ins.then_inc(done, 1)

            def expert_gate(b, c):
                if c == 0:
                    e.wait_ge(d_xlo, b + 1)
                    wait_ge(e, dres_done, b)
                if is_step(b, 0) and c == 0:
                    e.wait_ge(fres_done, B)
                if is_step(b, 0):
                    e.wait_ge(stage_lo, 2 * TERN + 2 + c)
                expert_half(b, c, 0, g_bank, g2_done, g_act)

            def expert_up(b, c):
                expert_half(b, c, 1, u_bank, u2_done, h2_done)

            def hidden_turn(b, c):
                a, z = CHUNK_TILES[c]
                e.wait_ge(h2_done, 4 * b + c + 1)
                wait_ge(e, h2t_lo, 4 * b + c)
                turn(m3, lambda k: H2[:, (a + k) * P:(a + k + 1) * P], z - a, h2t_done)

            def down(b, c):
                e.wait_ge(h2t_lo, 4 * b + c + 1)
                if is_step(b, 0) and c == 0:
                    e.wait_ge(stage_lo, 2 * TERN + L1_CHUNKS)
                if c == 0:
                    e.wait_ge(g_act, 4 * b + 4)
                for k in range(*CHUNK_TILES[c]):
                    cols = slice(k * P, (k + 1) * P)
                    ins = three(g_bank[:, 0:D], HT2[0][:, cols], HT2[1][:, cols], woh[:, k * D:(k + 1) * D],
                                wol[:, k * D:(k + 1) * D], k == 0, k == F2 // P - 1)
                if c == 3:
                    ins.then_inc(dn_done, 1)

            def layer0_step(i, cur, prv, old, nxt):
                if cur:
                    project_q(i, 0)
                    project_k(i, 0)
                if prv:
                    scores(i - 1, 3)
                if cur:
                    project_v(i, 0)
                if prv:
                    values(i - 1, 2)
                    out_project(i - 1, 1)
                if is_step(i, B):
                    c_turn(0)
                if cur:
                    turn_q(i, 0)
                if old:
                    up(i - 2, 1)
                if cur:
                    turn_k(i, 0)
                if is_step(i, B + 1):
                    shifted_group(0, 0)
                    shifted_group(0, 1)
                if old:
                    gate(i - 2, 1)
                if is_step(i, B):
                    c_project(0)
                if cur:
                    sum_weights(i, 0)
                if is_step(i, B + 1):
                    av_group(0, 0)
                    shifted_group(0, 2)
                if old:
                    turn_hidden(i - 2, 0)
                if prv:
                    turn_p(i - 1, 3)
                if is_step(i, B + 1):
                    av_group(0, 1)
                if cur:
                    project_q(i, 1)
                    project_k(i, 1)
                    project_v(i, 1)
                    scores(i, 0)
                if prv:
                    values(i - 1, 3)
                    out_project(i - 1, 2)
                if cur:
                    turn_q(i, 1)
                if is_step(i, B + 1):
                    shifted_group(0, 3)
                if cur:
                    turn_k(i, 1)
                    project_k(i, 2)
                if old:
                    turn_hidden(i - 2, 1)
                if is_step(i, B):
                    t1(0)
                if is_step(i, B + 1):
                    av_group(0, 2)
                    shifted_group(0, 4)
                if cur:
                    turn_p(i, 0)
                    sum_weights(i, 1)
                    project_q(i, 2)
                if is_step(i, B + 1):
                    c_turn(1)
                if cur:
                    project_v(i, 2)
                    scores(i, 1)
                if prv:
                    out_project(i - 1, 3)
                if cur:
                    values(i, 0)
                    turn_q(i, 2)
                if is_step(i, B + 1):
                    av_group(0, 3)
                if cur:
                    turn_k(i, 2)
                if old:
                    ffn_down(i - 2)
                if is_step(i, B):
                    score_group(0, 0)
                    score_group(0, 1)
                if cur:
                    project_q(i, 3)
                if is_step(i, B):
                    score_group(0, 2)
                if cur:
                    turn_p(i, 1)
                    sum_weights(i, 2)
                if is_step(i, B):
                    score_group(0, 3)
                if prv:
                    turn_ffn_in(i - 1)
                if is_step(i, B):
                    score_group(0, 4)
                    score_group(0, 5)
                    score_group(0, 6)
                if is_step(i, B + 1):
                    shifted_group(0, 5)
                if is_step(i, B):
                    score_group(0, 7)
                    t2(0)
                if cur:
                    project_k(i, 3)
                    project_v(i, 3)
                    scores(i, 2)
                if nxt:
                    prep(i + 1)
                if cur:
                    values(i, 1)
                    out_project(i, 0)
                if prv:
                    up(i - 1, 0)
                if cur:
                    turn_q(i, 3)
                    turn_k(i, 3)
                if prv:
                    gate(i - 1, 0)
                if cur:
                    turn_p(i, 2)
                if is_step(i, B + 1):
                    av_group(0, 4)
                    shifted_group(0, 6)
                    av_group(0, 5)
                    c_project(1)
                    shifted_group(0, 7)
                    av_group(0, 6)
                    av_group(0, 7)
                    t1(1)
                    ot2_turn(0, 1)
                    score_group(1, 0)
                    score_group(1, 1)
                    score_group(1, 2)
                    attn_out(0)
                    score_group(1, 3)
                    score_group(1, 4)
                    score_group(1, 5)
                    d_turn(0)
                    score_group(1, 6)
                    score_group(1, 7)
                    logits(0)
                    t2(1)

            batches(e, layer0_step)

            def layer1_step(i, cur, prv, nxt):
                if prv:
                    expert_gate(i - 1, 0)
                if cur:
                    shifted_group(i, 0)
                    shifted_group(i, 1)
                if prv:
                    expert_up(i - 1, 0)
                if cur:
                    av_group(i, 0)
                    shifted_group(i, 2)
                    av_group(i, 1)
                    shifted_group(i, 3)
                if nxt:
                    c_turn(i + 1)
                if prv:
                    expert_gate(i - 1, 1)
                if cur:
                    av_group(i, 2)
                    shifted_group(i, 4)
                if prv:
                    expert_up(i - 1, 1)
                if cur:
                    av_group(i, 3)
                    shifted_group(i, 5)
                if prv:
                    hidden_turn(i - 1, 0)
                if cur:
                    av_group(i, 4)
                    shifted_group(i, 6)
                if nxt:
                    c_project(i + 1)
                if cur:
                    av_group(i, 5)
                    shifted_group(i, 7)
                if prv:
                    expert_gate(i - 1, 2)
                    expert_up(i - 1, 2)
                if cur:
                    av_group(i, 6)
                    av_group(i, 7)
                if prv:
                    hidden_turn(i - 1, 1)
                    expert_gate(i - 1, 3)
                    expert_up(i - 1, 3)
                if nxt:
                    t1(i + 1)
                if prv:
                    hidden_turn(i - 1, 2)
                    down(i - 1, 0)
                if cur:
                    ot2_turn(i, i + 1 if nxt else B - 1)
                if nxt:
                    score_group(i + 1, 0)
                    score_group(i + 1, 1)
                if prv:
                    down(i - 1, 1)
                if nxt:
                    score_group(i + 1, 2)
                if cur:
                    attn_out(i)
                if prv:
                    hidden_turn(i - 1, 3)
                if nxt:
                    score_group(i + 1, 3)
                if prv:
                    down(i - 1, 2)
                if nxt:
                    score_group(i + 1, 4)
                    score_group(i + 1, 5)
                if cur:
                    d_turn(i)
                if nxt:
                    score_group(i + 1, 6)
                    score_group(i + 1, 7)
                if prv:
                    down(i - 1, 3)
                if cur:
                    logits(i)
                if nxt:
                    t2(i + 1)

            steps(e, layer1_step)


INS = {"x": "x", "ctxT": "ctx_1024", "g_xattn": "g_xattn", "g_ffn": "g_ffn", "Wq0": "L0_xattn_Wq",
       "Wk0": "L0_xattn_Wk", "Wv0": "L0_xattn_Wv", "Wo0": "L0_xattn_Wo", "gq": "L0_xattn_gq",
       "gk": "L0_xattn_gk", "WuT": "L0_ffn_W_up", "WgT": "L0_ffn_W_gate", "WdT": "L0_ffn_W_down",
       "pos": "fside_BxSx2_0", "Wq1": "L1_xattn_Wq", "Wkv1": "L1_xattn_Wkv", "Wout1": "L1_xattn_Wout",
       "bout": "L1_xattn_bout", "gwT": "L1_ffn_gate_w", "e_gate": "L1_ffn_w_gate", "e_up": "L1_ffn_w_up",
       "e_down": "L1_ffn_w_down"}
TURNED = {"ctxT": (2, 0, 1), "WuT": (1, 0), "WgT": (1, 0), "WdT": (1, 0), "gwT": (1, 0)}


def kernel(**inputs):
    import numpy as np
    import concourse.bacc as bacc
    from concourse.bass_utils import run_bass_kernel_spmd

    nc = bacc.Bacc("TRN2", target_bir_lowering=False, num_devices=1)
    arrays, io = {}, {}
    for name, source in INS.items():
        a = np.asarray(inputs[source])
        a = np.ascontiguousarray(a.transpose(TURNED[name]) if name in TURNED else a)
        arrays[f"in_{name}"] = a
        io[name] = nc.dram_tensor(f"in_{name}", a.shape, mybir.dt.from_np(a.dtype), kind="ExternalInput").ap()
    shape = np.asarray(inputs["x"]).shape
    io["out"] = nc.dram_tensor("out_x", shape, F32, kind="ExternalOutput").ap()
    build(nc, io)
    return run_bass_kernel_spmd(nc, [arrays], core_ids=[0]).results[0]["out_x"]
```
